# Optimizing a Trainium2 kernel written in Bass

```python
import numpy as np
import jax
import jax.numpy as jnp

def _softmax(x, axis=-1):
    return jax.nn.softmax(x, axis=axis)

def _gelu(x):
    return jax.nn.gelu(x, approximate=True)

def _silu(x):
    return jax.nn.silu(x)

def _sigmoid(x):
    return jax.nn.sigmoid(x)

def _layernorm(x, axis=-1, eps=1e-05):
    m = jnp.mean(x, axis=axis, keepdims=True)
    v = jnp.var(x, axis=axis, keepdims=True)
    return (x - m) / jnp.sqrt(v + eps)

def _scatter_add(tgt, idx, src, axis=0):
    return tgt.at[idx].add(src)

def _segment_sum(src, seg, n):
    return jax.ops.segment_sum(src, seg, n)
kernel_name = 'mk_gnn_resnorm_d4_gnn_r64_e9e97c'

def setup_inputs(seed: int=0):
    np.random.seed(seed)
    _w = jnp.asarray

    def _rec_inputs():
        import jax
        import jax.numpy as jnp
        _gk = jax.random.key(seed)
        x = -0.000202 + 1 * jax.random.normal(jax.random.fold_in(_gk, 1), (50000, 128), jnp.float32)
        src = jax.random.randint(jax.random.fold_in(_gk, 2), (25000,), 0, 50000, jnp.int32)
        dst = jnp.minimum((50000 * jax.random.uniform(jax.random.fold_in(_gk, 3), (25000,)) ** 2.0).astype(jnp.int32), 49999)
        _o = jnp.argsort(dst, stable=True)
        src = src[_o]
        dst = dst[_o]
        edge_attr_32 = 0.000196303 + 1.00016 * jax.random.normal(jax.random.fold_in(_gk, 11), (25000, 32), jnp.float32)
        return (x, src, dst, edge_attr_32)
    x, src, dst, edge_attr_32 = _rec_inputs()

    def _L0_gnn_setup():
        import jax, jax.numpy as jnp
        import numpy as np
        import math
        N, E = (50000, 12500)
        HID, EDIM, H = (128, 32, 8)
        D = HID // H
        FFN = 4 * HID
        EPS = 1e-05

        def layer_norm(x, g, b):
            mu = jnp.mean(x, axis=-1, keepdims=True)
            var = jnp.var(x, axis=-1, keepdims=True)
            return (x - mu) * jax.lax.rsqrt(var + EPS) * g + b
        key = jax.random.key(seed)
        ks = jax.random.split(key, 16)
        s = 1.0 / math.sqrt(HID)
        inp = {'x': jax.random.normal(ks[0], (N, HID), jnp.float32), 'edge_index': jax.random.randint(ks[1], (2, E), 0, N, jnp.int32), 'edge_attr': jax.random.normal(ks[2], (E, EDIM), jnp.float32), 'qW': jax.random.normal(ks[3], (HID, HID), jnp.float32) * s, 'qb': jnp.zeros((HID,), jnp.float32), 'kW': jax.random.normal(ks[4], (HID, HID), jnp.float32) * s, 'kb': jnp.zeros((HID,), jnp.float32), 'vW': jax.random.normal(ks[5], (HID, HID), jnp.float32) * s, 'vb': jnp.zeros((HID,), jnp.float32), 'eW': jax.random.normal(ks[6], (EDIM, H), jnp.float32) / math.sqrt(EDIM), 'eb': jnp.zeros((H,), jnp.float32), 'oW': jax.random.normal(ks[7], (HID, HID), jnp.float32) * s, 'ob': jnp.zeros((HID,), jnp.float32), 'ln1_g': jnp.ones((HID,), jnp.float32), 'ln1_b': jnp.zeros((HID,), jnp.float32), 'f1W': jax.random.normal(ks[8], (HID, FFN), jnp.float32) * s, 'f1b': jnp.zeros((FFN,), jnp.float32), 'lnf_g': jnp.ones((FFN,), jnp.float32), 'lnf_b': jnp.zeros((FFN,), jnp.float32), 'f2W': jax.random.normal(ks[9], (FFN, HID), jnp.float32) / math.sqrt(FFN), 'f2b': jnp.zeros((HID,), jnp.float32), 'ln2_g': jnp.ones((HID,), jnp.float32), 'ln2_b': jnp.zeros((HID,), jnp.float32)}
        return inp
    _L0_gnn_all = _L0_gnn_setup()
    _L0_gnn_in = {k: v for k, v in _L0_gnn_all.items() if k in ('qW', 'qb', 'kW', 'kb', 'vW', 'vb', 'eW', 'eb', 'oW', 'ob', 'ln1_g', 'ln1_b', 'f1W', 'f1b', 'lnf_g', 'lnf_b', 'f2W', 'f2b', 'ln2_g', 'ln2_b')}
    del _L0_gnn_all

    def _L1_gnn_setup():
        import jax, jax.numpy as jnp
        import numpy as np
        N_NODES = 100000
        key = jax.random.key(seed)
        k1, k2, k3, k4, k5 = jax.random.split(key, 5)
        fts = jax.random.normal(k1, (N_NODES, 128), dtype=jnp.float32)
        u = jax.random.randint(k2, (25000,), 0, N_NODES)
        v = jax.random.randint(k3, (25000,), 0, N_NODES)
        edge_index = jnp.stack([u, v]).astype(jnp.int64)
        W_l = jax.random.normal(k4, (128, 128), dtype=jnp.float32) * (1.0 / np.sqrt(128))
        W_r = jax.random.normal(k5, (128, 128), dtype=jnp.float32) * (1.0 / np.sqrt(128))
        return {'fts': fts, 'edge_index': edge_index, 'W_l': W_l, 'W_r': W_r}
    _L1_gnn_all = _L1_gnn_setup()
    _L1_gnn_in = {k: v for k, v in _L1_gnn_all.items() if k in ('W_l', 'W_r')}
    del _L1_gnn_all

    def _L2_gnn_setup():
        import jax, jax.numpy as jnp
        import numpy as np
        N = 100000
        E = 9375
        D_IN = 128
        D = 128
        L = 3

        def gru_cell(m, h, w_ih, w_hh, b_ih, b_hh):
            gi = m @ w_ih.T + b_ih
            gh = h @ w_hh.T + b_hh
            ir, iz, inn = jnp.split(gi, 3, axis=-1)
            hr, hz, hn = jnp.split(gh, 3, axis=-1)
            r = jax.nn.sigmoid(ir + hr)
            z = jax.nn.sigmoid(iz + hz)
            n = jnp.tanh(inn + r * hn)
            return (1.0 - z) * n + z * h
        key = jax.random.key(seed)
        ks = jax.random.split(key, 10)
        s = 1.0 / np.sqrt(D)
        x = jax.random.normal(ks[0], (N, D_IN), dtype=jnp.float32)
        edge_index = jax.random.randint(ks[1], (2, E), 0, N, dtype=jnp.int64)
        lin_w = jax.random.normal(ks[2], (D, D_IN), dtype=jnp.float32) * (1.0 / np.sqrt(D_IN))
        lin_b = jnp.zeros((D,), dtype=jnp.float32)
        weight = jax.random.normal(ks[3], (L, D, D), dtype=jnp.float32) * s
        w_ih = jax.random.normal(ks[4], (3 * D, D), dtype=jnp.float32) * s
        w_hh = jax.random.normal(ks[5], (3 * D, D), dtype=jnp.float32) * s
        b_ih = jnp.zeros((3 * D,), dtype=jnp.float32)
        b_hh = jnp.zeros((3 * D,), dtype=jnp.float32)
        return {'x': x, 'lin_w': lin_w, 'lin_b': lin_b, 'weight': weight, 'w_ih': w_ih, 'w_hh': w_hh, 'b_ih': b_ih, 'b_hh': b_hh, 'edge_index': edge_index}
    _L2_gnn_all = _L2_gnn_setup()
    _L2_gnn_in = {k: v for k, v in _L2_gnn_all.items() if k in ('lin_w', 'lin_b', 'weight', 'w_ih', 'w_hh', 'b_ih', 'b_hh')}
    del _L2_gnn_all

    def _L3_gnn_setup():
        import jax, jax.numpy as jnp
        import numpy as np
        N_NODES = 50000
        N_EDGES = 12500
        D_IN = 128
        D_OUT = 128
        key = jax.random.key(seed)
        k1, k2, k3 = jax.random.split(key, 3)
        x = jax.random.normal(k1, (N_NODES, D_IN), dtype=jnp.float32)
        edge_index = jax.random.randint(k2, (2, N_EDGES), 0, N_NODES, dtype=jnp.int64)
        weight = jax.random.normal(k3, (2 * D_IN, D_OUT), dtype=jnp.float32) * (6.0 / (2 * D_IN + D_OUT)) ** 0.5
        return {'x': x, 'edge_index': edge_index, 'weight': weight}
    _L3_gnn_all = _L3_gnn_setup()
    _L3_gnn_in = {k: v for k, v in _L3_gnn_all.items() if k in ('weight',)}
    del _L3_gnn_all
    return {'x': x, 'src': src, 'dst': dst, 'edge_attr_32': edge_attr_32, 'L0_gnn_qW': _L0_gnn_in['qW'], 'L0_gnn_qb': _L0_gnn_in['qb'], 'L0_gnn_kW': _L0_gnn_in['kW'], 'L0_gnn_kb': _L0_gnn_in['kb'], 'L0_gnn_vW': _L0_gnn_in['vW'], 'L0_gnn_vb': _L0_gnn_in['vb'], 'L0_gnn_eW': _L0_gnn_in['eW'], 'L0_gnn_eb': _L0_gnn_in['eb'], 'L0_gnn_oW': _L0_gnn_in['oW'], 'L0_gnn_ob': _L0_gnn_in['ob'], 'L0_gnn_ln1_g': _L0_gnn_in['ln1_g'], 'L0_gnn_ln1_b': _L0_gnn_in['ln1_b'], 'L0_gnn_f1W': _L0_gnn_in['f1W'], 'L0_gnn_f1b': _L0_gnn_in['f1b'], 'L0_gnn_lnf_g': _L0_gnn_in['lnf_g'], 'L0_gnn_lnf_b': _L0_gnn_in['lnf_b'], 'L0_gnn_f2W': _L0_gnn_in['f2W'], 'L0_gnn_f2b': _L0_gnn_in['f2b'], 'L0_gnn_ln2_g': _L0_gnn_in['ln2_g'], 'L0_gnn_ln2_b': _L0_gnn_in['ln2_b'], 'L1_gnn_W_l': _L1_gnn_in['W_l'], 'L1_gnn_W_r': _L1_gnn_in['W_r'], 'L2_gnn_lin_w': _L2_gnn_in['lin_w'], 'L2_gnn_lin_b': _L2_gnn_in['lin_b'], 'L2_gnn_weight': _L2_gnn_in['weight'], 'L2_gnn_w_ih': _L2_gnn_in['w_ih'], 'L2_gnn_w_hh': _L2_gnn_in['w_hh'], 'L2_gnn_b_ih': _L2_gnn_in['b_ih'], 'L2_gnn_b_hh': _L2_gnn_in['b_hh'], 'L3_gnn_weight': _L3_gnn_in['weight']}

def reference(x, src, dst, edge_attr_32, L0_gnn_qW, L0_gnn_qb, L0_gnn_kW, L0_gnn_kb, L0_gnn_vW, L0_gnn_vb, L0_gnn_eW, L0_gnn_eb, L0_gnn_oW, L0_gnn_ob, L0_gnn_ln1_g, L0_gnn_ln1_b, L0_gnn_f1W, L0_gnn_f1b, L0_gnn_lnf_g, L0_gnn_lnf_b, L0_gnn_f2W, L0_gnn_f2b, L0_gnn_ln2_g, L0_gnn_ln2_b, L1_gnn_W_l, L1_gnn_W_r, L2_gnn_lin_w, L2_gnn_lin_b, L2_gnn_weight, L2_gnn_w_ih, L2_gnn_w_hh, L2_gnn_b_ih, L2_gnn_b_hh, L3_gnn_weight):
    import jax
    import jax.numpy as jnp

    def _L0_gnn_ref(x, edge_index, edge_attr, qW, qb, kW, kb, vW, vb, eW, eb, oW, ob, ln1_g, ln1_b, f1W, f1b, lnf_g, lnf_b, f2W, f2b, ln2_g, ln2_b):
        import jax, jax.numpy as jnp
        import numpy as np
        import math
        N, E = (50000, 12500)
        HID, EDIM, H = (128, 32, 8)
        D = HID // H
        FFN = 4 * HID
        EPS = 1e-05

        def layer_norm(x, g, b):
            mu = jnp.mean(x, axis=-1, keepdims=True)
            var = jnp.var(x, axis=-1, keepdims=True)
            return (x - mu) * jax.lax.rsqrt(var + EPS) * g + b
        src, dst = (edge_index[0], edge_index[1])
        q = (x @ qW + qb).reshape(N, H, D)
        k = (x @ kW + kb).reshape(N, H, D)
        v = (x @ vW + vb).reshape(N, H, D)
        edge_bias = edge_attr @ eW + eb
        scores = jnp.sum(q[src] * k[dst], axis=-1) / math.sqrt(D) + edge_bias
        mx = jax.ops.segment_max(scores, dst, num_segments=N)
        mx = jnp.where(jnp.isinf(mx), jnp.zeros_like(mx), mx)
        ex = jnp.exp(scores - mx[dst])
        den = jax.ops.segment_sum(ex, dst, num_segments=N)
        den = jnp.maximum(den, 1e-08)
        attn = ex / den[dst]
        wv = v[src] * attn[:, :, None]
        out = jax.ops.segment_sum(wv, dst, num_segments=N)
        out = out.reshape(N, HID) @ oW + ob
        x = layer_norm(x + out, ln1_g, ln1_b)
        h = x @ f1W + f1b
        h = jax.nn.gelu(layer_norm(h, lnf_g, lnf_b), approximate=False)
        h = h @ f2W + f2b
        x = layer_norm(x + h, ln2_g, ln2_b)
        return x

    def _L1_gnn_ref(fts, edge_index, W_l, W_r):
        import jax, jax.numpy as jnp
        import numpy as np
        N_NODES = 100000
        u, v = (edge_index[0], edge_index[1])
        n = fts.shape[0]
        gathered = fts[v]
        seg_sum = jax.ops.segment_sum(gathered, u, num_segments=n)
        counts = jax.ops.segment_sum(jnp.ones((u.shape[0],), fts.dtype), u, num_segments=n)
        aggregate = seg_sum / jnp.maximum(counts, 1.0)[:, None]
        out = fts @ W_l.T + aggregate @ W_r.T
        out = out / jnp.linalg.norm(out, axis=1, keepdims=True)
        return out

    def _L2_gnn_ref(x, lin_w, lin_b, weight, w_ih, w_hh, b_ih, b_hh, edge_index):
        import jax, jax.numpy as jnp
        import numpy as np
        N = 100000
        E = 9375
        D_IN = 128
        D = 128
        L = 3

        def gru_cell(m, h, w_ih, w_hh, b_ih, b_hh):
            gi = m @ w_ih.T + b_ih
            gh = h @ w_hh.T + b_hh
            ir, iz, inn = jnp.split(gi, 3, axis=-1)
            hr, hz, hn = jnp.split(gh, 3, axis=-1)
            r = jax.nn.sigmoid(ir + hr)
            z = jax.nn.sigmoid(iz + hz)
            n = jnp.tanh(inn + r * hn)
            return (1.0 - z) * n + z * h
        h = x @ lin_w.T + lin_b
        src, dst = (edge_index[0], edge_index[1])
        n_nodes = h.shape[0]
        for i in range(weight.shape[0]):
            m = h @ weight[i]
            agg = jax.ops.segment_sum(m[src], dst, num_segments=n_nodes)
            h = gru_cell(agg, h, w_ih, w_hh, b_ih, b_hh)
        return h

    def _L3_gnn_ref(x, edge_index, weight):
        import jax, jax.numpy as jnp
        import numpy as np
        N_NODES = 50000
        N_EDGES = 12500
        D_IN = 128
        D_OUT = 128
        src = edge_index[0]
        dst = edge_index[1]
        n = x.shape[0]
        msgs = x[src]
        agg_sum = jax.ops.segment_sum(msgs, dst, num_segments=n)
        counts = jax.ops.segment_sum(jnp.ones((src.shape[0],), dtype=x.dtype), dst, num_segments=n)
        agg_mean = agg_sum / jnp.maximum(counts, 1.0)[:, None]
        h = jnp.concatenate([x, agg_mean], axis=-1)
        return h @ weight
    edge_index = jnp.stack([src, dst])
    x = _layernorm(x + _L0_gnn_ref(x, edge_index, edge_attr_32, L0_gnn_qW, L0_gnn_qb, L0_gnn_kW, L0_gnn_kb, L0_gnn_vW, L0_gnn_vb, L0_gnn_eW, L0_gnn_eb, L0_gnn_oW, L0_gnn_ob, L0_gnn_ln1_g, L0_gnn_ln1_b, L0_gnn_f1W, L0_gnn_f1b, L0_gnn_lnf_g, L0_gnn_lnf_b, L0_gnn_f2W, L0_gnn_f2b, L0_gnn_ln2_g, L0_gnn_ln2_b), axis=-1)
    x = _layernorm(x + _L1_gnn_ref(x, edge_index, L1_gnn_W_l, L1_gnn_W_r), axis=-1)
    x = _layernorm(x + _L2_gnn_ref(x, L2_gnn_lin_w, L2_gnn_lin_b, L2_gnn_weight, L2_gnn_w_ih, L2_gnn_w_hh, L2_gnn_b_ih, L2_gnn_b_hh, edge_index), axis=-1)
    x = _layernorm(x + _L3_gnn_ref(x, edge_index, L3_gnn_weight), axis=-1)
    return x

_drawn_inputs = setup_inputs


def setup_inputs(seed=0):
    import zlib

    import numpy as np

    out = dict(_drawn_inputs(seed))
    spreads = {'L0_gnn_qb': (0.0, 0.8),
     'L0_gnn_kb': (0.0, 0.8),
     'L0_gnn_vb': (0.0, 0.335),
     'L0_gnn_eb': (0.0, 0.8),
     'L0_gnn_ob': (0.0, 0.1),
     'L0_gnn_ln1_g': (1.0, 0.2),
     'L0_gnn_ln1_b': (0.0, 0.1),
     'L0_gnn_f1b': (0.0, 0.1),
     'L0_gnn_lnf_g': (1.0, 0.2),
     'L0_gnn_lnf_b': (0.0, 0.287),
     'L0_gnn_f2b': (0.0, 0.1),
     'L0_gnn_ln2_g': (1.0, 0.2),
     'L0_gnn_ln2_b': (0.0, 0.1),
     'L2_gnn_lin_b': (0.0, 0.1),
     'L2_gnn_b_ih': (0.0, 0.1),
     'L2_gnn_b_hh': (0.0, 0.1)}
    factors = {}
    for name, (base, spread) in spreads.items():
        noise = np.random.default_rng([zlib.crc32(name.encode()), seed]).standard_normal(out[name].shape)
        drawn = base * np.exp(spread * noise) if base else spread * noise
        out[name] = jnp.asarray(drawn.astype(out[name].dtype))
    for name, factor in factors.items():
        out[name] = (out[name] * factor).astype(out[name].dtype)
    return out
```

```python
import concourse.bass as bass
from concourse import mybir
from contextlib import ExitStack

F32 = mybir.dt.float32
BF16 = mybir.dt.bfloat16
I32 = mybir.dt.int32
ALU = mybir.AluOpType
ACT = mybir.ActivationFunctionType
AX = mybir.AxisListType

N, E, D, HEADS, EDIM, FFN = 50000, 25000, 128, 8, 32, 512
P, J = 128, 4
SUPER = P * J
NT = -(-N // (2 * SUPER)) * 2
ET = -(-E // (2 * SUPER)) * 2
NP, EP = NT * SUPER, ET * SUPER
ECOLS = EP // P
PAD_NODE = NP - 1
DIGIT = 256
HI_DIGITS = NP // DIGIT
EPS = 1e-5
BIG = 1e30
HEAD_DIM = D // HEADS


class Tile:

    def __init__(self, u, slot):
        self.u, self.slot, self.n = u, slot, 2 * u + slot


def over_tiles(eng, tiles, lag, step):
    def pair(k):
        for b in range(2):
            def tile_at(behind):
                u, slot = k + (b - behind) // 2, (b - behind) % 2
                if isinstance(k, int) and not 0 <= 2 * u + slot < tiles:
                    return None
                return Tile(u, slot)
            step(tile_at)
    first = (lag + 3) // 2
    for k in range(first):
        pair(k)
    with eng.Fori(first, tiles // 2) as k:
        pair(k)
    for k in range(tiles // 2, tiles // 2 + (lag + 1) // 2):
        pair(k)


def wait(eng, sem, count):
    if not isinstance(count, int) or count > 0:
        eng.wait_ge(sem, count)


def wait_alone(eng, sem, count):
    if not isinstance(count, int) or count > 0:
        eng.wait_ge(sem, count)
        eng.nop(nofuse=True)


def nm_tile(table, t):
    view = table.rearrange("(s p j) d -> s p (j d)", p=P, j=J)
    return view[bass.ds(t.n, 1), :, :].rearrange("s p n -> (s p) n")


def list_tile(values, t):
    view = values.rearrange("(s p j) -> s p j", p=P, j=J)
    return view[bass.ds(t.n, 1), :, :].rearrange("s p j -> (s p) j")


def row_tile(values, t, parts=P):
    view = values.rearrange("(s n) -> s n", n=SUPER)
    return view[bass.ds(t.n, 1), :].broadcast_to([parts, SUPER])


def fm_tile(table, t):
    return table[bass.ds(t.n, 1), :, :].rearrange("s p n -> (s p) n")


def on_all(row):
    n = row.shape[0]
    return row.rearrange("(a n) -> a n", a=1).broadcast_to([P, n])


def column(row):
    return row.rearrange("(n a) -> n a", a=1)


class Phase:

    def __init__(self, nc, ctx, name):
        self.nc, self.ctx, self.name = nc, ctx, name
        self.semaphores = []
        ctx.callback(self.clear)

    def clear(self):
        self.nc.clear_and_free_semaphores(self.semaphores)
        self.nc.all_engine_barrier()

    def sb(self, name, shape, dt=F32):
        return self.ctx.enter_context(self.nc.sbuf_tensor(f"{self.name}_{name}", shape, dt))

    def ps(self, name, shape=(P, SUPER), dt=F32):
        return self.ctx.enter_context(self.nc.psum_tensor(f"{self.name}_{name}", list(shape), dt))

    def sem(self, name):
        self.semaphores.append(self.nc.alloc_semaphore(f"{self.name}_{name}"))
        return self.semaphores[-1]

    def sems(self, name):
        return [self.sem(f"{name}{b}") for b in range(2)]


def flat(buf):
    return buf.rearrange("p j d -> p (j d)")


def edge_columns(buf):
    return buf.rearrange("f (p j) -> f j p", j=J)


def sum_pass(nc, name, g, gather_from, pairs, mask, weight):
    with ExitStack() as ctx:
        f = Phase(nc, ctx, name)
        idx = f.sb("idx", [P, 2, J, 2], I32)
        rows = f.sb("rows", [P, 2, J, D])
        keep = f.sb("keep", [P, 2, SUPER], BF16)
        run = f.sb("run", [P, 2, SUPER])
        sums = f.sb("sums", [P, 2, SUPER])
        w = f.sb("w", [P, D])
        ps_rows = [f.ps(f"ps_rows{b}") for b in range(2)]
        ps_sums = [f.ps(f"ps_sums{b}") for b in range(2)]
        w_loaded, idx_loaded, keep_loaded = f.sem("w_loaded"), f.sems("idx_loaded"), f.sems("keep_loaded")
        gathered, stored = f.sems("gathered"), f.sems("stored")
        rows_turned, scanned, sums_made, sums_copied = (
            f.sem("rows_turned"), f.sem("scanned"), f.sem("sums_made"), f.sem("sums_copied"))
        block = ctx.enter_context(nc.Block())

        @block.sync
        def _(sp):
            if weight is not None:
                sp.dma_start(w[:, :], weight).then_inc(w_loaded, 16)

            def step(tile_at):
                if t := tile_at(0):
                    wait_alone(sp, gathered[t.slot], 64 * t.u)
                    sp.dma_start(idx[:, t.slot, :, :].rearrange("p j c -> p (j c)"),
                                 nm_tile(pairs, t)).then_inc(idx_loaded[t.slot], 16)
                    wait_alone(sp, scanned, t.n - 1)
                    sp.dma_start(keep[:, t.slot, :], row_tile(mask, t)).then_inc(keep_loaded[t.slot], 16)
            over_tiles(sp, ET, 0, step)

        @block.gpsimd
        def _(pool):
            def step(tile_at):
                if t := tile_at(0):
                    wait(pool, idx_loaded[t.slot], 16 * (t.u + 1))
                    wait(pool, rows_turned, t.n - 1)
                    pool.nop(nofuse=True)
                    for j in range(J):
                        nc.gpsimd.indirect_dma_start(
                            out=rows[:, t.slot, j, :], out_offset=None, in_=gather_from[:, :],
                            in_offset=bass.IndirectOffsetOnAxis(ap=idx[:, t.slot, j, 1:2], axis=0)).then_inc(gathered[t.slot], 16)
            over_tiles(pool, ET, 0, step)

        @block.tensor
        def _(pe):
            if weight is not None:
                pe.wait_ge(w_loaded, 16)

            def step(tile_at):
                if t := tile_at(0):
                    wait(pe, gathered[t.slot], 64 * (t.u + 1))
                    wait(pe, scanned, t.n - 1)
                    for j in range(J):
                        last = nc.tensor.transpose(edge_columns(ps_rows[t.slot][:, :])[:, j, :],
                                                   rows[:, t.slot, j, :], g["ident"][:, :])
                    last.then_inc(rows_turned, 1)
                if t := tile_at(1):
                    wait(pe, scanned, t.n + 1)
                    wait(pe, sums_copied, t.n - 1)
                    for j in range(J):
                        out = ps_sums[t.slot][:, j * D:(j + 1) * D]
                        part = edge_columns(run[:, t.slot, :])[:, j, :]
                        if weight is None:
                            last = nc.tensor.transpose(out, part, g["ident"][:, :])
                        else:
                            last = nc.tensor.matmul(out, part, w[:, :], start=True, stop=True)
                    last.then_inc(sums_made, 1)
            over_tiles(pe, ET, 1, step)

        @block.vector
        def _(dve):
            def step(tile_at):
                if t := tile_at(0):
                    wait(dve, keep_loaded[t.slot], 16 * (t.u + 1))
                    wait(dve, rows_turned, t.n + 1)
                    wait(dve, sums_made, t.n - 1)
                    wait(dve, scanned, t.n)
                    first = isinstance(t.n, int) and t.n == 0
                    nc.vector.tensor_tensor_scan(
                        run[:, t.slot, :], keep[:, t.slot, :], ps_rows[t.slot][:, :],
                        0.0 if first else run[:, 1 - t.slot, SUPER - 1:SUPER],
                        ALU.mult, ALU.add).then_inc(scanned, 1)
            over_tiles(dve, ET, 0, step)

        @block.scalar
        def _(act):
            def step(tile_at):
                if t := tile_at(1):
                    wait(act, sums_made, t.n + 1)
                    wait(act, stored[t.slot], 16 * t.u)
                    nc.scalar.activation(sums[:, t.slot, :], ps_sums[t.slot][:, :],
                                         ACT.Copy).then_inc(sums_copied, 1)
                if t := tile_at(2):
                    wait(act, sums_copied, t.n + 1)
                    act.dma_start(nm_tile(g["sums"], t), sums[:, t.slot, :]).then_inc(stored[t.slot], 16)
            over_tiles(act, ET, 2, step)
            for b in range(2):
                act.wait_ge(stored[b], 16 * (ET // 2))


def gather_step(nc, pool, t, idx, rows, table, idx_loaded, rows_free, gathered):
    wait(pool, idx_loaded[t.slot], 16 * (t.u + 1))
    wait(pool, rows_free, t.n - 1)
    pool.nop(nofuse=True)
    for j in range(J):
        nc.gpsimd.indirect_dma_start(
            out=rows[:, t.slot, j, :], out_offset=None, in_=table[:, :],
            in_offset=bass.IndirectOffsetOnAxis(ap=idx[:, t.slot, j:j + 1], axis=0)).then_inc(gathered[t.slot], 16)


def gated_pass(nc, name, g, i, h_in, ht_in, h_out, ht_out, x_res, x_out):
    final = x_out is not None
    with ExitStack() as ctx:
        f = Phase(nc, ctx, name)
        wt = f.sb("wt", [P, D])
        wih = f.sb("wih", [P, 3 * D])
        whh = f.sb("whh", [P, 3 * D])
        win = f.sb("win", [P, 3 * D])
        b_ih = f.sb("b_ih", [P, 3])
        b_hh = f.sb("b_hh", [P, 3])
        b_rz = f.sb("b_rz", [P, 2])
        idx = f.sb("idx", [P, 2, J], I32)
        rows = f.sb("rows", [P, 2, J, D])
        ht = f.sb("ht", [P, 2, SUPER])
        st = f.sb("st", [P, 2, SUPER])
        r, z, n1, n2, n3 = (f.sb(s, [P, 2, SUPER]) for s in ("r", "z", "n1", "n2", "n3"))
        d1, d2, hn = (f.sb(s, [P, 2, SUPER]) for s in ("d1", "d2", "hn"))
        out = f.sb("out", [P, 2, J, D])
        bank = [f.ps(f"bank{b}") for b in range(8)]
        ps_s, ps_out, ps_r, ps_z, ps_nh, ps_ni = bank[0], bank[1], bank[2:4], bank[4:6], bank[6], bank[7]
        w_loaded, w_made, w_copied, b_made = (f.sem(s) for s in ("w_loaded", "w_made", "w_copied", "b_made"))
        idx_loaded, gathered, ht_loaded = f.sems("idx_loaded"), f.sems("gathered"), f.sems("ht_loaded")
        stored, ht_stored = f.sems("stored"), f.sems("ht_stored")
        s_turned, s_copied, r_made, z_made, nh_made, ni_made, h_turned = (
            f.sem(s) for s in ("s_turned", "s_copied", "r_made", "z_made", "nh_made", "ni_made", "h_turned"))
        r_done, z_done, n_done, n1_done, n2_done, d1_done, d2_done, h_done, out_done = (
            f.sem(s) for s in ("r_done", "z_done", "n_done", "n1_done", "n2_done", "d1_done", "d2_done",
                               "h_done", "out_done"))
        if final:
            x = f.sb("x", [P, 2, J, D])
            y = f.sb("y", [P, 2, J, D])
            ln = LayerNormBuffers(f, "ln")
            x_loaded, y_done = f.sems("x_loaded"), f.sem("y_done")
        block = ctx.enter_context(nc.Block())

        @block.sync
        def _(sp):
            for dst_, src_ in ((wt[:, :], g["msg_wt"][i]), (wih[:, :], g["wih_t"]), (whh[:, :], g["whh_t"]),
                               (b_ih[:, :], g["b_ih"].rearrange("(c p) -> p c", p=P)),
                               (b_hh[:, :], g["b_hh"].rearrange("(c p) -> p c", p=P))):
                sp.dma_start(dst_, src_, allow_slow_non_contiguous=True).then_inc(w_loaded, 16)

            def step(tile_at):
                if t := tile_at(0):
                    wait_alone(sp, gathered[t.slot], 64 * t.u)
                    sp.dma_start(idx[:, t.slot, :], list_tile(g["ptr_dst"], t)).then_inc(idx_loaded[t.slot], 16)
                    wait_alone(sp, h_done, t.n - 1)
                    sp.dma_start(ht[:, t.slot, :], fm_tile(ht_in, t)).then_inc(ht_loaded[t.slot], 16)
                    if final:
                        wait_alone(sp, out_done, t.n - 1)
                        sp.dma_start(x[:, t.slot, :, :].rearrange("p j d -> p (j d)"),
                                     nm_tile(x_res, t)).then_inc(x_loaded[t.slot], 16)
            over_tiles(sp, NT, 0, step)

        @block.gpsimd
        def _(pool):
            if final:
                nc.gpsimd.memset(ln.power[:, :], -0.5).then_inc(ln.power_set, 1)

            def step(tile_at):
                if t := tile_at(0):
                    gather_step(nc, pool, t, idx, rows, g["sums"], idx_loaded, s_turned, gathered)
                if final and (t := tile_at(2)):
                    ln.rstd(nc, pool, t)
            over_tiles(pool, NT, 2, step)

        @block.tensor
        def _(pe):
            pe.wait_ge(w_loaded, 16 * 5)
            nc.tensor.matmul(ps_s[:, 0:3 * D], wt[:, :], wih[:, :], start=True, stop=True).then_inc(w_made, 1)
            pe.wait_ge(w_copied, 1)

            def gate(bank_, c, t, sem, hidden=True, inputs=True):
                if inputs:
                    last = nc.tensor.matmul(bank_[:, :], win[:, c * D:(c + 1) * D], st[:, t.slot, :],
                                            start=True, stop=not hidden)
                if hidden:
                    last = nc.tensor.matmul(bank_[:, :], whh[:, c * D:(c + 1) * D], ht[:, t.slot, :],
                                            start=not inputs, stop=True)
                last.then_inc(sem, 1)

            def step(tile_at):
                if t := tile_at(0):
                    wait(pe, gathered[t.slot], 64 * (t.u + 1))
                    wait(pe, s_copied, t.n)
                    for j in range(J):
                        last = nc.tensor.transpose(ps_s[:, j * P:(j + 1) * P], rows[:, t.slot, j, :],
                                                   g["ident"][:, :])
                    last.then_inc(s_turned, 1)
                if t := tile_at(1):
                    wait(pe, s_copied, t.n + 1)
                    wait(pe, ht_loaded[t.slot], 16 * (t.u + 1))
                    wait(pe, r_done, t.n - 1)
                    gate(ps_r[t.slot], 0, t, r_made)
                    wait(pe, n1_done, t.n)
                    gate(ps_nh, 2, t, nh_made, inputs=False)
                    wait(pe, z_done, t.n - 1)
                    gate(ps_z[t.slot], 1, t, z_made)
                    wait(pe, n2_done, t.n)
                    gate(ps_ni, 2, t, ni_made, hidden=False)
                if t := tile_at(2):
                    wait(pe, h_done, t.n + 1)
                    wait(pe, out_done, t.n)
                    for j in range(J):
                        last = nc.tensor.transpose(ps_out[:, j * D:(j + 1) * D],
                                                   hn[:, t.slot, j * P:(j + 1) * P], g["ident"][:, :])
                    last.then_inc(h_turned, 1)
            over_tiles(pe, NT, 2, step)

        @block.vector
        def _(dve):
            dve.wait_ge(w_loaded, 16 * 5)
            nc.vector.tensor_tensor(b_rz[:, :], b_ih[:, 0:2], b_hh[:, 0:2], ALU.add).then_inc(b_made, 1)
            dve.wait_ge(w_made, 1)
            nc.vector.tensor_copy(win[:, :], ps_s[:, 0:3 * D]).then_inc(w_copied, 1)

            def step(tile_at):
                if final and (t := tile_at(3)):
                    ln.shifts(nc, dve, t)
                if t := tile_at(1):
                    wait(dve, nh_made, t.n + 1)
                    wait(dve, r_done, t.n + 1)
                    nc.vector.scalar_tensor_tensor(n1[:, t.slot, :], ps_nh[:, :], b_hh[:, 2:3], r[:, t.slot, :],
                                                   ALU.add, ALU.mult).then_inc(n1_done, 1)
                    wait(dve, n1_done, t.n + 1)
                    wait(dve, ni_made, t.n + 1)
                    wait(dve, n_done, t.n - 1)
                    nc.vector.tensor_tensor(n2[:, t.slot, :], n1[:, t.slot, :], ps_ni[:, :],
                                            ALU.add).then_inc(n2_done, 1)
                if t := tile_at(2):
                    wait(dve, n_done, t.n + 1)
                    nc.vector.tensor_tensor(d1[:, t.slot, :], ht[:, t.slot, :], n3[:, t.slot, :],
                                            ALU.subtract).then_inc(d1_done, 1)
                    wait(dve, z_done, t.n + 1)
                    wait(dve, d1_done, t.n + 1)
                    nc.vector.tensor_tensor(d2[:, t.slot, :], d1[:, t.slot, :], z[:, t.slot, :],
                                            ALU.mult).then_inc(d2_done, 1)
                    wait(dve, d2_done, t.n + 1)
                    wait(dve, h_turned, t.n - 1)
                    if not final:
                        wait(dve, ht_stored[t.slot], 16 * t.u)
                    nc.vector.tensor_tensor(hn[:, t.slot, :], d2[:, t.slot, :], n3[:, t.slot, :],
                                            ALU.add).then_inc(h_done, 1)
                if t := tile_at(2):
                    wait(dve, h_turned, t.n + 1)
                    if final:
                        wait(dve, x_loaded[t.slot], 16 * (t.u + 1))
                        wait(dve, y_done, t.n - 1)
                        nc.vector.tensor_tensor(out[:, t.slot, :, :].rearrange("p j d -> p (j d)"),
                                                ps_out[:, :], x[:, t.slot, :, :].rearrange("p j d -> p (j d)"),
                                                ALU.add).then_inc(out_done, 1)
                        wait(dve, out_done, t.n + 1)
                        ln.statistics(nc, dve, t, [out[:, t.slot, j, :] for j in range(J)], y_done)
                    else:
                        wait(dve, stored[t.slot], 16 * t.u)
                        nc.vector.tensor_copy(out[:, t.slot, :, :].rearrange("p j d -> p (j d)"),
                                              ps_out[:, :]).then_inc(out_done, 1)
            over_tiles(dve, NT, 3 if final else 2, step)

        @block.scalar
        def _(act):
            act.wait_ge(b_made, 1)

            def step(tile_at):
                if t := tile_at(0):
                    wait(act, s_turned, t.n + 1)
                    wait(act, ni_made, t.n - 1)
                    nc.scalar.activation(st[:, t.slot, :], ps_s[:, :], ACT.Copy).then_inc(s_copied, 1)
                if t := tile_at(1):
                    wait(act, r_made, t.n + 1)
                    wait(act, n1_done, t.n - 1)
                    nc.scalar.activation(r[:, t.slot, :], ps_r[t.slot][:, :], ACT.Sigmoid,
                                         bias=b_rz[:, 0:1]).then_inc(r_done, 1)
                    wait(act, z_made, t.n + 1)
                    wait(act, d2_done, t.n - 1)
                    nc.scalar.activation(z[:, t.slot, :], ps_z[t.slot][:, :], ACT.Sigmoid,
                                         bias=b_rz[:, 1:2]).then_inc(z_done, 1)
                    wait(act, n2_done, t.n + 1)
                    wait(act, h_done, t.n - 1)
                    nc.scalar.activation(n3[:, t.slot, :], n2[:, t.slot, :], ACT.Tanh,
                                         bias=b_ih[:, 2:3]).then_inc(n_done, 1)
                if final:
                    if t := tile_at(3):
                        wait(act, stored[t.slot], 16 * t.u)
                        ln.apply(nc, act, t, [out[:, t.slot, j, :] for j in range(J)],
                                 [y[:, t.slot, j, :] for j in range(J)], y_done)
                    if t := tile_at(4):
                        wait(act, y_done, t.n + 1)
                        act.dma_start(nm_tile(x_out, t), y[:, t.slot, :, :].rearrange("p j d -> p (j d)")
                                      ).then_inc(stored[t.slot], 16)
                elif t := tile_at(3):
                    wait(act, h_done, t.n + 1)
                    act.dma_start(fm_tile(ht_out, t), hn[:, t.slot, :]).then_inc(ht_stored[t.slot], 16)
                    wait(act, out_done, t.n + 1)
                    act.dma_start(nm_tile(h_out, t), out[:, t.slot, :, :].rearrange("p j d -> p (j d)")
                                  ).then_inc(stored[t.slot], 16)
            over_tiles(act, NT, 4, step)
            for b in range(2):
                act.wait_ge(stored[b], 16 * (NT // 2))
                if not final:
                    act.wait_ge(ht_stored[b], 16 * (NT // 2))


class LayerNormBuffers:

    def __init__(self, f, name):
        self.stats = f.sb(f"{name}_stats", [P, 2, J, 6])
        self.mv = f.sb(f"{name}_mv", [P, 2, J, 2])
        self.var = f.sb(f"{name}_var", [P, 2, J])
        self.inv = f.sb(f"{name}_inv", [P, 2, J])
        self.shift = f.sb(f"{name}_shift", [P, 2, J])
        self.power = f.sb(f"{name}_power", [P, J])
        self.power_set = f.sem(f"{name}_power_set")
        self.stats_done, self.mv_done, self.var_done, self.inv_done, self.shift_done = (
            f.sem(f"{name}_{s}") for s in ("stats_done", "mv_done", "var_done", "inv_done", "shift_done"))

    def statistics(self, nc, dve, t, parts, applied):
        wait(dve, applied, t.n - 1)
        for j, part in enumerate(parts):
            last = nc.vector.bn_stats(self.stats[:, t.slot, j, :], part)
        last.then_inc(self.stats_done, 1)
        wait_alone(dve, self.stats_done, t.n + 1)
        for j in range(J):
            last = nc.vector.bn_aggr(self.mv[:, t.slot, j, :], self.stats[:, t.slot, j, :])
        last.then_inc(self.mv_done, 1)
        wait(dve, self.mv_done, t.n + 1)
        nc.vector.tensor_scalar(self.var[:, t.slot, :], self.mv[:, t.slot, :, 1], EPS, None,
                                ALU.add).then_inc(self.var_done, 1)

    def rstd(self, nc, pool, t):
        if isinstance(t.n, int) and t.n == 0:
            pool.wait_ge(self.power_set, 1)
        wait(pool, self.var_done, t.n + 1)
        nc.gpsimd.tensor_tensor(self.inv[:, t.slot, :], self.var[:, t.slot, :], self.power[:, :],
                                ALU.pow).then_inc(self.inv_done, 1)

    def shifts(self, nc, dve, t):
        wait(dve, self.inv_done, t.n + 1)
        nc.vector.scalar_tensor_tensor(self.shift[:, t.slot, :], self.mv[:, t.slot, :, 0], -1.0,
                                       self.inv[:, t.slot, :], ALU.mult, ALU.mult).then_inc(self.shift_done, 1)

    def apply(self, nc, act, t, parts, outs, applied):
        wait(act, self.shift_done, t.n + 1)
        for j, (part, out) in enumerate(zip(parts, outs)):
            last = nc.scalar.activation(out, part, ACT.Identity, bias=self.shift[:, t.slot, j:j + 1],
                                        scale=self.inv[:, t.slot, j:j + 1])
        last.then_inc(applied, 1)


def mean_pass(nc, name, g, x_in, ptr, inv_count, w_x, x_out, normed, h_out=None, ht_out=None):
    with ExitStack() as ctx:
        f = Phase(nc, ctx, name)
        w = f.sb("w", [P, D])
        idx = f.sb("idx", [P, 2, J], I32)
        inv_n = f.sb("inv_n", [P, 2, J])
        rows = f.sb("rows", [P, 2, J, D])
        x = f.sb("x", [P, 2, J, D])
        xt = f.sb("xt", [P, 2, SUPER])
        v = f.sb("v", [P, 2, J, D])
        res = f.sb("res", [P, 2, J, D])
        y = f.sb("y", [P, 2, J, D])
        ln = LayerNormBuffers(f, "ln")
        ps_x, ps_v = f.ps("ps_x"), [f.ps(f"ps_v{b}") for b in range(2)]
        w_loaded = f.sem("w_loaded")
        idx_loaded, inv_loaded, x_loaded, gathered, stored = (
            f.sems(s) for s in ("idx_loaded", "inv_loaded", "x_loaded", "gathered", "stored"))
        x_turned, xt_done, product_made, v_done, res_done, y_done = (
            f.sem(s) for s in ("x_turned", "xt_done", "product_made", "v_done", "res_done", "y_done"))
        if normed:
            squares = f.sb("squares", [P, 2, J, D])
            length2 = f.sb("length2", [P, 2, J])
            inv_len = f.sb("inv_len", [P, 2, J])
            length2_done, inv_len_done = f.sem("length2_done"), f.sem("inv_len_done")
        if h_out is not None:
            lin = f.sb("lin", [P, D])
            lin_b = f.sb("lin_b", [P, 1])
            yt = f.sb("yt", [P, 2, SUPER])
            ht = f.sb("ht", [P, 2, SUPER])
            h = f.sb("h", [P, 2, SUPER])
            ps_y, ps_ht, ps_h = f.ps("ps_y"), f.ps("ps_ht"), f.ps("ps_h")
            ht_stored, h_stored = f.sems("ht_stored"), f.sems("h_stored")
            y_turned, yt_done, ht_made, ht_done, h_turned, h_done = (
                f.sem(s) for s in ("y_turned", "yt_done", "ht_made", "ht_done", "h_turned", "h_done"))
        block = ctx.enter_context(nc.Block())

        @block.sync
        def _(sp):
            sp.dma_start(w[:, :], w_x).then_inc(w_loaded, 16)
            if h_out is not None:
                sp.dma_start(lin[:, :], g["lin_wt"]).then_inc(w_loaded, 16)
                sp.dma_start(lin_b[:, :], column(g["lin_b"])).then_inc(w_loaded, 16)

            def step(tile_at):
                if t := tile_at(0):
                    wait_alone(sp, gathered[t.slot], 64 * t.u)
                    sp.dma_start(idx[:, t.slot, :], list_tile(ptr, t)).then_inc(idx_loaded[t.slot], 16)
                    wait_alone(sp, v_done, t.n - 1)
                    sp.dma_start(inv_n[:, t.slot, :], list_tile(inv_count, t)).then_inc(inv_loaded[t.slot], 16)
                    wait_alone(sp, x_turned, t.n - 1)
                    wait_alone(sp, res_done, t.n - 1)
                    sp.dma_start(flat(x[:, t.slot, :, :]), nm_tile(x_in, t)).then_inc(x_loaded[t.slot], 16)
                if h_out is not None and (t := tile_at(6)):
                    wait_alone(sp, ht_done, t.n + 1)
                    sp.dma_start(fm_tile(ht_out, t), ht[:, t.slot, :]).then_inc(ht_stored[t.slot], 16)
                    wait_alone(sp, h_done, t.n + 1)
                    sp.dma_start(nm_tile(h_out, t), h[:, t.slot, :]).then_inc(h_stored[t.slot], 16)
            over_tiles(sp, NT, 6 if h_out is not None else 0, step)
            if h_out is not None:
                for b in range(2):
                    sp.wait_ge(ht_stored[b], 16 * (NT // 2))
                    sp.wait_ge(h_stored[b], 16 * (NT // 2))

        @block.gpsimd
        def _(pool):
            nc.gpsimd.memset(ln.power[:, :], -0.5).then_inc(ln.power_set, 1)

            def step(tile_at):
                if t := tile_at(0):
                    gather_step(nc, pool, t, idx, rows, g["sums"], idx_loaded, v_done, gathered)
                if normed and (t := tile_at(1)):
                    if isinstance(t.n, int) and t.n == 0:
                        pool.wait_ge(ln.power_set, 1)
                    wait(pool, length2_done, t.n + 1)
                    nc.gpsimd.tensor_tensor(inv_len[:, t.slot, :], length2[:, t.slot, :], ln.power[:, :],
                                            ALU.pow).then_inc(inv_len_done, 1)
                if t := tile_at(2):
                    ln.rstd(nc, pool, t)
            over_tiles(pool, NT, 2, step)

        @block.tensor
        def _(pe):
            pe.wait_ge(w_loaded, 16 * (3 if h_out is not None else 1))

            def step(tile_at):
                if t := tile_at(0):
                    wait(pe, x_loaded[t.slot], 16 * (t.u + 1))
                    wait(pe, xt_done, t.n)
                    for j in range(J):
                        last = nc.tensor.transpose(ps_x[:, j * P:(j + 1) * P], x[:, t.slot, j, :], g["ident"][:, :])
                    last.then_inc(x_turned, 1)
                if h_out is not None and (t := tile_at(4)):
                    wait(pe, y_done, t.n + 1)
                    wait(pe, yt_done, t.n)
                    for j in range(J):
                        last = nc.tensor.transpose(ps_y[:, j * P:(j + 1) * P], y[:, t.slot, j, :], g["ident"][:, :])
                    last.then_inc(y_turned, 1)
                if t := tile_at(0):
                    wait(pe, xt_done, t.n + 1)
                    wait(pe, v_done, t.n - 1)
                    for j in range(J):
                        last = nc.tensor.matmul(ps_v[t.slot][:, j * D:(j + 1) * D], xt[:, t.slot, j * P:(j + 1) * P],
                                                w[:, :], start=True, stop=True)
                    last.then_inc(product_made, 1)
                if h_out is not None and (t := tile_at(5)):
                    wait(pe, yt_done, t.n + 1)
                    wait(pe, ht_done, t.n)
                    nc.tensor.matmul(ps_ht[:, :], lin[:, :], yt[:, t.slot, :], start=True,
                                     stop=True).then_inc(ht_made, 1)
                    wait(pe, ht_done, t.n + 1)
                    wait(pe, h_done, t.n)
                    for j in range(J):
                        last = nc.tensor.transpose(ps_h[:, j * D:(j + 1) * D], ht[:, t.slot, j * P:(j + 1) * P],
                                                   g["ident"][:, :])
                    last.then_inc(h_turned, 1)
            over_tiles(pe, NT, 5 if h_out is not None else 0, step)

        @block.vector
        def _(dve):
            def step(tile_at):
                if t := tile_at(1):
                    wait(dve, gathered[t.slot], 64 * (t.u + 1))
                    wait(dve, inv_loaded[t.slot], 16 * (t.u + 1))
                    wait(dve, product_made, t.n + 1)
                    wait(dve, res_done, t.n - 1)
                    if normed:
                        wait(dve, length2_done, t.n - 1)
                    for j in range(J):
                        last = nc.vector.scalar_tensor_tensor(
                            v[:, t.slot, j, :], rows[:, t.slot, j, :], inv_n[:, t.slot, j:j + 1],
                            ps_v[t.slot][:, j * D:(j + 1) * D], ALU.mult, ALU.add)
                    last.then_inc(v_done, 1)
                if t := tile_at(3):
                    ln.shifts(nc, dve, t)
                if t := tile_at(2):
                    if normed:
                        wait(dve, inv_len_done, t.n + 1)
                    wait(dve, y_done, t.n - 1)
                    wait(dve, v_done, t.n + 1)
                    wait(dve, x_loaded[t.slot], 16 * (t.u + 1))
                    if normed:
                        for j in range(J):
                            last = nc.vector.scalar_tensor_tensor(
                                res[:, t.slot, j, :], v[:, t.slot, j, :], inv_len[:, t.slot, j:j + 1],
                                x[:, t.slot, j, :], ALU.mult, ALU.add)
                    else:
                        last = nc.vector.tensor_tensor(flat(res[:, t.slot, :, :]), flat(v[:, t.slot, :, :]),
                                                       flat(x[:, t.slot, :, :]), ALU.add)
                    last.then_inc(res_done, 1)
                    wait(dve, res_done, t.n + 1)
                    ln.statistics(nc, dve, t, [res[:, t.slot, j, :] for j in range(J)], y_done)
                if h_out is not None and (t := tile_at(5)):
                    wait(dve, h_turned, t.n + 1)
                    wait(dve, h_stored[t.slot], 16 * t.u)
                    nc.vector.tensor_copy(h[:, t.slot, :], ps_h[:, :]).then_inc(h_done, 1)
            over_tiles(dve, NT, 5 if h_out is not None else 3, step)

        @block.scalar
        def _(act):
            act.wait_ge(w_loaded, 16 * (3 if h_out is not None else 1))

            def step(tile_at):
                if t := tile_at(0):
                    wait(act, x_turned, t.n + 1)
                    wait(act, product_made, t.n - 1)
                    nc.scalar.activation(xt[:, t.slot, :], ps_x[:, :], ACT.Copy).then_inc(xt_done, 1)
                if normed and (t := tile_at(1)):
                    wait(act, v_done, t.n + 1)
                    wait(act, inv_len_done, t.n - 1)
                    for j in range(J):
                        last = nc.scalar.activation(squares[:, t.slot, j, :], v[:, t.slot, j, :], ACT.Square,
                                                    accum_out=length2[:, t.slot, j:j + 1])
                    last.then_inc(length2_done, 1)
                if t := tile_at(3):
                    wait(act, stored[t.slot], 16 * t.u)
                    if h_out is not None:
                        wait(act, y_turned, t.n - 1)
                    ln.apply(nc, act, t, [res[:, t.slot, j, :] for j in range(J)],
                             [y[:, t.slot, j, :] for j in range(J)], y_done)
                if t := tile_at(4):
                    wait(act, y_done, t.n + 1)
                    act.dma_start(nm_tile(x_out, t), flat(y[:, t.slot, :, :])).then_inc(stored[t.slot], 16)
                    if h_out is not None:
                        wait(act, y_turned, t.n + 1)
                        wait(act, ht_made, t.n - 1)
                        nc.scalar.activation(yt[:, t.slot, :], ps_y[:, :], ACT.Copy).then_inc(yt_done, 1)
                if h_out is not None and (t := tile_at(5)):
                    wait(act, ht_made, t.n + 1)
                    wait(act, ht_stored[t.slot], 16 * t.u)
                    wait(act, h_turned, t.n - 1)
                    nc.scalar.activation(ht[:, t.slot, :], ps_ht[:, :], ACT.Identity,
                                         bias=lin_b[:, :]).then_inc(ht_done, 1)
            over_tiles(act, NT, 5 if h_out is not None else 4, step)
            for b in range(2):
                act.wait_ge(stored[b], 16 * (NT // 2))


def attention_pass(nc, name, g):
    with ExitStack() as ctx:
        f = Phase(nc, ctx, name)
        qw, kw, vw, ow = (f.sb(s, [P, D]) for s in ("qw", "kw", "vw", "ow"))
        qb, kb, vb, eb = (f.sb(s, [P, 1]) for s in ("qb", "kb", "vb", "eb"))
        ew = f.sb("ew", [EDIM, HEADS])
        ew_rows = f.sb("ew_rows", [EDIM, HEADS, HEAD_DIM])
        eb_row = f.sb("eb_row", [1, HEADS])
        ones = f.sb("ones", [1, 1])
        eb_wide = f.sb("eb_wide", [1, HEADS, HEAD_DIM])
        ob = f.sb("ob", [P, D])
        blocks = f.sb("blocks", [P, HEADS, HEAD_DIM])
        heads = f.sb("heads", [P, HEADS])
        idx = f.sb("idx", [P, 2, J, 2], I32)
        send = f.sb("send", [P, 2, J, D])
        recv = f.sb("recv", [P, 2, J, D])
        edge_t = f.sb("edge_t", [EDIM, 2, SUPER])
        keep = f.sb("keep", [P, 2, SUPER], BF16)
        cut = f.sb("cut", [P, 2, SUPER], BF16)
        send_t, recv_t, q, v, qk, s = (f.sb(n, [P, 2, SUPER]) for n in ("send_t", "recv_t", "q", "v", "qk", "s"))
        top = f.sb("top", [P, 2, SUPER + 1])
        drop = f.sb("drop", [P, 2, SUPER])
        arg = f.sb("arg", [P, 2, 2, SUPER])
        ex = f.sb("ex", [P, 2, 2, SUPER])
        pv, den, num, att = (f.sb(n, [P, 2, SUPER]) for n in ("pv", "den", "num", "att"))
        den_max = f.sb("den_max", [P, 2, J, HEADS])
        den_inv = f.sb("den_inv", [P, 2, J, HEADS])
        inv_wide = f.sb("inv_wide", [P, 2, J, HEADS, HEAD_DIM])
        out = f.sb("out", [P, 2, SUPER])
        ps_send, ps_recv, ps_q, ps_k, ps_v, ps_s, ps_inv, ps_out = (
            f.ps(n) for n in ("ps_send", "ps_recv", "ps_q", "ps_k", "ps_v", "ps_s", "ps_inv", "ps_out"))
        w_loaded, consts_set, eb_made, eb_done, ew_done = (
            f.sem(n) for n in ("w_loaded", "consts_set", "eb_made", "eb_done", "ew_done"))
        idx_loaded, edge_loaded, keep_loaded, cut_loaded, sent, received, stored = (
            f.sems(n) for n in ("idx_loaded", "edge_loaded", "keep_loaded", "cut_loaded", "sent", "received", "stored"))
        (rows_turned, send_done, recv_done, q_made, k_made, v_made, q_done, v_done, qk_done, s_made, s_done,
         carry_done, top_done, arg0_done, drop_done, arg_done, ex_done, pv_done, den_done, num_done,
         den_made, max_done, inv_done, wide_done, inv_turned, att_done, out_made, out_done) = (
            f.sem(n) for n in ("rows_turned", "send_done", "recv_done", "q_made", "k_made", "v_made", "q_done",
                               "v_done", "qk_done", "s_made", "s_done", "carry_done", "top_done", "arg0_done",
                               "drop_done", "arg_done", "ex_done", "pv_done", "den_done", "num_done", "den_made",
                               "max_done", "inv_done", "wide_done", "inv_turned", "att_done", "out_made",
                               "out_done"))
        loads = 12
        block = ctx.enter_context(nc.Block())

        @block.sync
        def _(sp):
            for dst_, src_ in ((qw[:, :], g["qW"]), (kw[:, :], g["kW"]), (vw[:, :], g["vW"]), (ow[:, :], g["oW"]),
                               (qb[:, :], column(g["qb"])), (kb[:, :], column(g["kb"])), (vb[:, :], column(g["vb"])),
                               (ew[:, :], g["eW"]), (ob[:, :], on_all(g["ob"])),
                               (eb_row[:, :], g["eb"].rearrange("(a n) -> a n", a=1)),
                               (blocks[:, :, :], g["blocks_c"]), (heads[:, :], g["heads_c"])):
                sp.dma_start(dst_, src_, allow_slow_non_contiguous=True).then_inc(w_loaded, 16)

            def step(tile_at):
                if t := tile_at(0):
                    wait_alone(sp, sent[t.slot], 64 * t.u)
                    wait_alone(sp, received[t.slot], 64 * t.u)
                    sp.dma_start(idx[:, t.slot, :, :].rearrange("p j c -> p (j c)"),
                                 nm_tile(g["by_dst"], t)).then_inc(idx_loaded[t.slot], 16)
                    wait_alone(sp, s_made, t.n - 1)
                    sp.dma_start(edge_t[:, t.slot, :], g["edge_attr_t"][:, bass.ds(t.n * SUPER, SUPER)]
                                 ).then_inc(edge_loaded[t.slot], 16)
                    wait_alone(sp, drop_done, t.n - 1)
                    wait_alone(sp, arg_done, t.n - 1)
                    sp.dma_start(cut[:, t.slot, :], row_tile(g["cut_dst"], t)).then_inc(cut_loaded[t.slot], 16)
            over_tiles(sp, ET, 0, step)

        @block.gpsimd
        def _(pool):
            def step(tile_at):
                if t := tile_at(0):
                    wait(pool, idx_loaded[t.slot], 16 * (t.u + 1))
                    wait(pool, rows_turned, t.n - 1)
                    pool.nop(nofuse=True)
                    for j in range(J):
                        for col, rows, sem in ((1, send, sent), (0, recv, received)):
                            nc.gpsimd.indirect_dma_start(
                                out=rows[:, t.slot, j, :], out_offset=None, in_=g["x_in"][:, :],
                                in_offset=bass.IndirectOffsetOnAxis(ap=idx[:, t.slot, j, col:col + 1], axis=0)).then_inc(sem[t.slot], 16)
            over_tiles(pool, ET, 0, step)

        @block.tensor
        def _(pe):
            pe.wait_ge(w_loaded, 16 * loads)
            pe.wait_ge(eb_done, 1)
            nc.tensor.matmul(ps_s[:, 0:1], eb_wide[:, :, :].rearrange("a h d -> a (h d)"), ones[:, :],
                             start=True, stop=True).then_inc(eb_made, 1)
            pe.wait_ge(eb_done, 2)
            pe.wait_ge(ew_done, 1)

            def step(tile_at):
                if t := tile_at(0):
                    wait(pe, sent[t.slot], 64 * (t.u + 1))
                    wait(pe, send_done, t.n)
                    for j in range(J):
                        nc.tensor.transpose(edge_columns(ps_send[:, :])[:, j, :], send[:, t.slot, j, :], g["ident"][:, :])
                    wait(pe, received[t.slot], 64 * (t.u + 1))
                    wait(pe, recv_done, t.n)
                    for j in range(J):
                        last = nc.tensor.transpose(edge_columns(ps_recv[:, :])[:, j, :], recv[:, t.slot, j, :],
                                                   g["ident"][:, :])
                    last.then_inc(rows_turned, 1)
                if t := tile_at(2):
                    wait(pe, den_done, t.n + 1)
                    wait(pe, att_done, t.n)
                    for j in range(J):
                        last = nc.tensor.matmul(ps_inv[:, j * HEADS:(j + 1) * HEADS],
                                                edge_columns(den[:, t.slot, :])[:, j, :], heads[:, :],
                                                start=True, stop=True)
                    last.then_inc(den_made, 1)
                if t := tile_at(0):
                    wait(pe, send_done, t.n + 1)
                    wait(pe, q_done, t.n)
                    nc.tensor.matmul(ps_q[:, :], qw[:, :], send_t[:, t.slot, :], start=True,
                                     stop=True).then_inc(q_made, 1)
                    wait(pe, recv_done, t.n + 1)
                    wait(pe, qk_done, t.n)
                    nc.tensor.matmul(ps_k[:, :], kw[:, :], recv_t[:, t.slot, :], start=True,
                                     stop=True).then_inc(k_made, 1)
                    wait(pe, v_done, t.n)
                    nc.tensor.matmul(ps_v[:, :], vw[:, :], send_t[:, t.slot, :], start=True,
                                     stop=True).then_inc(v_made, 1)
                if t := tile_at(2):
                    wait(pe, wide_done, t.n + 1)
                    wait(pe, inv_done, t.n + 1)
                    for j in range(J):
                        last = nc.tensor.transpose(edge_columns(ps_inv[:, :])[:, j, :],
                                                   inv_wide[:, t.slot, j, :, :].rearrange("p h d -> p (h d)"),
                                                   g["ident"][:, :])
                    last.then_inc(inv_turned, 1)
                if t := tile_at(0):
                    wait(pe, qk_done, t.n + 1)
                    wait(pe, edge_loaded[t.slot], 16 * (t.u + 1))
                    wait(pe, s_done, t.n)
                    nc.tensor.matmul(ps_s[:, :], blocks[:, :, :].rearrange("p h d -> p (h d)"), qk[:, t.slot, :],
                                     start=True, stop=False)
                    nc.tensor.matmul(ps_s[:, :], ew_rows[:, :, :].rearrange("p h d -> p (h d)"),
                                     edge_t[:, t.slot, :], start=False, stop=True).then_inc(s_made, 1)
                if t := tile_at(2):
                    wait(pe, att_done, t.n + 1)
                    wait(pe, out_done, t.n)
                    for j in range(J):
                        last = nc.tensor.matmul(ps_out[:, j * D:(j + 1) * D], edge_columns(att[:, t.slot, :])[:, j, :],
                                                ow[:, :], start=True, stop=True)
                    last.then_inc(out_made, 1)
            over_tiles(pe, ET, 2, step)

        @block.vector
        def _(dve):
            dve.wait_ge(w_loaded, 16 * loads)
            nc.vector.memset(ones[:, :], 1.0).then_inc(consts_set, 1)
            dve.wait_ge(consts_set, 1)
            nc.vector.tensor_copy(eb_wide[:, :, :], eb_row[:, :].unsqueeze(2).broadcast_to([1, HEADS, HEAD_DIM])
                                  ).then_inc(eb_done, 1)
            nc.vector.tensor_copy(ew_rows[:, :, :], ew[:, :].unsqueeze(2).broadcast_to([EDIM, HEADS, HEAD_DIM])
                                  ).then_inc(ew_done, 1)
            dve.wait_ge(eb_made, 1)
            nc.vector.tensor_copy(eb[:, :], ps_s[:, 0:1]).then_inc(eb_done, 1)

            def step(tile_at):
                if t := tile_at(0):
                    wait(dve, k_made, t.n + 1)
                    wait(dve, q_done, t.n + 1)
                    wait(dve, s_made, t.n - 1)
                    nc.vector.scalar_tensor_tensor(qk[:, t.slot, :], ps_k[:, :], kb[:, :], q[:, t.slot, :],
                                                   ALU.add, ALU.mult).then_inc(qk_done, 1)
                if t := tile_at(2):
                    wait(dve, den_made, t.n + 1)
                    nc.vector.tensor_scalar(den_max[:, t.slot, :, :].rearrange("p j h -> p (j h)"),
                                            ps_inv[:, 0:J * HEADS], 1e-8, None, ALU.max).then_inc(max_done, 1)
                    wait(dve, max_done, t.n + 1)
                    wait(dve, wide_done, t.n - 1)
                    nc.vector.reciprocal(den_inv[:, t.slot, :, :].rearrange("p j h -> p (j h)"),
                                         den_max[:, t.slot, :, :].rearrange("p j h -> p (j h)")).then_inc(inv_done, 1)
                if t := tile_at(1):
                    wait(dve, top_done, t.n)
                    wait(dve, arg_done, t.n - 1)
                    prev = top[:, 1 - t.slot, SUPER:SUPER + 1]
                    first = isinstance(t.n, int) and t.n == 0
                    if first:
                        nc.vector.memset(top[:, 0, 0:1], 0.0).then_inc(carry_done, 1)
                    else:
                        nc.vector.tensor_copy(top[:, t.slot, 0:1], prev).then_inc(carry_done, 1)
                    wait(dve, carry_done, t.n + 1)
                    wait(dve, cut_loaded[t.slot], 16 * (t.u + 1))
                    wait(dve, s_done, t.n + 1)
                    nc.vector.tensor_tensor_scan(top[:, t.slot, 1:SUPER + 1], cut[:, t.slot, :], s[:, t.slot, :],
                                                 top[:, t.slot, 0:1], ALU.add, ALU.max).then_inc(top_done, 1)
                    wait(dve, top_done, t.n + 1)
                    wait(dve, ex_done, t.n - 1)
                    nc.vector.tensor_tensor(arg[:, t.slot, 0, :], s[:, t.slot, :], top[:, t.slot, 1:SUPER + 1],
                                            ALU.subtract).then_inc(arg0_done, 1)
                    nc.vector.tensor_tensor(drop[:, t.slot, :], top[:, t.slot, 0:SUPER], cut[:, t.slot, :],
                                            ALU.add).then_inc(drop_done, 1)
                    wait(dve, drop_done, t.n + 1)
                    nc.vector.tensor_tensor(arg[:, t.slot, 1, :], drop[:, t.slot, :], top[:, t.slot, 1:SUPER + 1],
                                            ALU.subtract).then_inc(arg_done, 1)
                if t := tile_at(2):
                    wait(dve, inv_turned, t.n + 1)
                    wait(dve, out_made, t.n - 1)
                    nc.vector.tensor_tensor(att[:, t.slot, :], num[:, t.slot, :], ps_inv[:, :],
                                            ALU.mult).then_inc(att_done, 1)
                if t := tile_at(1):
                    wait(dve, ex_done, t.n + 1)
                    wait(dve, v_done, t.n + 1)
                    nc.vector.tensor_tensor(pv[:, t.slot, :], v[:, t.slot, :], ex[:, t.slot, 0, :],
                                            ALU.mult).then_inc(pv_done, 1)
                    first = isinstance(t.n, int) and t.n == 0
                    wait(dve, den_made, t.n - 1)
                    wait(dve, den_done, t.n)
                    nc.vector.tensor_tensor_scan(
                        den[:, t.slot, :], ex[:, t.slot, 1, :], ex[:, t.slot, 0, :],
                        0.0 if first else den[:, 1 - t.slot, SUPER - 1:SUPER],
                        ALU.mult, ALU.add).then_inc(den_done, 1)
                    wait(dve, pv_done, t.n + 1)
                    wait(dve, num_done, t.n)
                    wait(dve, att_done, t.n - 1)
                    nc.vector.tensor_tensor_scan(
                        num[:, t.slot, :], ex[:, t.slot, 1, :], pv[:, t.slot, :],
                        0.0 if first else num[:, 1 - t.slot, SUPER - 1:SUPER],
                        ALU.mult, ALU.add).then_inc(num_done, 1)
                if t := tile_at(2):
                    wait(dve, out_made, t.n + 1)
                    wait(dve, stored[t.slot], 16 * t.u)
                    nc.vector.tensor_tensor(
                        out[:, t.slot, :].rearrange("p (j d) -> p j d", j=J),
                        ps_out[:, :].rearrange("p (j d) -> p j d", j=J),
                        ob[:, :].unsqueeze(1).broadcast_to([P, J, D]), ALU.add).then_inc(out_done, 1)
            over_tiles(dve, ET, 2, step)

        @block.scalar
        def _(act):
            act.wait_ge(w_loaded, 16 * loads)
            act.wait_ge(eb_done, 2)

            def step(tile_at):
                if t := tile_at(0):
                    wait(act, rows_turned, t.n + 1)
                    wait(act, v_made, t.n - 1)
                    nc.scalar.activation(send_t[:, t.slot, :], ps_send[:, :], ACT.Copy).then_inc(send_done, 1)
                    nc.scalar.activation(recv_t[:, t.slot, :], ps_recv[:, :], ACT.Copy).then_inc(recv_done, 1)
                    wait(act, q_made, t.n + 1)
                    wait(act, qk_done, t.n - 1)
                    nc.scalar.activation(q[:, t.slot, :], ps_q[:, :], ACT.Identity, bias=qb[:, :]).then_inc(q_done, 1)
                if t := tile_at(2):
                    wait(act, inv_done, t.n + 1)
                    wait(act, inv_turned, t.n - 1)
                    nc.scalar.activation(
                        inv_wide[:, t.slot, :, :, :].rearrange("p j h d -> p (j h) d"),
                        den_inv[:, t.slot, :, :].rearrange("p j h -> p (j h)").unsqueeze(2).broadcast_to(
                            [P, J * HEADS, HEAD_DIM]), ACT.Copy).then_inc(wide_done, 1)
                if t := tile_at(1):
                    wait(act, arg0_done, t.n + 1)
                    wait(act, arg_done, t.n + 1)
                    wait(act, num_done, t.n - 1)
                    nc.scalar.activation(ex[:, t.slot, :, :].rearrange("p a n -> p (a n)"),
                                         arg[:, t.slot, :, :].rearrange("p a n -> p (a n)"), ACT.Exp
                                         ).then_inc(ex_done, 1)
                if t := tile_at(0):
                    wait(act, v_made, t.n + 1)
                    wait(act, pv_done, t.n - 1)
                    nc.scalar.activation(v[:, t.slot, :], ps_v[:, :], ACT.Identity, bias=vb[:, :]).then_inc(v_done, 1)
                    wait(act, s_made, t.n + 1)
                    wait(act, arg0_done, t.n - 1)
                    nc.scalar.activation(s[:, t.slot, :], ps_s[:, :], ACT.Identity, bias=eb[:, :]).then_inc(s_done, 1)
                if t := tile_at(3):
                    wait(act, out_done, t.n + 1)
                    act.dma_start(nm_tile(g["att_sums"], t), out[:, t.slot, :]).then_inc(stored[t.slot], 16)
            over_tiles(act, ET, 3, step)
            for b in range(2):
                act.wait_ge(stored[b], 16 * (ET // 2))


def ffn_pass(nc, name, g):
    with ExitStack() as ctx:
        f = Phase(nc, ctx, name)
        C = FFN // P
        f1, f1c = f.sb("f1", [P, FFN]), f.sb("f1c", [P, FFN])
        fb, fbc, rest1, rest2 = (f.sb(s, [P, FFN]) for s in ("fb", "fbc", "rest1", "rest2"))
        hi, mid, lo, bias_rows = (f.sb(s, [P, FFN], BF16) for s in ("hi", "mid", "lo", "bias_rows"))
        ones = f.sb("ones", [P, P], BF16)
        total, mean = f.sb("total", [P, 2]), f.sb("mean", [P, 2])
        f2 = f.sb("f2", [P, C, D])
        g1, b1, f2b = (f.sb(s, [P, 1]) for s in ("g1", "b1", "f2b"))
        gf, bf = f.sb("gf", [P, C]), f.sb("bf", [P, C])
        g2, b2 = f.sb("g2", [P, D]), f.sb("b2", [P, D])
        idx = f.sb("idx", [P, 2, J], I32)
        rows, x, xr, a, xh, u, xb, z, y = (f.sb(s, [P, 2, J, D])
                                           for s in ("rows", "x", "xr", "a", "xh", "u", "xb", "z", "y"))
        x1t, y2t = f.sb("x1t", [P, 2, SUPER]), f.sb("y2t", [P, 2, SUPER])
        squares = f.sb("squares", [P, J, FFN])
        sumsq, varf, invf = (f.sb(s, [P, 2, J]) for s in ("sumsq", "varf", "invf"))
        hs = f.sb("hs", [P, J, FFN])
        hg = f.sb("hg", [P, C, SUPER])
        ln1, ln2, ln3 = (LayerNormBuffers(f, s) for s in ("ln1", "ln2", "ln3"))
        ps_h = [f.ps(f"ps_h{j}") for j in range(J)]
        ps_g = [f.ps(f"ps_g{b}") for b in range(2)]
        ps_f, ps_t = f.ps("ps_f"), f.ps("ps_t")
        idx_loaded, x_loaded, xr_loaded, gathered, stored = (
            f.sems(s) for s in ("idx_loaded", "x_loaded", "xr_loaded", "gathered", "stored"))
        (w_loaded, ones_set, total_done, mean_done, centred, hi_done, rest1_done, mid_done, rest2_done,
         lo_done, rows_done) = (
            f.sem(s) for s in ("w_loaded", "ones_set", "total_done", "mean_done", "centred", "hi_done",
                               "rest1_done", "mid_done", "rest2_done", "lo_done", "rows_done"))
        (a_done, xh_done, xh_turned, x1t_done, h_made, sumsq_done, varf_done, invf_done, hs_done, g_turned, gelu_done,
         f2_made, y2t_done, y2_turned, u_done, xb_done, z_done, y_done) = (
            f.sem(s) for s in ("a_done", "xh_done", "xh_turned", "x1t_done", "h_made", "sumsq_done", "varf_done",
                               "invf_done", "hs_done", "g_turned", "gelu_done", "f2_made", "y2t_done", "y2_turned",
                               "u_done", "xb_done", "z_done", "y_done"))
        power = ln1.power
        loads = 11
        block = ctx.enter_context(nc.Block())

        @block.sync
        def _(sp):
            for dst_, src_ in ((f1[:, :], g["f1W"]), (fb[:, :], on_all(g["f1b"])),
                               (f2[:, :, :], g["f2W"].rearrange("(c p) d -> p c d", p=P)),
                               (g1[:, :], column(g["ln1_g"])), (b1[:, :], column(g["ln1_b"])), (f2b[:, :], column(g["f2b"])),
                               (gf[:, :], g["lnf_g"].rearrange("(c p) -> p c", p=P)),
                               (bf[:, :], g["lnf_b"].rearrange("(c p) -> p c", p=P)),
                               (g2[:, :], on_all(g["ln2_g"])), (b2[:, :], on_all(g["ln2_b"]))):
                sp.dma_start(dst_, src_, allow_slow_non_contiguous=True).then_inc(w_loaded, 16)

            def step(tile_at):
                if t := tile_at(0):
                    wait_alone(sp, gathered[t.slot], 64 * t.u)
                    sp.dma_start(idx[:, t.slot, :], list_tile(g["ptr_dst"], t)).then_inc(idx_loaded[t.slot], 16)
                    wait_alone(sp, a_done, t.n - 1)
                    sp.dma_start(flat(x[:, t.slot, :, :]), nm_tile(g["x_in"], t)).then_inc(x_loaded[t.slot], 16)
                if t := tile_at(3):
                    wait_alone(sp, xb_done, t.n - 1)
                    sp.dma_start(flat(xr[:, t.slot, :, :]), nm_tile(g["x_in"], t)).then_inc(xr_loaded[t.slot], 16)
            over_tiles(sp, NT, 3, step)

        @block.gpsimd
        def _(pool):
            nc.gpsimd.memset(power[:, :], -0.5).then_inc(ln1.power_set, 1)
            pool.wait_ge(ln1.power_set, 1)
            pool.wait_ge(w_loaded, 16 * (loads - 1))

            def gather(t, js):
                for j in js:
                    nc.gpsimd.indirect_dma_start(
                        out=rows[:, t.slot, j, :], out_offset=None, in_=g["att_sums"][:, :],
                        in_offset=bass.IndirectOffsetOnAxis(ap=idx[:, t.slot, j:j + 1], axis=0)).then_inc(gathered[t.slot], 16)

            def inverse_root(out, var, ready, done, t):
                wait(pool, ready, t.n + 1)
                nc.gpsimd.tensor_tensor(out[:, t.slot, :], var[:, t.slot, :], power[:, :], ALU.pow).then_inc(done, 1)

            def step(tile_at):
                if t := tile_at(3):
                    inverse_root(invf, varf, varf_done, invf_done, t)
                if t := tile_at(1):
                    wait(pool, gathered[t.slot], 64 * (t.u + 1))
                    wait(pool, x_loaded[t.slot], 16 * (t.u + 1))
                    wait(pool, xh_done, t.n - 1)
                    wait(pool, ln1.stats_done, t.n - 1)
                    nc.gpsimd.tensor_tensor(flat(a[:, t.slot, :, :]), flat(rows[:, t.slot, :, :]),
                                            flat(x[:, t.slot, :, :]), ALU.add).then_inc(a_done, 1)
                if t := tile_at(4):
                    inverse_root(ln2.inv, ln2.var, ln2.var_done, ln2.inv_done, t)
                if t := tile_at(3):
                    wait(pool, xr_loaded[t.slot], 16 * (t.u + 1))
                    wait(pool, z_done, t.n - 1)
                    nc.gpsimd.tensor_tensor(xb[:, t.slot, :, :], xr[:, t.slot, :, :],
                                            b2[:, :].unsqueeze(1).broadcast_to([P, J, D]), ALU.add
                                            ).then_inc(xb_done, 1)
                if t := tile_at(0):
                    wait(pool, idx_loaded[t.slot], 16 * (t.u + 1))
                    wait(pool, a_done, t.n - 1)
                    pool.nop(nofuse=True)
                    gather(t, (0, 1))
                if t := tile_at(1):
                    inverse_root(ln1.inv, ln1.var, ln1.var_done, ln1.inv_done, t)
                if t := tile_at(0):
                    gather(t, (2, 3))
                if t := tile_at(4):
                    inverse_root(ln3.inv, ln3.var, ln3.var_done, ln3.inv_done, t)
            over_tiles(pool, NT, 4, step)

        @block.tensor
        def _(pe):
            pe.wait_ge(w_loaded, 16 * (loads - 1))
            pe.wait_ge(rows_done, 3)
            pe.wait_ge(centred, 2)
            pe.wait_ge(ones_set, 2)

            def step(tile_at):
                if t := tile_at(2):
                    wait(pe, xh_done, t.n + 1)
                    wait(pe, u_done, t.n - 1)
                    wait(pe, x1t_done, t.n)
                    for j in range(J):
                        last = nc.tensor.transpose(ps_t[:, j * P:(j + 1) * P], xh[:, t.slot, j, :], g["ident"][:, :])
                    last.then_inc(xh_turned, 1)
                if t := tile_at(3):
                    wait(pe, hs_done, t.n + 1)
                    wait(pe, y2t_done, t.n)

                    def turn(c):
                        wait(pe, gelu_done, 4 * t.n + c - 1)
                        for j in range(J):
                            last = nc.tensor.transpose(ps_g[c % 2][:, j * P:(j + 1) * P],
                                                       hs[:, j, c * P:(c + 1) * P], g["ident"][:, :])
                        last.then_inc(g_turned, 1)

                    def down(c):
                        wait(pe, gelu_done, 4 * t.n + c + 1)
                        last = nc.tensor.matmul(ps_f[:, :], f2[:, c, :], hg[:, c, :], start=c == 0, stop=c == C - 1)
                        if c == C - 1:
                            last.then_inc(f2_made, 1)
                    turn(0)
                    turn(1)
                    for c in range(C):
                        down(c)
                        if c + 2 < C:
                            turn(c + 2)
                if t := tile_at(2):
                    wait(pe, x1t_done, t.n + 1)
                    wait(pe, hs_done, t.n)
                    for j in range(J):
                        nc.tensor.matmul(ps_h[j][:, :], x1t[:, t.slot, j * P:(j + 1) * P], f1c[:, :],
                                         start=True, stop=False)
                        nc.tensor.matmul(ps_h[j][:, :], ones[:, :], bias_rows[:, :], start=False,
                                         stop=True).then_inc(h_made, 1)
                if t := tile_at(3):
                    wait(pe, y2t_done, t.n + 1)
                    wait(pe, x1t_done, t.n + 2 if not isinstance(t.n, int) else min(t.n + 2, NT))
                    for j in range(J):
                        last = nc.tensor.transpose(ps_t[:, j * D:(j + 1) * D], y2t[:, t.slot, j * P:(j + 1) * P],
                                                   g["ident"][:, :])
                    last.then_inc(y2_turned, 1)
            over_tiles(pe, NT, 3, step)

        @block.vector
        def _(dve):
            dve.wait_ge(w_loaded, 16 * (loads - 1))
            nc.vector.memset(ones[:, :], 1.0).then_inc(ones_set, 1)
            nc.vector.memset(bias_rows[:, :], 0.0).then_inc(ones_set, 1)
            nc.vector.reduce_sum(total[:, 0:1], f1[:, :], axis=AX.X).then_inc(total_done, 1)
            nc.vector.reduce_sum(total[:, 1:2], fb[:, :], axis=AX.X).then_inc(total_done, 1)
            dve.wait_ge(total_done, 2)
            nc.vector.tensor_scalar(mean[:, :], total[:, :], 1.0 / FFN, None, ALU.mult).then_inc(mean_done, 1)
            dve.wait_ge(mean_done, 1)
            nc.vector.tensor_scalar(f1c[:, :], f1[:, :], mean[:, 0:1], None, ALU.subtract).then_inc(centred, 1)
            nc.vector.tensor_scalar(fbc[:, :], fb[:, :], mean[:, 1:2], None, ALU.subtract).then_inc(centred, 1)
            dve.wait_ge(centred, 2)
            nc.vector.tensor_copy(hi[:, :], fbc[:, :]).then_inc(hi_done, 1)
            dve.wait_ge(hi_done, 1)
            nc.vector.tensor_tensor(rest1[:, :], fbc[:, :], hi[:, :], ALU.subtract).then_inc(rest1_done, 1)
            dve.wait_ge(rest1_done, 1)
            nc.vector.tensor_copy(mid[:, :], rest1[:, :]).then_inc(mid_done, 1)
            dve.wait_ge(mid_done, 1)
            nc.vector.tensor_tensor(rest2[:, :], rest1[:, :], mid[:, :], ALU.subtract).then_inc(rest2_done, 1)
            dve.wait_ge(rest2_done, 1)
            nc.vector.tensor_copy(lo[:, :], rest2[:, :]).then_inc(lo_done, 1)
            dve.wait_ge(lo_done, 1)
            dve.wait_ge(ones_set, 2)
            for row, part in ((0, hi), (32, mid), (64, lo)):
                nc.vector.tensor_copy(bias_rows[row:row + 1, :], part[row:row + 1, :]).then_inc(rows_done, 1)

            def step(tile_at):
                if t := tile_at(2):
                    wait(dve, ln1.inv_done, t.n + 1)
                    wait(dve, xh_turned, t.n - 1)
                    for j in range(J):
                        last = nc.vector.tensor_scalar(xh[:, t.slot, j, :], a[:, t.slot, j, :],
                                                       ln1.mv[:, t.slot, j, 0:1], ln1.inv[:, t.slot, j:j + 1],
                                                       ALU.subtract, ALU.mult)
                    last.then_inc(xh_done, 1)
                if t := tile_at(3):
                    wait(dve, invf_done, t.n + 1)
                    wait(dve, g_turned, 4 * t.n)
                    for j in range(J):
                        last = nc.vector.tensor_scalar(hs[:, j, :], ps_h[j][:, :], invf[:, t.slot, j:j + 1], None,
                                                       ALU.mult)
                    last.then_inc(hs_done, 1)
                if t := tile_at(1):
                    wait(dve, a_done, t.n + 1)
                    ln1.statistics(nc, dve, t, [a[:, t.slot, j, :] for j in range(J)], xh_done)
                if t := tile_at(4):
                    wait(dve, ln2.inv_done, t.n + 1)
                    wait(dve, xb_done, t.n + 1)
                    wait(dve, u_done, t.n + 1)
                    wait(dve, y_done, t.n - 1)
                    for j in range(J):
                        last = nc.vector.scalar_tensor_tensor(z[:, t.slot, j, :], u[:, t.slot, j, :],
                                                              ln2.inv[:, t.slot, j:j + 1], xb[:, t.slot, j, :],
                                                              ALU.mult, ALU.add)
                    last.then_inc(z_done, 1)
                    wait(dve, z_done, t.n + 1)
                    ln3.statistics(nc, dve, t, [z[:, t.slot, j, :] for j in range(J)], y_done)
                if t := tile_at(5):
                    ln3.shifts(nc, dve, t)
                if t := tile_at(3):
                    wait(dve, f2_made, t.n + 1)
                    wait(dve, y2_turned, t.n - 1)
                    nc.vector.scalar_tensor_tensor(y2t[:, t.slot, :], ps_f[:, :], f2b[:, :], x1t[:, t.slot, :],
                                                   ALU.add, ALU.add).then_inc(y2t_done, 1)
                if t := tile_at(2):
                    wait(dve, sumsq_done, t.n + 1)
                    wait(dve, invf_done, t.n - 1)
                    nc.vector.tensor_scalar(varf[:, t.slot, :], sumsq[:, t.slot, :], 1.0 / FFN, EPS,
                                            ALU.mult, ALU.add).then_inc(varf_done, 1)
                if t := tile_at(3):
                    wait(dve, y2_turned, t.n + 1)
                    ln2.statistics(nc, dve, t, [ps_t[:, j * D:(j + 1) * D] for j in range(J)], z_done)
                    for j in range(J):
                        last = nc.vector.scalar_tensor_tensor(u[:, t.slot, j, :], ps_t[:, j * D:(j + 1) * D],
                                                              ln2.mv[:, t.slot, j, 0:1], g2[:, :],
                                                              ALU.subtract, ALU.mult)
                    last.then_inc(u_done, 1)
            over_tiles(dve, NT, 5, step)

        @block.scalar
        def _(act):
            act.wait_ge(w_loaded, 16 * (loads - 1))

            def step(tile_at):
                if t := tile_at(2):
                    wait(act, xh_turned, t.n + 1)
                    wait(act, y2t_done, t.n - 1)
                    nc.scalar.activation(x1t[:, t.slot, :], ps_t[:, :], ACT.Identity, bias=b1[:, :],
                                         scale=g1[:, :]).then_inc(x1t_done, 1)
                if t := tile_at(3):
                    for c in range(C):
                        wait(act, g_turned, 4 * t.n + c + 1)
                        wait(act, f2_made, t.n)
                        nc.scalar.activation(hg[:, c, :], ps_g[c % 2][:, :], ACT.Gelu, bias=bf[:, c:c + 1],
                                             scale=gf[:, c:c + 1]).then_inc(gelu_done, 1)
                if t := tile_at(2):
                    wait(act, varf_done, t.n - 1)
                    for j in range(J):
                        wait(act, h_made, 4 * t.n + j + 1)
                        last = nc.scalar.activation(squares[:, j, :], ps_h[j][:, :], ACT.Square,
                                                    accum_out=sumsq[:, t.slot, j:j + 1])
                    last.then_inc(sumsq_done, 1)
                if t := tile_at(5):
                    wait(act, stored[t.slot], 16 * t.u)
                    ln3.apply(nc, act, t, [z[:, t.slot, j, :] for j in range(J)],
                              [y[:, t.slot, j, :] for j in range(J)], y_done)
                if t := tile_at(6):
                    wait(act, y_done, t.n + 1)
                    act.dma_start(nm_tile(g["x_a"], t), flat(y[:, t.slot, :, :])).then_inc(stored[t.slot], 16)
            over_tiles(act, NT, 6, step)
            for b in range(2):
                act.wait_ge(stored[b], 16 * (NT // 2))


class Chain:

    def __init__(self, f, eng, name):
        self.eng, self.sem, self.count = eng, f.sem(name), 0

    def __call__(self, instruction):
        self.count += 1
        instruction.then_inc(self.sem, 1)
        self.eng.wait_ge(self.sem, self.count)


def segment_starts(nc, name, pairs, keep_out, cut_out):
    rows, width = ECOLS // 2, 2 * P
    with ExitStack() as ctx:
        f = Phase(nc, ctx, name)
        now, before = f.sb("now", [rows, width, 2], I32), f.sb("before", [rows, width, 2], I32)
        keep, cut = f.sb("keep", [rows, width], BF16), f.sb("cut", [rows, width], BF16)
        loaded, made, stored = f.sem("loaded"), f.sem("made"), f.sem("stored")
        block = ctx.enter_context(nc.Block())

        @block.sync
        def _(sp):
            for buf, lead in ((now, 1), (before, 0)):
                sp.dma_start(buf[:, :, :], pairs[lead:lead + EP, :].rearrange("(r w) two -> r w two", w=width)
                             ).then_inc(loaded, 16)
            sp.wait_ge(made, 1)
            sp.dma_start(keep_out.rearrange("(r w) -> r w", w=width), keep[:, :]).then_inc(stored, 16)
            if cut_out is not None:
                sp.wait_ge(made, 2)
                sp.dma_start(cut_out.rearrange("(r w) -> r w", w=width), cut[:, :]).then_inc(stored, 16)
            sp.wait_ge(stored, 16 if cut_out is None else 32)

        @block.vector
        def _(dve):
            dve.wait_ge(loaded, 32)
            nc.vector.tensor_tensor(keep[:, :], now[:, :, 0], before[:, :, 0], ALU.is_equal).then_inc(made, 1)
            if cut_out is not None:
                dve.wait_ge(made, 1)
                nc.vector.tensor_scalar(cut[:, :], keep[:, :], BIG, -BIG, ALU.mult, ALU.add).then_inc(made, 1)


def node_lists(nc, name, g, side, ptr_out, inv_out):
    ROWS = NP // SUPER
    with ExitStack() as ctx:
        f = Phase(nc, ctx, name)
        pairs = f.sb("pairs", [P, ECOLS, 2], I32)
        low_i, high_i = f.sb("low_i", [P, ECOLS], I32), f.sb("high_i", [P, ECOLS], I32)
        low, high = f.sb("low", [P, ECOLS]), f.sb("high", [P, ECOLS])
        digits_f, digits = f.sb("digits_f", [P, DIGIT]), f.sb("digits", [P, DIGIT], BF16)
        before = f.sb("before", [P, P])
        hot_high, hot_low = f.sb("hot_high", [P, 2, HI_DIGITS], BF16), f.sb("hot_low", [P, 2, DIGIT], BF16)
        (ones, count, cum, last_e, has, clipped, inverse, spare, moved, picked) = (
            f.sb(s, [ROWS, SUPER]) for s in ("ones", "count", "cum", "last_e", "has", "clipped", "inverse", "spare",
                                             "moved", "picked"))
        ptr_i = f.sb("ptr_i", [ROWS, SUPER], I32)
        offset = f.sb("offset", [ROWS, 1])
        ps_hist = [f.ps(f"ps_hist{b}") for b in range(2)]
        ps_off = f.ps("ps_off")
        loaded, hot_done, counted, cum_done, off_made, lists_made, stored = (
            f.sem(s) for s in ("loaded", "hot_done", "counted", "cum_done", "off_made", "lists_made", "stored"))
        block = ctx.enter_context(nc.Block())

        @block.sync
        def _(sp):
            for dst_, src_ in ((pairs[:, :, :], g["edges"][1:EP + 1, :].rearrange("(p c) two -> p c two", p=P)),
                               (digits_f[:, :], g["digits_c"]), (before[:, :], g["before_c"]), (spare[:, :], g["spare_c"])):
                sp.dma_start(dst_, src_).then_inc(loaded, 16)
            sp.wait_ge(lists_made, 2)
            sp.dma_start(ptr_out.rearrange("(r w) -> r w", w=SUPER), ptr_i[:, :]).then_inc(stored, 16)
            sp.dma_start(inv_out.rearrange("(r w) -> r w", w=SUPER), inverse[:, :]).then_inc(stored, 16)
            sp.wait_ge(stored, 32)

        @block.tensor
        def _(pe):
            def count_column(c, b, first):
                wait(pe, hot_done, 2 * (c + 1))
                for half in range(2):
                    last = nc.tensor.matmul(
                        ps_hist[half][0:ROWS, 0:DIGIT],
                        hot_high[:, b, :].rearrange("p (a h) -> p h a", h=2)[:, half, :],
                        hot_low[:, b, :], start=first, stop=True, skip_group_check=True)
                last.then_inc(counted, 1)
            for c in range(2):
                count_column(c, c, c == 0)
            with pe.Fori(1, ECOLS // 2) as k:
                for b in range(2):
                    count_column(2 * k + b, b, False)
            pe.wait_ge(cum_done, 1)
            nc.tensor.matmul(ps_off[0:ROWS, 0:1], before[0:ROWS, 0:ROWS], cum[:, SUPER - 1:SUPER],
                             start=True, stop=True).then_inc(off_made, 1)

        @block.vector
        def _(dve):
            link = Chain(f, dve, "link")
            dve.wait_ge(loaded, 16 * 4)
            link(nc.vector.memset(ones[:, :], 1.0))
            link(nc.vector.tensor_copy(digits[:, :], digits_f[:, :]))
            link(nc.vector.tensor_scalar(low_i[:, :], pairs[:, :, side], DIGIT - 1, None, ALU.bitwise_and))
            link(nc.vector.tensor_scalar(high_i[:, :], pairs[:, :, side], 8, None, ALU.logical_shift_right))
            link(nc.vector.tensor_copy(low[:, :], low_i[:, :]))
            link(nc.vector.tensor_copy(high[:, :], high_i[:, :]))

            def one_hot(c, b):
                wait(dve, counted, c - 1)
                nc.vector.tensor_scalar(hot_high[:, b, :], digits[:, 0:HI_DIGITS], high[:, bass.ds(c, 1)], None,
                                        ALU.is_equal).then_inc(hot_done, 1)
                nc.vector.tensor_scalar(hot_low[:, b, :], digits[:, :], low[:, bass.ds(c, 1)], None,
                                        ALU.is_equal).then_inc(hot_done, 1)
            for c in range(2):
                one_hot(c, c)
            with dve.Fori(1, ECOLS // 2) as k:
                for b in range(2):
                    one_hot(2 * k + b, b)
            dve.wait_ge(counted, ECOLS)
            for half in range(2):
                link(nc.vector.tensor_copy(count[:, half * DIGIT:(half + 1) * DIGIT], ps_hist[half][0:ROWS, 0:DIGIT]))
            nc.vector.tensor_tensor_scan(cum[:, :], ones[:, :], count[:, :], 0.0, ALU.mult,
                                         ALU.add).then_inc(cum_done, 1)
            link(nc.vector.tensor_scalar(has[:, :], count[:, :], 1.0, None, ALU.min))
            link(nc.vector.tensor_scalar(clipped[:, :], count[:, :], 1.0, None, ALU.max))
            nc.vector.reciprocal(inverse[:, :], clipped[:, :]).then_inc(lists_made, 1)
            dve.wait_ge(off_made, 1)
            link(nc.vector.tensor_copy(offset[:, :], ps_off[0:ROWS, 0:1]))
            link(nc.vector.tensor_scalar(last_e[:, :], cum[:, :], offset[:, :], -1.0, ALU.add, ALU.add))
            link(nc.vector.tensor_tensor(moved[:, :], last_e[:, :], spare[:, :], ALU.subtract))
            link(nc.vector.tensor_tensor(picked[:, :], moved[:, :], has[:, :], ALU.mult))
            nc.vector.tensor_tensor(ptr_i[:, :], picked[:, :], spare[:, :], ALU.add).then_inc(lists_made, 1)


def sort_digit(nc, name, g, pairs_in, swap, high_digit, pairs_out):
    GROUP = ECOLS // 2
    with ExitStack() as ctx:
        f = Phase(nc, ctx, name)
        raw, pairs = f.sb("raw", [P, ECOLS, 2], I32), f.sb("pairs", [P, ECOLS, 2], I32)
        digit_i, digit = f.sb("digit_i", [P, ECOLS], I32), f.sb("digit", [P, ECOLS])
        digits_f, digits = f.sb("digits_f", [P, DIGIT]), f.sb("digits", [P, DIGIT], BF16)
        before_f, before = f.sb("before_f", [P, P]), f.sb("before", [P, P], BF16)
        hot = f.sb("hot", [P, ECOLS, DIGIT], BF16)
        window = f.sb("window", [P, 2 * P], BF16)
        pick = f.sb("pick", [GROUP, GROUP, P], BF16)
        ones = f.sb("ones", [P, DIGIT], BF16)
        counts = f.sb("counts", [GROUP, 2, DIGIT], BF16)
        upto, smaller = f.sb("upto", [P, DIGIT]), f.sb("smaller", [P, DIGIT])
        start, start_i, start_lo_i = (f.sb("start", [GROUP, 2, DIGIT]), f.sb("start_i", [GROUP, 2, DIGIT], I32),
                                      f.sb("start_lo_i", [GROUP, 2, DIGIT], I32))
        start_hi, start_lo = f.sb("start_hi", [GROUP, 2, DIGIT], BF16), f.sb("start_lo", [GROUP, 2, DIGIT], BF16)
        own = f.sb("own", [P, 2, DIGIT])
        rank = f.sb("rank", [P, ECOLS])
        rank_i, rank_p, rank_c, dest = (f.sb(s, [P, ECOLS], I32) for s in ("rank_i", "rank_p", "rank_c", "dest"))
        dest_slot, pair_slot = f.sb("dest_slot", [P, 2, J], I32), f.sb("pair_slot", [P, 2, J, 2], I32)
        lead = f.sb("lead", [1, 2], I32)
        ps_count = [f.ps(f"ps_count{b}") for b in range(2)]
        ps_total, ps_start = f.ps("ps_total"), [f.ps(f"ps_start{b}") for b in range(2)]
        ps_rank = [f.ps(f"ps_rank{b}") for b in range(2)]
        (loaded, tables_set, pick_set, hot_done, counted, counts_done, total_made, starts_made, start_done, rank_made,
         rank_done, dest_done, slots_filled, lead_set, lead_stored) = (
            f.sem(s) for s in ("loaded", "tables_set", "pick_set", "hot_done", "counted", "counts_done", "total_made",
                               "starts_made", "start_done", "rank_made", "rank_done", "dest_done", "slots_filled",
                               "lead_set", "lead_stored"))
        scattered = f.sems("scattered")
        block = ctx.enter_context(nc.Block())

        @block.sync
        def _(sp):
            for dst_, src_ in ((raw[:, :, :], pairs_in), (digits_f[:, :], g["digits_c"]), (before_f[:, :], g["before_c"])):
                sp.dma_start(dst_, src_).then_inc(loaded, 16)
            if high_digit:
                sp.wait_ge(lead_set, 1)
                sp.dma_start(pairs_out[0:1, :], lead[:, :]).then_inc(lead_stored, 16)
                sp.wait_ge(lead_stored, 16)

        @block.gpsimd
        def _(pool):
            nc.gpsimd.tensor_copy(pick[:, :, :], g["ident"][0:GROUP, 0:GROUP].unsqueeze(2).broadcast_to(
                [GROUP, GROUP, P])).then_inc(pick_set, 1)
            pool.wait_ge(dest_done, 1)

            def scatter(c4, u, b):
                wait(pool, scattered[b], 64 * u)
                pool.nop(nofuse=True)
                nc.gpsimd.tensor_copy(dest_slot[:, b, :], dest[:, bass.ds(J * c4, J)]).then_inc(slots_filled, 1)
                nc.gpsimd.tensor_copy(pair_slot[:, b, :, :], pairs[:, bass.ds(J * c4, J), :]).then_inc(slots_filled, 1)
                wait(pool, slots_filled, 2 * (c4 + 1))
                pool.nop(nofuse=True)
                for j in range(J):
                    nc.gpsimd.indirect_dma_start(
                        out=pairs_out[:, :], out_offset=bass.IndirectOffsetOnAxis(ap=dest_slot[:, b, j:j + 1], axis=0),
                        in_=pair_slot[:, b, j, :], in_offset=None).then_inc(scattered[b], 16)
            for b in range(2):
                scatter(b, 0, b)
            with pool.Fori(1, ECOLS // (2 * J)) as k:
                for b in range(2):
                    scatter(2 * k + b, k, b)
            for b in range(2):
                pool.wait_ge(scattered[b], 64 * (ECOLS // (2 * J)))

        @block.tensor
        def _(pe):
            pe.wait_ge(tables_set, 3)

            def count_column(c, m, h, first):
                wait(pe, hot_done, c + 1)
                nc.tensor.matmul(ps_count[h][:, 0:DIGIT], window[:, bass.ds(P - 1 - m, P)],
                                 hot[:, bass.ds(c, 1), :].rearrange("p a d -> p (a d)"), start=first, stop=True,
                                 skip_group_check=True).then_inc(counted, 1)
            for h in range(2):
                count_column(h * GROUP, 0, h, True)
                with pe.Fori(1, GROUP) as m:
                    count_column(h * GROUP + m, m, h, False)
            pe.wait_ge(counts_done, 2)
            for h in range(2):
                last = nc.tensor.matmul(ps_total[:, 0:DIGIT], ones[0:GROUP, 0:P], counts[:, h, :],
                                        start=h == 0, stop=h == 1)
            last.then_inc(total_made, 1)
            nc.tensor.matmul(ps_start[0][0:GROUP, 0:DIGIT], before[0:GROUP, 0:GROUP], counts[:, 0, :],
                             start=True, stop=True).then_inc(starts_made, 1)
            nc.tensor.matmul(ps_start[1][0:GROUP, 0:DIGIT], ones[0:GROUP, 0:GROUP], counts[:, 0, :],
                             start=True, stop=False)
            nc.tensor.matmul(ps_start[1][0:GROUP, 0:DIGIT], before[0:GROUP, 0:GROUP], counts[:, 1, :],
                             start=False, stop=True).then_inc(starts_made, 1)
            pe.wait_ge(start_done, 1)
            pe.wait_ge(pick_set, 1)

            def rank_column(c, m, h, b):
                wait(pe, rank_done, c - 1)
                out = ps_rank[b][:, 0:DIGIT]
                nc.tensor.matmul(out, before[:, :], hot[:, bass.ds(c, 1), :].rearrange("p a d -> p (a d)"),
                                 start=True, stop=False)
                row = pick[:, bass.ds(m, 1), :].rearrange("k a p -> k (a p)")
                nc.tensor.matmul(out, row, start_hi[:, h, :], start=False, stop=False)
                nc.tensor.matmul(out, row, start_lo[:, h, :], start=False, stop=True).then_inc(rank_made, 1)
            for h in range(2):
                for b in range(2):
                    rank_column(h * GROUP + b, b, h, b)
                with pe.Fori(1, GROUP // 2) as k:
                    for b in range(2):
                        rank_column(h * GROUP + 2 * k + b, 2 * k + b, h, b)

        @block.vector
        def _(dve):
            link = Chain(f, dve, "link")
            nc.vector.memset(lead[:, :], -1).then_inc(lead_set, 1)
            link(nc.vector.memset(window[:, :], 0.0))
            nc.vector.memset(window[:, P - 1:P], 1.0).then_inc(tables_set, 1)
            nc.vector.memset(ones[:, :], 1.0).then_inc(tables_set, 1)
            dve.wait_ge(loaded, 16 * 3)
            nc.vector.tensor_copy(before[:, :], before_f[:, :]).then_inc(tables_set, 1)
            link(nc.vector.tensor_copy(digits[:, :], digits_f[:, :]))
            for col in range(2):
                link(nc.vector.tensor_copy(pairs[:, :, col], raw[:, :, 1 - col if swap else col]))
            if high_digit:
                link(nc.vector.tensor_scalar(digit_i[:, :], pairs[:, :, 0], 8, None, ALU.logical_shift_right))
            else:
                link(nc.vector.tensor_scalar(digit_i[:, :], pairs[:, :, 0], DIGIT - 1, None, ALU.bitwise_and))
            link(nc.vector.tensor_copy(digit[:, :], digit_i[:, :]))
            with dve.Fori(0, ECOLS) as c:
                nc.vector.tensor_scalar(hot[:, bass.ds(c, 1), :].rearrange("p a d -> p (a d)"), digits[:, :],
                                        digit[:, bass.ds(c, 1)], None, ALU.is_equal).then_inc(hot_done, 1)
            dve.wait_ge(counted, ECOLS)
            for h in range(2):
                nc.vector.tensor_copy(counts[:, h, :], ps_count[h][0:GROUP, 0:DIGIT]).then_inc(counts_done, 1)
            dve.wait_ge(total_made, 1)
            dve.wait_ge(tables_set, 2)
            link(nc.vector.tensor_tensor_scan(upto[:, :], ones[:, :], ps_total[:, 0:DIGIT], 0.0, ALU.mult, ALU.add))
            link(nc.vector.tensor_tensor(smaller[:, :], upto[:, :], ps_total[:, 0:DIGIT], ALU.subtract))
            dve.wait_ge(starts_made, 2)
            for h in range(2):
                link(nc.vector.tensor_tensor(start[:, h, :], smaller[0:GROUP, :], ps_start[h][0:GROUP, 0:DIGIT],
                                             ALU.add))
            link(nc.vector.tensor_copy(start_i[:, :, :], start[:, :, :]))
            link(nc.vector.tensor_scalar(start_lo_i[:, :, :], start_i[:, :, :], DIGIT - 1, None, ALU.bitwise_and))
            link(nc.vector.tensor_copy(start_lo[:, :, :], start_lo_i[:, :, :]))
            nc.vector.tensor_tensor(start_hi[:, :, :], start[:, :, :], start_lo[:, :, :],
                                    ALU.subtract).then_inc(start_done, 1)

            def rank_column(c, b):
                wait(dve, rank_made, c + 1)
                wait(dve, rank_done, c - 1)
                nc.vector.scalar_tensor_tensor(own[:, b, :], ps_rank[b][:, 0:DIGIT], 1.0,
                                               hot[:, bass.ds(c, 1), :].rearrange("p a d -> p (a d)"),
                                               ALU.mult, ALU.mult, accum_out=rank[:, bass.ds(c, 1)]
                                               ).then_inc(rank_done, 1)
            for b in range(2):
                rank_column(b, b)
            with dve.Fori(1, ECOLS // 2) as k:
                for b in range(2):
                    rank_column(2 * k + b, b)
            dve.wait_ge(rank_done, ECOLS)
            link(nc.vector.tensor_copy(rank_i[:, :], rank[:, :]))
            if high_digit:
                nc.vector.tensor_scalar(dest[:, :], rank_i[:, :], 1, None, ALU.add).then_inc(dest_done, 1)
            else:
                link(nc.vector.tensor_scalar(rank_p[:, :], rank_i[:, :], P - 1, None, ALU.bitwise_and))
                link(nc.vector.tensor_scalar(rank_c[:, :], rank_i[:, :], 7, None, ALU.logical_shift_right))
                nc.vector.scalar_tensor_tensor(dest[:, :], rank_p[:, :], float(ECOLS), rank_c[:, :], ALU.mult,
                                               ALU.add).then_inc(dest_done, 1)


def set_up(nc, name, g):
    with ExitStack() as ctx:
        f = Phase(nc, ctx, name)
        zeros, ob = f.sb("zeros", [P, J, D]), f.sb("ob", [P, D])
        loaded, zeros_set, stored = f.sem("loaded"), f.sem("zeros_set"), f.sem("stored")
        block = ctx.enter_context(nc.Block())

        @block.sync
        def _(sp):
            sp.dma_start(g["ident"][:, :], g["ident_c"]).then_inc(loaded, 16)
            sp.dma_start(ob[:, :], on_all(g["ob"])).then_inc(loaded, 16)
            sp.wait_ge(loaded, 32)
            for j in range(J):
                sp.dma_start(g["att_sums"][EP + j * P:EP + (j + 1) * P, :], ob[:, :]).then_inc(stored, 16)
            sp.wait_ge(zeros_set, 1)
            sp.dma_start(g["sums"][EP:EP + SUPER, :].rearrange("(p j) d -> p j d", j=J), zeros[:, :, :]
                         ).then_inc(stored, 16)
            sp.wait_ge(stored, 16 * (J + 1))

        @block.vector
        def _(dve):
            nc.vector.memset(zeros[:, :, :], 0.0).then_inc(zeros_set, 1)


FLOAT_INPUTS = {
    "L0_gnn_qW": "qW", "L0_gnn_qb": "qb", "L0_gnn_kW": "kW", "L0_gnn_kb": "kb", "L0_gnn_vW": "vW", "L0_gnn_vb": "vb",
    "L0_gnn_eW": "eW", "L0_gnn_eb": "eb", "L0_gnn_oW": "oW", "L0_gnn_ob": "ob", "L0_gnn_ln1_g": "ln1_g",
    "L0_gnn_ln1_b": "ln1_b", "L0_gnn_f1W": "f1W", "L0_gnn_f1b": "f1b", "L0_gnn_lnf_g": "lnf_g",
    "L0_gnn_lnf_b": "lnf_b", "L0_gnn_f2W": "f2W", "L0_gnn_f2b": "f2b", "L0_gnn_ln2_g": "ln2_g",
    "L0_gnn_ln2_b": "ln2_b", "L2_gnn_lin_b": "lin_b", "L2_gnn_b_ih": "b_ih", "L2_gnn_b_hh": "b_hh",
    "L3_gnn_weight": "w_cat",
}
TRANSPOSED_INPUTS = {
    "L1_gnn_W_l": "wl_t", "L1_gnn_W_r": "wr_t", "L2_gnn_lin_w": "lin_wt", "L2_gnn_w_ih": "wih_t",
    "L2_gnn_w_hh": "whh_t",
}


def build(nc, ins, out):
    g = dict(ins)

    def dram(name, shape, dt=F32):
        return nc.dram_tensor(name, shape, dt, kind="Internal").ap()

    g["att_sums"], g["sums"] = dram("att_sums", [EP + SUPER, D]), dram("sums", [EP + SUPER, D])
    g["x_a"], g["x_b"], g["x_c"] = (dram(n, [NP, D]) for n in ("x_a", "x_b", "x_c"))
    g["h_a"], g["h_b"] = (dram(n, [NP, D]) for n in ("h_a", "h_b"))
    g["ht_a"], g["ht_b"] = (dram(n, [NT, P, SUPER]) for n in ("ht_a", "ht_b"))
    g["ptr_dst"], g["ptr_src"] = dram("ptr_dst", [NP], I32), dram("ptr_src", [NP], I32)
    g["inv_dst"], g["inv_src"] = dram("inv_dst", [NP]), dram("inv_src", [NP])
    g["keep_dst"], g["cut_dst"], g["keep_src"] = (dram(n, [EP], BF16) for n in ("keep_dst", "cut_dst", "keep_src"))
    g["half_sorted"] = dram("half_sorted", [EP, 2], I32)
    g["by_src"] = dram("by_src", [EP + 1, 2], I32)
    g["by_dst"] = by_dst = g["edges"][1:EP + 1, :]
    by_src = g["by_src"][1:EP + 1, :]

    with ExitStack() as ctx:
        g["ident"] = ctx.enter_context(nc.sbuf_tensor("ident", [P, P], F32))
        set_up(nc, "setup", g)
        segment_starts(nc, "starts_dst", g["edges"], g["keep_dst"], g["cut_dst"])
        node_lists(nc, "lists_dst", g, 0, g["ptr_dst"], g["inv_dst"])
        node_lists(nc, "lists_src", g, 1, g["ptr_src"], g["inv_src"])
        sort_digit(nc, "sort_low", g, by_dst.rearrange("(p c) two -> p c two", p=P), True, False, g["half_sorted"])
        sort_digit(nc, "sort_high", g, g["half_sorted"].rearrange("(p c) two -> p c two", p=P), False, True, g["by_src"])
        segment_starts(nc, "starts_src", g["by_src"], g["keep_src"], None)
        attention_pass(nc, "attend", g)
        ffn_pass(nc, "ffn", g)
        sum_pass(nc, "sum1", g, g["x_a"], by_src, g["keep_src"], g["wr_t"])
        mean_pass(nc, "mean1", g, g["x_a"], g["ptr_src"], g["inv_src"], g["wl_t"], g["x_b"], True, g["h_a"], g["ht_a"])
        h = [(g["h_a"], g["ht_a"]), (g["h_b"], g["ht_b"]), (g["h_a"], g["ht_a"]), (None, None)]
        for i in range(3):
            sum_pass(nc, f"sum2{i}", g, h[i][0], by_dst, g["keep_dst"], None)
            gated_pass(nc, f"gate{i}", g, i, *h[i], *h[i + 1], g["x_b"], g["x_c"] if i == 2 else None)
        sum_pass(nc, "sum3", g, g["x_c"], by_dst, g["keep_dst"], g["w_cat"][D:2 * D, :])
        mean_pass(nc, "mean3", g, g["x_c"], g["ptr_dst"], g["inv_dst"], g["w_cat"][0:D, :], out, False)


def kernel(**inputs):
    import numpy as np
    import concourse.bacc as bacc
    from concourse import mybir as my
    from concourse.bass_utils import run_bass_kernel_spmd as run

    nc = bacc.Bacc("TRN2", target_bir_lowering=False, num_devices=1)
    arrays = {short: np.ascontiguousarray(inputs[key]) for key, short in FLOAT_INPUTS.items()}
    arrays.update({short: np.ascontiguousarray(np.asarray(inputs[key]).T) for key, short in TRANSPOSED_INPUTS.items()})
    arrays["msg_wt"] = np.ascontiguousarray(np.asarray(inputs["L2_gnn_weight"]).transpose(0, 2, 1))
    x = np.zeros((NP, D), np.float32)
    x[:N] = inputs["x"]
    edges = np.full((EP + 1, 2), PAD_NODE, np.int32)
    edges[0] = -1
    edges[1:E + 1, 0] = inputs["dst"]
    edges[1:E + 1, 1] = inputs["src"]
    edge_t = np.zeros((EDIM, EP), np.float32)
    edge_t[:, :E] = np.asarray(inputs["edge_attr_32"]).T
    arrays.update(x_in=x, edges=edges, edge_attr_t=edge_t)
    head = np.arange(D) // HEAD_DIM
    arrays["ident_c"] = np.eye(P, dtype=np.float32)
    arrays["before_c"] = np.triu(np.ones((P, P), np.float32), 1)
    arrays["digits_c"] = np.tile(np.arange(DIGIT, dtype=np.float32), (P, 1))
    arrays["spare_c"] = np.tile(np.arange(EP, EP + SUPER, dtype=np.float32), (NP // SUPER, 1))
    arrays["blocks_c"] = ((head[:, None] == head[None, :]) * HEAD_DIM ** -0.5).astype(np.float32).reshape(
        P, HEADS, HEAD_DIM)
    arrays["heads_c"] = (np.arange(D)[:, None] == HEAD_DIM * np.arange(HEADS)[None, :]).astype(np.float32)
    ins = {key: nc.dram_tensor(f"in_{key}", a.shape, my.dt.from_np(a.dtype), kind="ExternalInput").ap()
           for key, a in arrays.items()}
    out = nc.dram_tensor("out", (NP, D), F32, kind="ExternalOutput").ap()
    build(nc, ins, out)
    r = run(nc, [{f"in_{key}": a for key, a in arrays.items()}], core_ids=[0])
    return r.results[0]["out"][:N]
```

```python
import concourse.bass as bass
from concourse import mybir
from contextlib import ExitStack

F32 = mybir.dt.float32
BF16 = mybir.dt.bfloat16
I32 = mybir.dt.int32
ALU = mybir.AluOpType
ACT = mybir.ActivationFunctionType
AX = mybir.AxisListType

N, E, D, HEADS, EDIM, FFN = 50000, 25000, 128, 8, 32, 512
P, J = 128, 4
SUPER = P * J
NT = -(-N // (2 * SUPER)) * 2
ET = -(-E // (2 * SUPER)) * 2
NP, EP = NT * SUPER, ET * SUPER
ECOLS = EP // P
PAD_NODE = NP - 1
DIGIT = 256
HI_DIGITS = NP // DIGIT
EPS = 1e-5
BIG = 1e30
HEAD_DIM = D // HEADS


UNROLL = 4


class Tile:

    def __init__(self, u4, slot4):
        self.u4, self.slot4, self.n = u4, slot4, UNROLL * u4 + slot4
        self.slot, self.u = slot4 % 2, 2 * u4 + slot4 // 2


def over_tiles(eng, tiles, lag, step):
    def group(k):
        for b in range(UNROLL):
            def tile_at(behind):
                u4, slot4 = k + (b - behind) // UNROLL, (b - behind) % UNROLL
                if isinstance(k, int) and not 0 <= UNROLL * u4 + slot4 < tiles:
                    return None
                return Tile(u4, slot4)
            step(tile_at)
    first = (lag + 2 * UNROLL - 1) // UNROLL
    for k in range(first):
        group(k)
    with eng.Fori(first, tiles // UNROLL) as k:
        group(k)
    for k in range(tiles // UNROLL, -(-(tiles + lag) // UNROLL)):
        group(k)


def wait(eng, sem, count):
    if not isinstance(count, int) or count > 0:
        eng.wait_ge(sem, count)


def wait_alone(eng, sem, count):
    if not isinstance(count, int) or count > 0:
        eng.wait_ge(sem, count)
        eng.nop(nofuse=True)


def nm_tile(table, t):
    view = table.rearrange("(s p j) d -> s p (j d)", p=P, j=J)
    return view[bass.ds(t.n, 1), :, :].rearrange("s p n -> (s p) n")


def list_tile(values, t):
    view = values.rearrange("(s p j) -> s p j", p=P, j=J)
    return view[bass.ds(t.n, 1), :, :].rearrange("s p j -> (s p) j")


def row_tile(values, t, parts=P):
    view = values.rearrange("(s n) -> s n", n=SUPER)
    return view[bass.ds(t.n, 1), :].broadcast_to([parts, SUPER])


def fm_tile(table, t):
    return table[bass.ds(t.n, 1), :, :].rearrange("s p n -> (s p) n")


def on_all(row):
    n = row.shape[0]
    return row.rearrange("(a n) -> a n", a=1).broadcast_to([P, n])


def column(row):
    return row.rearrange("(n a) -> n a", a=1)


class Phase:

    def __init__(self, nc, ctx, name):
        self.nc, self.ctx, self.name = nc, ctx, name
        self.semaphores = []
        ctx.callback(self.clear)

    def clear(self):
        self.nc.clear_and_free_semaphores(self.semaphores)
        self.nc.all_engine_barrier()

    def sb(self, name, shape, dt=F32):
        return self.ctx.enter_context(self.nc.sbuf_tensor(f"{self.name}_{name}", shape, dt))

    def ps(self, name, shape=(P, SUPER), dt=F32):
        return self.ctx.enter_context(self.nc.psum_tensor(f"{self.name}_{name}", list(shape), dt))

    def sem(self, name):
        self.semaphores.append(self.nc.alloc_semaphore(f"{self.name}_{name}"))
        return self.semaphores[-1]

    def sems(self, name, buffers=2):
        return [self.sem(f"{name}{b}") for b in range(buffers)]


def flat(buf):
    return buf.rearrange("p j d -> p (j d)")


def edge_columns(buf):
    return buf.rearrange("f (p j) -> f j p", j=J)


def sum_pass(nc, name, g, gather_from, pairs, mask, weight):
    with ExitStack() as ctx:
        f = Phase(nc, ctx, name)
        idx = f.sb("idx", [P, 4, J, 2], I32)
        rows = f.sb("rows", [P, 4, J, D])
        keep = f.sb("keep", [P, 4, SUPER], BF16)
        run = f.sb("run", [P, 2, SUPER])
        sums = f.sb("sums", [P, 2, SUPER])
        w = f.sb("w", [P, D])
        ps_rows = [f.ps(f"ps_rows{b}") for b in range(2)]
        ps_sums = [f.ps(f"ps_sums{b}") for b in range(2)]
        w_loaded, idx_loaded, keep_loaded = f.sem("w_loaded"), f.sems("idx_loaded", 4), f.sems("keep_loaded", 4)
        gathered, stored = f.sems("gathered", 4), f.sems("stored")
        rows_turned, scanned, sums_made, sums_copied = (
            f.sem("rows_turned"), f.sem("scanned"), f.sem("sums_made"), f.sem("sums_copied"))
        block = ctx.enter_context(nc.Block())

        @block.sync
        def _(sp):
            if weight is not None:
                sp.dma_start(w[:, :], weight).then_inc(w_loaded, 16)

            def step(tile_at):
                if t := tile_at(0):
                    wait_alone(sp, gathered[t.slot4], 64 * t.u4)
                    sp.dma_start(idx[:, t.slot4, :, :].rearrange("p j c -> p (j c)"),
                                 nm_tile(pairs, t)).then_inc(idx_loaded[t.slot4], 16)
                    wait_alone(sp, scanned, t.n - 3)
                    sp.dma_start(keep[:, t.slot4, :], row_tile(mask, t)).then_inc(keep_loaded[t.slot4], 16)
            over_tiles(sp, ET, 0, step)

        @block.gpsimd
        def _(pool):
            def step(tile_at):
                if t := tile_at(0):
                    wait(pool, idx_loaded[t.slot4], 16 * (t.u4 + 1))
                    wait(pool, rows_turned, t.n - 3)
                    pool.nop(nofuse=True)
                    for j in range(J):
                        nc.gpsimd.indirect_dma_start(
                            out=rows[:, t.slot4, j, :], out_offset=None, in_=gather_from[:, :],
                            in_offset=bass.IndirectOffsetOnAxis(ap=idx[:, t.slot4, j, 1:2], axis=0)).then_inc(gathered[t.slot4], 16)
            over_tiles(pool, ET, 0, step)

        @block.tensor
        def _(pe):
            if weight is not None:
                pe.wait_ge(w_loaded, 16)

            def step(tile_at):
                if t := tile_at(0):
                    wait(pe, gathered[t.slot4], 64 * (t.u4 + 1))
                    wait(pe, scanned, t.n - 1)
                    for j in range(J):
                        last = nc.tensor.transpose(edge_columns(ps_rows[t.slot][:, :])[:, j, :],
                                                   rows[:, t.slot4, j, :], g["ident"][:, :])
                    last.then_inc(rows_turned, 1)
                if t := tile_at(1):
                    wait(pe, scanned, t.n + 1)
                    wait(pe, sums_copied, t.n - 1)
                    for j in range(J):
                        out = ps_sums[t.slot][:, j * D:(j + 1) * D]
                        part = edge_columns(run[:, t.slot, :])[:, j, :]
                        if weight is None:
                            last = nc.tensor.transpose(out, part, g["ident"][:, :])
                        else:
                            last = nc.tensor.matmul(out, part, w[:, :], start=True, stop=True)
                    last.then_inc(sums_made, 1)
            over_tiles(pe, ET, 1, step)

        @block.vector
        def _(dve):
            def step(tile_at):
                if t := tile_at(0):
                    wait(dve, keep_loaded[t.slot4], 16 * (t.u4 + 1))
                    wait(dve, rows_turned, t.n + 1)
                    wait(dve, sums_made, t.n - 1)
                    wait(dve, scanned, t.n)
                    first = isinstance(t.n, int) and t.n == 0
                    nc.vector.tensor_tensor_scan(
                        run[:, t.slot, :], keep[:, t.slot4, :], ps_rows[t.slot][:, :],
                        0.0 if first else run[:, 1 - t.slot, SUPER - 1:SUPER],
                        ALU.mult, ALU.add).then_inc(scanned, 1)
            over_tiles(dve, ET, 0, step)

        @block.scalar
        def _(act):
            def step(tile_at):
                if t := tile_at(1):
                    wait(act, sums_made, t.n + 1)
                    wait(act, stored[t.slot], 16 * t.u)
                    nc.scalar.activation(sums[:, t.slot, :], ps_sums[t.slot][:, :],
                                         ACT.Copy).then_inc(sums_copied, 1)
                if t := tile_at(2):
                    wait(act, sums_copied, t.n + 1)
                    act.dma_start(nm_tile(g["sums"], t), sums[:, t.slot, :]).then_inc(stored[t.slot], 16)
            over_tiles(act, ET, 2, step)
            for b in range(2):
                act.wait_ge(stored[b], 16 * (ET // 2))


def gather_step(nc, pool, t, idx, rows, table, idx_loaded, rows_free, gathered):
    wait(pool, idx_loaded[t.slot4], 16 * (t.u4 + 1))
    wait(pool, rows_free, t.n - 3)
    pool.nop(nofuse=True)
    for j in range(J):
        nc.gpsimd.indirect_dma_start(
            out=rows[:, t.slot4, j, :], out_offset=None, in_=table[:, :],
            in_offset=bass.IndirectOffsetOnAxis(ap=idx[:, t.slot4, j:j + 1], axis=0)).then_inc(gathered[t.slot4], 16)


def gated_pass(nc, name, g, i, h_in, ht_in, h_out, ht_out, x_res, x_out):
    final = x_out is not None
    with ExitStack() as ctx:
        f = Phase(nc, ctx, name)
        wt = f.sb("wt", [P, D])
        wih = f.sb("wih", [P, 3 * D])
        whh = f.sb("whh", [P, 3 * D])
        win = f.sb("win", [P, 3 * D])
        b_ih = f.sb("b_ih", [P, 3])
        b_hh = f.sb("b_hh", [P, 3])
        b_rz = f.sb("b_rz", [P, 2])
        idx = f.sb("idx", [P, 4, J], I32)
        rows = f.sb("rows", [P, 4, J, D])
        ht = f.sb("ht", [P, 4, SUPER])
        st = f.sb("st", [P, 2, SUPER])
        r, z, n1, n2, n3 = (f.sb(s, [P, 2, SUPER]) for s in ("r", "z", "n1", "n2", "n3"))
        d1, d2, hn = (f.sb(s, [P, 2, SUPER]) for s in ("d1", "d2", "hn"))
        out = f.sb("out", [P, 2, J, D])
        bank = [f.ps(f"bank{b}") for b in range(8)]
        ps_s, ps_out, ps_r, ps_z, ps_nh, ps_ni = bank[0], bank[1], bank[2:4], bank[4:6], bank[6], bank[7]
        w_loaded, w_made, w_copied, b_made = (f.sem(s) for s in ("w_loaded", "w_made", "w_copied", "b_made"))
        idx_loaded, gathered, ht_loaded = (
            f.sems(s, 4) for s in ("idx_loaded", "gathered", "ht_loaded"))
        stored, ht_stored = f.sems("stored"), f.sems("ht_stored")
        s_turned, s_copied, r_made, z_made, nh_made, ni_made, h_turned = (
            f.sem(s) for s in ("s_turned", "s_copied", "r_made", "z_made", "nh_made", "ni_made", "h_turned"))
        r_done, z_done, n_done, n1_done, n2_done, d1_done, d2_done, h_done, out_done = (
            f.sem(s) for s in ("r_done", "z_done", "n_done", "n1_done", "n2_done", "d1_done", "d2_done",
                               "h_done", "out_done"))
        if final:
            x = f.sb("x", [P, 4, J, D])
            y = f.sb("y", [P, 2, J, D])
            ln = LayerNormBuffers(f, "ln")
            x_loaded, y_done = f.sems("x_loaded", 4), f.sem("y_done")
        block = ctx.enter_context(nc.Block())

        @block.sync
        def _(sp):
            for dst_, src_ in ((wt[:, :], g["msg_wt"][i]), (wih[:, :], g["wih_t"]), (whh[:, :], g["whh_t"]),
                               (b_ih[:, :], g["b_ih"].rearrange("(c p) -> p c", p=P)),
                               (b_hh[:, :], g["b_hh"].rearrange("(c p) -> p c", p=P))):
                sp.dma_start(dst_, src_, allow_slow_non_contiguous=True).then_inc(w_loaded, 16)

            def step(tile_at):
                if t := tile_at(0):
                    wait_alone(sp, gathered[t.slot4], 64 * t.u4)
                    sp.dma_start(idx[:, t.slot4, :], list_tile(g["ptr_dst"], t)).then_inc(idx_loaded[t.slot4], 16)
                    wait_alone(sp, h_done, t.n - 3)
                    sp.dma_start(ht[:, t.slot4, :], fm_tile(ht_in, t)).then_inc(ht_loaded[t.slot4], 16)
                    if final:
                        wait_alone(sp, out_done, t.n - 3)
                        sp.dma_start(x[:, t.slot4, :, :].rearrange("p j d -> p (j d)"),
                                     nm_tile(x_res, t)).then_inc(x_loaded[t.slot4], 16)
            over_tiles(sp, NT, 0, step)

        @block.gpsimd
        def _(pool):
            if final:
                nc.gpsimd.memset(ln.power[:, :], -0.5).then_inc(ln.power_set, 1)

            def step(tile_at):
                if t := tile_at(0):
                    gather_step(nc, pool, t, idx, rows, g["sums"], idx_loaded, s_turned, gathered)
                if final and (t := tile_at(4)):
                    ln.rstd(nc, pool, t)
            over_tiles(pool, NT, 4, step)

        @block.tensor
        def _(pe):
            pe.wait_ge(w_loaded, 16 * 5)
            nc.tensor.matmul(ps_s[:, 0:3 * D], wt[:, :], wih[:, :], start=True, stop=True).then_inc(w_made, 1)
            pe.wait_ge(w_copied, 1)

            def gate(bank_, c, t, sem, hidden=True, inputs=True):
                if inputs:
                    last = nc.tensor.matmul(bank_[:, :], win[:, c * D:(c + 1) * D], st[:, t.slot, :],
                                            start=True, stop=not hidden)
                if hidden:
                    last = nc.tensor.matmul(bank_[:, :], whh[:, c * D:(c + 1) * D], ht[:, t.slot4, :],
                                            start=not inputs, stop=True)
                last.then_inc(sem, 1)

            def step(tile_at):
                if t := tile_at(0):
                    wait(pe, gathered[t.slot4], 64 * (t.u4 + 1))
                    wait(pe, s_copied, t.n)
                    for j in range(J):
                        last = nc.tensor.transpose(ps_s[:, j * P:(j + 1) * P], rows[:, t.slot4, j, :],
                                                   g["ident"][:, :])
                    last.then_inc(s_turned, 1)
                if t := tile_at(1):
                    wait(pe, s_copied, t.n + 1)
                    wait(pe, ht_loaded[t.slot4], 16 * (t.u4 + 1))
                    wait(pe, r_done, t.n - 1)
                    gate(ps_r[t.slot], 0, t, r_made)
                    wait(pe, n1_done, t.n)
                    gate(ps_nh, 2, t, nh_made, inputs=False)
                if t := tile_at(2):
                    wait(pe, h_done, t.n + 1)
                    wait(pe, out_done, t.n)
                    for j in range(J):
                        last = nc.tensor.transpose(ps_out[:, j * D:(j + 1) * D],
                                                   hn[:, t.slot, j * P:(j + 1) * P], g["ident"][:, :])
                    last.then_inc(h_turned, 1)
                if t := tile_at(1):
                    wait(pe, z_done, t.n - 1)
                    gate(ps_z[t.slot], 1, t, z_made)
                    wait(pe, n2_done, t.n)
                    gate(ps_ni, 2, t, ni_made, hidden=False)
            over_tiles(pe, NT, 2, step)

        @block.vector
        def _(dve):
            dve.wait_ge(w_loaded, 16 * 5)
            nc.vector.tensor_tensor(b_rz[:, :], b_ih[:, 0:2], b_hh[:, 0:2], ALU.add).then_inc(b_made, 1)
            dve.wait_ge(w_made, 1)
            nc.vector.tensor_copy(win[:, :], ps_s[:, 0:3 * D]).then_inc(w_copied, 1)

            def step(tile_at):
                if final and (t := tile_at(3)):
                    ln.shifts(nc, dve, t)
                if t := tile_at(2):
                    wait(dve, n_done, t.n + 1)
                    nc.vector.tensor_tensor(d1[:, t.slot, :], ht[:, t.slot4, :], n3[:, t.slot, :],
                                            ALU.subtract).then_inc(d1_done, 1)
                    wait(dve, z_done, t.n + 1)
                    wait(dve, d1_done, t.n + 1)
                    nc.vector.tensor_tensor(d2[:, t.slot, :], d1[:, t.slot, :], z[:, t.slot, :],
                                            ALU.mult).then_inc(d2_done, 1)
                    wait(dve, d2_done, t.n + 1)
                    wait(dve, h_turned, t.n - 1)
                    if not final:
                        wait(dve, ht_stored[t.slot], 16 * t.u)
                    nc.vector.tensor_tensor(hn[:, t.slot, :], d2[:, t.slot, :], n3[:, t.slot, :],
                                            ALU.add).then_inc(h_done, 1)
                if t := tile_at(1):
                    wait(dve, nh_made, t.n + 1)
                    wait(dve, r_done, t.n + 1)
                    nc.vector.scalar_tensor_tensor(n1[:, t.slot, :], ps_nh[:, :], b_hh[:, 2:3], r[:, t.slot, :],
                                                   ALU.add, ALU.mult).then_inc(n1_done, 1)
                if t := tile_at(2):
                    wait(dve, h_turned, t.n + 1)
                    if final:
                        wait(dve, x_loaded[t.slot4], 16 * (t.u4 + 1))
                        wait(dve, y_done, t.n - 1)
                        nc.vector.tensor_tensor(out[:, t.slot, :, :].rearrange("p j d -> p (j d)"),
                                                ps_out[:, :], x[:, t.slot4, :, :].rearrange("p j d -> p (j d)"),
                                                ALU.add).then_inc(out_done, 1)
                        wait(dve, out_done, t.n + 1)
                        ln.statistics(nc, dve, t, [out[:, t.slot, j, :] for j in range(J)], y_done)
                    else:
                        wait(dve, stored[t.slot], 16 * t.u)
                        nc.vector.tensor_copy(out[:, t.slot, :, :].rearrange("p j d -> p (j d)"),
                                              ps_out[:, :]).then_inc(out_done, 1)
                if t := tile_at(1):
                    wait(dve, n1_done, t.n + 1)
                    wait(dve, ni_made, t.n + 1)
                    wait(dve, n_done, t.n - 1)
                    nc.vector.tensor_tensor(n2[:, t.slot, :], n1[:, t.slot, :], ps_ni[:, :],
                                            ALU.add).then_inc(n2_done, 1)
            over_tiles(dve, NT, 3 if final else 2, step)

        @block.scalar
        def _(act):
            act.wait_ge(b_made, 1)

            def step(tile_at):
                if t := tile_at(0):
                    wait(act, s_turned, t.n + 1)
                    wait(act, ni_made, t.n - 1)
                    nc.scalar.activation(st[:, t.slot, :], ps_s[:, :], ACT.Copy).then_inc(s_copied, 1)
                if t := tile_at(1):
                    wait(act, r_made, t.n + 1)
                    wait(act, n1_done, t.n - 1)
                    nc.scalar.activation(r[:, t.slot, :], ps_r[t.slot][:, :], ACT.Sigmoid,
                                         bias=b_rz[:, 0:1]).then_inc(r_done, 1)
                    wait(act, z_made, t.n + 1)
                    wait(act, d2_done, t.n - 1)
                    nc.scalar.activation(z[:, t.slot, :], ps_z[t.slot][:, :], ACT.Sigmoid,
                                         bias=b_rz[:, 1:2]).then_inc(z_done, 1)
                    wait(act, n2_done, t.n + 1)
                    wait(act, h_done, t.n - 1)
                    nc.scalar.activation(n3[:, t.slot, :], n2[:, t.slot, :], ACT.Tanh,
                                         bias=b_ih[:, 2:3]).then_inc(n_done, 1)
                if final:
                    if t := tile_at(3):
                        wait(act, stored[t.slot], 16 * t.u)
                        ln.apply(nc, act, t, [out[:, t.slot, j, :] for j in range(J)],
                                 [y[:, t.slot, j, :] for j in range(J)], y_done)
                    if t := tile_at(4):
                        wait(act, y_done, t.n + 1)
                        act.dma_start(nm_tile(x_out, t), y[:, t.slot, :, :].rearrange("p j d -> p (j d)")
                                      ).then_inc(stored[t.slot], 16)
                elif t := tile_at(3):
                    wait(act, h_done, t.n + 1)
                    act.dma_start(fm_tile(ht_out, t), hn[:, t.slot, :]).then_inc(ht_stored[t.slot], 16)
                    wait(act, out_done, t.n + 1)
                    act.dma_start(nm_tile(h_out, t), out[:, t.slot, :, :].rearrange("p j d -> p (j d)")
                                  ).then_inc(stored[t.slot], 16)
            over_tiles(act, NT, 4, step)
            for b in range(2):
                act.wait_ge(stored[b], 16 * (NT // 2))
                if not final:
                    act.wait_ge(ht_stored[b], 16 * (NT // 2))


class LayerNormBuffers:

    def __init__(self, f, name):
        self.stats = f.sb(f"{name}_stats", [P, 2, J, 6])
        self.mv = f.sb(f"{name}_mv", [P, 2, J, 2])
        self.var = f.sb(f"{name}_var", [P, 2, J])
        self.inv = f.sb(f"{name}_inv", [P, 2, J])
        self.shift = f.sb(f"{name}_shift", [P, 2, J])
        self.power = f.sb(f"{name}_power", [P, J])
        self.power_set = f.sem(f"{name}_power_set")
        self.std = f.sb(f"{name}_std", [P, 2, J])
        self.stats_done, self.mv_done, self.var_done, self.std_done, self.inv_done, self.shift_done = (
            f.sem(f"{name}_{s}") for s in ("stats_done", "mv_done", "var_done", "std_done", "inv_done", "shift_done"))

    def statistics(self, nc, dve, t, parts, applied):
        wait(dve, applied, t.n - 1)
        for j, part in enumerate(parts):
            last = nc.vector.bn_stats(self.stats[:, t.slot, j, :], part)
        last.then_inc(self.stats_done, 1)
        wait_alone(dve, self.stats_done, t.n + 1)
        for j in range(J):
            last = nc.vector.bn_aggr(self.mv[:, t.slot, j, :], self.stats[:, t.slot, j, :])
        last.then_inc(self.mv_done, 1)
        wait(dve, self.mv_done, t.n + 1)
        nc.vector.tensor_scalar(self.var[:, t.slot, :], self.mv[:, t.slot, :, 1], EPS, None,
                                ALU.add).then_inc(self.var_done, 1)

    def root(self, nc, act, t):
        wait(act, self.var_done, t.n + 1)
        nc.scalar.activation(self.std[:, t.slot, :], self.var[:, t.slot, :], ACT.Sqrt).then_inc(self.std_done, 1)

    def invert(self, nc, dve, t):
        wait(dve, self.std_done, t.n + 1)
        nc.vector.reciprocal(self.inv[:, t.slot, :], self.std[:, t.slot, :]).then_inc(self.inv_done, 1)

    def rstd(self, nc, pool, t):
        if isinstance(t.n, int) and t.n == 0:
            pool.wait_ge(self.power_set, 1)
        wait(pool, self.var_done, t.n + 1)
        nc.gpsimd.tensor_tensor(self.inv[:, t.slot, :], self.var[:, t.slot, :], self.power[:, :],
                                ALU.pow).then_inc(self.inv_done, 1)

    def shifts(self, nc, dve, t):
        wait(dve, self.inv_done, t.n + 1)
        nc.vector.scalar_tensor_tensor(self.shift[:, t.slot, :], self.mv[:, t.slot, :, 0], -1.0,
                                       self.inv[:, t.slot, :], ALU.mult, ALU.mult).then_inc(self.shift_done, 1)

    def apply(self, nc, act, t, parts, outs, applied):
        wait(act, self.shift_done, t.n + 1)
        for j, (part, out) in enumerate(zip(parts, outs)):
            last = nc.scalar.activation(out, part, ACT.Identity, bias=self.shift[:, t.slot, j:j + 1],
                                        scale=self.inv[:, t.slot, j:j + 1])
        last.then_inc(applied, 1)


def mean_pass(nc, name, g, x_in, ptr, inv_count, w_x, x_out, normed, h_out=None, ht_out=None):
    with ExitStack() as ctx:
        f = Phase(nc, ctx, name)
        w = f.sb("w", [P, D])
        idx = f.sb("idx", [P, 4, J], I32)
        inv_n = f.sb("inv_n", [P, 4, J])
        rows = f.sb("rows", [P, 4, J, D])
        x = f.sb("x", [P, 4, J, D])
        xt = f.sb("xt", [P, 2, SUPER])
        v = f.sb("v", [P, 2, J, D])
        res = f.sb("res", [P, 2, J, D])
        y = f.sb("y", [P, 2, J, D])
        ln = LayerNormBuffers(f, "ln")
        ps_x, ps_v = f.ps("ps_x"), [f.ps(f"ps_v{b}") for b in range(2)]
        w_loaded = f.sem("w_loaded")
        idx_loaded, inv_loaded, x_loaded, gathered = (
            f.sems(s, 4) for s in ("idx_loaded", "inv_loaded", "x_loaded", "gathered"))
        stored = f.sems("stored")
        x_turned, xt_done, product_made, v_done, res_done, y_done = (
            f.sem(s) for s in ("x_turned", "xt_done", "product_made", "v_done", "res_done", "y_done"))
        if normed:
            squares = f.sb("squares", [P, 2, J, D])
            length2 = f.sb("length2", [P, 2, J])
            inv_len = f.sb("inv_len", [P, 2, J])
            length = f.sb("length", [P, 2, J])
            length2_done, length_done, inv_len_done = (
                f.sem(s) for s in ("length2_done", "length_done", "inv_len_done"))
        if h_out is not None:
            lin = f.sb("lin", [P, D])
            lin_b = f.sb("lin_b", [P, 1])
            yt = f.sb("yt", [P, 2, SUPER])
            ht = f.sb("ht", [P, 2, SUPER])
            h = f.sb("h", [P, 2, SUPER])
            ps_y, ps_ht, ps_h = f.ps("ps_y"), f.ps("ps_ht"), f.ps("ps_h")
            ht_stored, h_stored = f.sems("ht_stored"), f.sems("h_stored")
            y_turned, yt_done, ht_made, ht_done, h_turned, h_done = (
                f.sem(s) for s in ("y_turned", "yt_done", "ht_made", "ht_done", "h_turned", "h_done"))
        block = ctx.enter_context(nc.Block())

        last_lag = 7 if h_out is not None else 5

        @block.sync
        def _(sp):
            sp.dma_start(w[:, :], w_x).then_inc(w_loaded, 16)
            if h_out is not None:
                sp.dma_start(lin[:, :], g["lin_wt"]).then_inc(w_loaded, 16)
                sp.dma_start(lin_b[:, :], column(g["lin_b"])).then_inc(w_loaded, 16)

            def step(tile_at):
                if t := tile_at(0):
                    wait_alone(sp, gathered[t.slot4], 64 * t.u4)
                    sp.dma_start(idx[:, t.slot4, :], list_tile(ptr, t)).then_inc(idx_loaded[t.slot4], 16)
                    wait_alone(sp, v_done, t.n - 3)
                    sp.dma_start(inv_n[:, t.slot4, :], list_tile(inv_count, t)).then_inc(inv_loaded[t.slot4], 16)
                    wait_alone(sp, x_turned, t.n - 3)
                    wait_alone(sp, res_done, t.n - 3)
                    sp.dma_start(flat(x[:, t.slot4, :, :]), nm_tile(x_in, t)).then_inc(x_loaded[t.slot4], 16)
            over_tiles(sp, NT, 0, step)

        @block.gpsimd
        def _(pool):
            def step(tile_at):
                if t := tile_at(0):
                    gather_step(nc, pool, t, idx, rows, g["sums"], idx_loaded, v_done, gathered)
            over_tiles(pool, NT, 0, step)

        @block.tensor
        def _(pe):
            pe.wait_ge(w_loaded, 16 * (3 if h_out is not None else 1))

            def step(tile_at):
                if t := tile_at(0):
                    wait(pe, x_loaded[t.slot4], 16 * (t.u4 + 1))
                    wait(pe, xt_done, t.n)
                    for j in range(J):
                        last = nc.tensor.transpose(ps_x[:, j * P:(j + 1) * P], x[:, t.slot4, j, :], g["ident"][:, :])
                    last.then_inc(x_turned, 1)
                if t := tile_at(1):
                    wait(pe, xt_done, t.n + 1)
                    wait(pe, v_done, t.n - 1)
                    for j in range(J):
                        last = nc.tensor.matmul(ps_v[t.slot][:, j * D:(j + 1) * D], xt[:, t.slot, j * P:(j + 1) * P],
                                                w[:, :], start=True, stop=True)
                    last.then_inc(product_made, 1)
                if h_out is not None and (t := tile_at(7)):
                    wait(pe, ht_done, t.n + 1)
                    wait(pe, h_done, t.n)
                    for j in range(J):
                        last = nc.tensor.transpose(ps_h[:, j * D:(j + 1) * D], ht[:, t.slot, j * P:(j + 1) * P],
                                                   g["ident"][:, :])
                    last.then_inc(h_turned, 1)
                if h_out is not None and (t := tile_at(6)):
                    wait(pe, yt_done, t.n + 1)
                    wait(pe, ht_done, t.n)
                    nc.tensor.matmul(ps_ht[:, :], lin[:, :], yt[:, t.slot, :], start=True,
                                     stop=True).then_inc(ht_made, 1)
                if h_out is not None and (t := tile_at(5)):
                    wait(pe, y_done, t.n + 1)
                    wait(pe, yt_done, t.n)
                    for j in range(J):
                        last = nc.tensor.transpose(ps_y[:, j * P:(j + 1) * P], y[:, t.slot, j, :], g["ident"][:, :])
                    last.then_inc(y_turned, 1)
            over_tiles(pe, NT, last_lag, step)

        @block.vector
        def _(dve):
            def step(tile_at):
                if t := tile_at(3):
                    if normed:
                        wait(dve, length_done, t.n + 1)
                        nc.vector.reciprocal(inv_len[:, t.slot, :], length[:, t.slot, :]).then_inc(inv_len_done, 1)
                        wait_alone(dve, inv_len_done, t.n + 1)
                    wait(dve, y_done, t.n - 1)
                    wait(dve, v_done, t.n + 1)
                    if normed:
                        for j in range(J):
                            last = nc.vector.scalar_tensor_tensor(
                                res[:, t.slot, j, :], v[:, t.slot, j, :], inv_len[:, t.slot, j:j + 1],
                                x[:, t.slot4, j, :], ALU.mult, ALU.add)
                    else:
                        last = nc.vector.tensor_tensor(flat(res[:, t.slot, :, :]), flat(v[:, t.slot, :, :]),
                                                       flat(x[:, t.slot4, :, :]), ALU.add)
                    last.then_inc(res_done, 1)
                if t := tile_at(4):
                    ln.invert(nc, dve, t)
                    ln.shifts(nc, dve, t)
                if t := tile_at(3):
                    wait(dve, res_done, t.n + 1)
                    ln.statistics(nc, dve, t, [res[:, t.slot, j, :] for j in range(J)], y_done)
                if t := tile_at(1):
                    wait(dve, gathered[t.slot4], 64 * (t.u4 + 1))
                    wait(dve, inv_loaded[t.slot4], 16 * (t.u4 + 1))
                    wait(dve, product_made, t.n + 1)
                    wait(dve, res_done, t.n - 1)
                    if normed:
                        wait(dve, length2_done, t.n - 1)
                    for j in range(J):
                        last = nc.vector.scalar_tensor_tensor(
                            v[:, t.slot, j, :], rows[:, t.slot4, j, :], inv_n[:, t.slot4, j:j + 1],
                            ps_v[t.slot][:, j * D:(j + 1) * D], ALU.mult, ALU.add)
                    last.then_inc(v_done, 1)
                if h_out is not None and (t := tile_at(7)):
                    wait(dve, h_turned, t.n + 1)
                    wait(dve, h_stored[t.slot], 16 * t.u)
                    nc.vector.tensor_copy(h[:, t.slot, :], ps_h[:, :]).then_inc(h_done, 1)
            over_tiles(dve, NT, last_lag, step)

        @block.scalar
        def _(act):
            act.wait_ge(w_loaded, 16 * (3 if h_out is not None else 1))

            def step(tile_at):
                if t := tile_at(0):
                    wait(act, x_turned, t.n + 1)
                    wait(act, product_made, t.n - 1)
                    nc.scalar.activation(xt[:, t.slot, :], ps_x[:, :], ACT.Copy).then_inc(xt_done, 1)
                if normed and (t := tile_at(2)):
                    wait(act, v_done, t.n + 1)
                    wait(act, length_done, t.n - 1)
                    for j in range(J):
                        last = nc.scalar.activation(squares[:, t.slot, j, :], v[:, t.slot, j, :], ACT.Square,
                                                    accum_out=length2[:, t.slot, j:j + 1])
                    last.then_inc(length2_done, 1)
                    wait(act, length2_done, t.n + 1)
                    wait(act, inv_len_done, t.n - 1)
                    nc.scalar.activation(length[:, t.slot, :], length2[:, t.slot, :], ACT.Sqrt
                                         ).then_inc(length_done, 1)
                if h_out is not None and (t := tile_at(6)):
                    wait(act, ht_made, t.n + 1)
                    wait(act, ht_stored[t.slot], 16 * t.u)
                    wait(act, h_turned, t.n - 1)
                    nc.scalar.activation(ht[:, t.slot, :], ps_ht[:, :], ACT.Identity,
                                         bias=lin_b[:, :]).then_inc(ht_done, 1)
                if t := tile_at(4):
                    wait(act, stored[t.slot], 16 * t.u)
                    if h_out is not None:
                        wait(act, y_turned, t.n - 1)
                    ln.apply(nc, act, t, [res[:, t.slot, j, :] for j in range(J)],
                             [y[:, t.slot, j, :] for j in range(J)], y_done)
                if h_out is not None and (t := tile_at(5)):
                    wait(act, y_turned, t.n + 1)
                    wait(act, ht_made, t.n - 1)
                    nc.scalar.activation(yt[:, t.slot, :], ps_y[:, :], ACT.Copy).then_inc(yt_done, 1)
                if t := tile_at(5):
                    wait(act, y_done, t.n + 1)
                    act.dma_start(nm_tile(x_out, t), flat(y[:, t.slot, :, :])).then_inc(stored[t.slot], 16)
                if t := tile_at(3):
                    ln.root(nc, act, t)
                if h_out is not None and (t := tile_at(7)):
                    wait(act, ht_done, t.n + 1)
                    act.dma_start(fm_tile(ht_out, t), ht[:, t.slot, :]).then_inc(ht_stored[t.slot], 16)
                    wait(act, h_done, t.n + 1)
                    act.dma_start(nm_tile(h_out, t), h[:, t.slot, :]).then_inc(h_stored[t.slot], 16)
            over_tiles(act, NT, last_lag, step)
            for b in range(2):
                act.wait_ge(stored[b], 16 * (NT // 2))
                if h_out is not None:
                    act.wait_ge(ht_stored[b], 16 * (NT // 2))
                    act.wait_ge(h_stored[b], 16 * (NT // 2))


def attention_pass(nc, name, g):
    with ExitStack() as ctx:
        f = Phase(nc, ctx, name)
        qw, kw, vw, ow = (f.sb(s, [P, D]) for s in ("qw", "kw", "vw", "ow"))
        qb, kb, vb, eb = (f.sb(s, [P, 1]) for s in ("qb", "kb", "vb", "eb"))
        ew = f.sb("ew", [EDIM, HEADS])
        ew_rows = f.sb("ew_rows", [EDIM, HEADS, HEAD_DIM])
        eb_row = f.sb("eb_row", [1, HEADS])
        ones = f.sb("ones", [1, 1])
        eb_wide = f.sb("eb_wide", [1, HEADS, HEAD_DIM])
        ob = f.sb("ob", [P, D])
        blocks = f.sb("blocks", [P, HEADS, HEAD_DIM])
        heads = f.sb("heads", [P, HEADS])
        idx = f.sb("idx", [P, 4, J, 2], I32)
        send = f.sb("send", [P, 4, J, D])
        recv = f.sb("recv", [P, 4, J, D])
        edge_t = f.sb("edge_t", [EDIM, 4, SUPER])
        cut = f.sb("cut", [P, 4, SUPER], BF16)
        send_t, recv_t, q, v, qk, s = (f.sb(n, [P, 2, SUPER]) for n in ("send_t", "recv_t", "q", "v", "qk", "s"))
        top = f.sb("top", [P, 2, SUPER + 1])
        drop = f.sb("drop", [P, 2, SUPER])
        arg = f.sb("arg", [P, 2, 2, SUPER])
        ex = f.sb("ex", [P, 2, 2, SUPER])
        pv, den, num, att = (f.sb(n, [P, 2, SUPER]) for n in ("pv", "den", "num", "att"))
        den_max = f.sb("den_max", [P, 2, J, HEADS])
        den_inv = f.sb("den_inv", [P, 2, J, HEADS])
        inv_wide = f.sb("inv_wide", [P, 2, J, HEADS, HEAD_DIM])
        out = f.sb("out", [P, 2, SUPER])
        ps_send, ps_recv, ps_q, ps_k, ps_v, ps_s, ps_inv, ps_out = (
            f.ps(n) for n in ("ps_send", "ps_recv", "ps_q", "ps_k", "ps_v", "ps_s", "ps_inv", "ps_out"))
        w_loaded, consts_set, eb_made, eb_done, ew_done = (
            f.sem(n) for n in ("w_loaded", "consts_set", "eb_made", "eb_done", "ew_done"))
        idx_loaded, edge_loaded, cut_loaded, sent, received = (
            f.sems(n, 4) for n in ("idx_loaded", "edge_loaded", "cut_loaded", "sent", "received"))
        stored = f.sems("stored")
        (rows_turned, send_done, recv_done, q_made, k_made, v_made, q_done, v_done, qk_done, s_made, s_done,
         carry_done, top_done, arg0_done, drop_done, arg_done, ex_done, pv_done, den_done, num_done,
         den_made, max_done, inv_done, wide_done, inv_turned, att_done, out_made, out_done) = (
            f.sem(n) for n in ("rows_turned", "send_done", "recv_done", "q_made", "k_made", "v_made", "q_done",
                               "v_done", "qk_done", "s_made", "s_done", "carry_done", "top_done", "arg0_done",
                               "drop_done", "arg_done", "ex_done", "pv_done", "den_done", "num_done", "den_made",
                               "max_done", "inv_done", "wide_done", "inv_turned", "att_done", "out_made",
                               "out_done"))
        loads = 12
        block = ctx.enter_context(nc.Block())

        @block.sync
        def _(sp):
            for dst_, src_ in ((qw[:, :], g["qW"]), (kw[:, :], g["kW"]), (vw[:, :], g["vW"]), (ow[:, :], g["oW"]),
                               (qb[:, :], column(g["qb"])), (kb[:, :], column(g["kb"])), (vb[:, :], column(g["vb"])),
                               (ew[:, :], g["eW"]), (ob[:, :], on_all(g["ob"])),
                               (eb_row[:, :], g["eb"].rearrange("(a n) -> a n", a=1)),
                               (blocks[:, :, :], g["blocks_c"]), (heads[:, :], g["heads_c"])):
                sp.dma_start(dst_, src_, allow_slow_non_contiguous=True).then_inc(w_loaded, 16)

            def step(tile_at):
                if t := tile_at(0):
                    wait_alone(sp, sent[t.slot4], 64 * t.u4)
                    wait_alone(sp, received[t.slot4], 64 * t.u4)
                    sp.dma_start(idx[:, t.slot4, :, :].rearrange("p j c -> p (j c)"),
                                 nm_tile(g["by_dst"], t)).then_inc(idx_loaded[t.slot4], 16)
                    wait_alone(sp, s_made, t.n - 3)
                    sp.dma_start(edge_t[:, t.slot4, :], g["edge_attr_t"][:, bass.ds(t.n * SUPER, SUPER)]
                                 ).then_inc(edge_loaded[t.slot4], 16)
                    wait_alone(sp, drop_done, t.n - 3)
                    wait_alone(sp, top_done, t.n - 3)
                    sp.dma_start(cut[:, t.slot4, :], row_tile(g["cut_dst"], t)).then_inc(cut_loaded[t.slot4], 16)
            over_tiles(sp, ET, 0, step)

        @block.gpsimd
        def _(pool):
            def step(tile_at):
                if t := tile_at(0):
                    wait(pool, idx_loaded[t.slot4], 16 * (t.u4 + 1))
                    wait(pool, rows_turned, t.n - 3)
                    pool.nop(nofuse=True)
                    for j in range(J):
                        for col, rows, sem in ((1, send, sent), (0, recv, received)):
                            nc.gpsimd.indirect_dma_start(
                                out=rows[:, t.slot4, j, :], out_offset=None, in_=g["x_in"][:, :],
                                in_offset=bass.IndirectOffsetOnAxis(ap=idx[:, t.slot4, j, col:col + 1], axis=0)).then_inc(sem[t.slot4], 16)
            over_tiles(pool, ET, 0, step)

        @block.tensor
        def _(pe):
            pe.wait_ge(w_loaded, 16 * loads)
            pe.wait_ge(eb_done, 1)
            nc.tensor.matmul(ps_s[:, 0:1], eb_wide[:, :, :].rearrange("a h d -> a (h d)"), ones[:, :],
                             start=True, stop=True).then_inc(eb_made, 1)
            pe.wait_ge(eb_done, 2)
            pe.wait_ge(ew_done, 1)

            def step(tile_at):
                if t := tile_at(0):
                    wait(pe, sent[t.slot4], 64 * (t.u4 + 1))
                    wait(pe, send_done, t.n)
                    for j in range(J):
                        nc.tensor.transpose(edge_columns(ps_send[:, :])[:, j, :], send[:, t.slot4, j, :], g["ident"][:, :])
                    wait(pe, received[t.slot4], 64 * (t.u4 + 1))
                    wait(pe, recv_done, t.n)
                    for j in range(J):
                        last = nc.tensor.transpose(edge_columns(ps_recv[:, :])[:, j, :], recv[:, t.slot4, j, :],
                                                   g["ident"][:, :])
                    last.then_inc(rows_turned, 1)
                if t := tile_at(2):
                    wait(pe, den_done, t.n + 1)
                    wait(pe, att_done, t.n)
                    for j in range(J):
                        last = nc.tensor.matmul(ps_inv[:, j * HEADS:(j + 1) * HEADS],
                                                edge_columns(den[:, t.slot, :])[:, j, :], heads[:, :],
                                                start=True, stop=True)
                    last.then_inc(den_made, 1)
                if t := tile_at(0):
                    wait(pe, send_done, t.n + 1)
                    wait(pe, q_done, t.n)
                    nc.tensor.matmul(ps_q[:, :], qw[:, :], send_t[:, t.slot, :], start=True,
                                     stop=True).then_inc(q_made, 1)
                    wait(pe, recv_done, t.n + 1)
                    wait(pe, qk_done, t.n)
                    nc.tensor.matmul(ps_k[:, :], kw[:, :], recv_t[:, t.slot, :], start=True,
                                     stop=True).then_inc(k_made, 1)
                    wait(pe, v_done, t.n)
                    nc.tensor.matmul(ps_v[:, :], vw[:, :], send_t[:, t.slot, :], start=True,
                                     stop=True).then_inc(v_made, 1)
                if t := tile_at(2):
                    wait(pe, wide_done, t.n + 1)
                    wait(pe, inv_done, t.n + 1)
                    for j in range(J):
                        last = nc.tensor.transpose(edge_columns(ps_inv[:, :])[:, j, :],
                                                   inv_wide[:, t.slot, j, :, :].rearrange("p h d -> p (h d)"),
                                                   g["ident"][:, :])
                    last.then_inc(inv_turned, 1)
                if t := tile_at(0):
                    wait(pe, qk_done, t.n + 1)
                    wait(pe, edge_loaded[t.slot4], 16 * (t.u4 + 1))
                    wait(pe, s_done, t.n)
                    nc.tensor.matmul(ps_s[:, :], blocks[:, :, :].rearrange("p h d -> p (h d)"), qk[:, t.slot, :],
                                     start=True, stop=False)
                    nc.tensor.matmul(ps_s[:, :], ew_rows[:, :, :].rearrange("p h d -> p (h d)"),
                                     edge_t[:, t.slot4, :], start=False, stop=True).then_inc(s_made, 1)
                if t := tile_at(2):
                    wait(pe, att_done, t.n + 1)
                    wait(pe, out_done, t.n)
                    for j in range(J):
                        last = nc.tensor.matmul(ps_out[:, j * D:(j + 1) * D], edge_columns(att[:, t.slot, :])[:, j, :],
                                                ow[:, :], start=True, stop=True)
                    last.then_inc(out_made, 1)
            over_tiles(pe, ET, 2, step)

        @block.vector
        def _(dve):
            dve.wait_ge(w_loaded, 16 * loads)
            nc.vector.memset(ones[:, :], 1.0).then_inc(consts_set, 1)
            dve.wait_ge(consts_set, 1)
            nc.vector.tensor_copy(eb_wide[:, :, :], eb_row[:, :].unsqueeze(2).broadcast_to([1, HEADS, HEAD_DIM])
                                  ).then_inc(eb_done, 1)
            nc.vector.tensor_copy(ew_rows[:, :, :], ew[:, :].unsqueeze(2).broadcast_to([EDIM, HEADS, HEAD_DIM])
                                  ).then_inc(ew_done, 1)
            dve.wait_ge(eb_made, 1)
            nc.vector.tensor_copy(eb[:, :], ps_s[:, 0:1]).then_inc(eb_done, 1)

            def step(tile_at):
                if t := tile_at(0):
                    wait(dve, k_made, t.n + 1)
                    wait(dve, q_done, t.n + 1)
                    wait(dve, s_made, t.n - 1)
                    nc.vector.scalar_tensor_tensor(qk[:, t.slot, :], ps_k[:, :], kb[:, :], q[:, t.slot, :],
                                                   ALU.add, ALU.mult).then_inc(qk_done, 1)
                if t := tile_at(2):
                    wait(dve, den_made, t.n + 1)
                    nc.vector.tensor_scalar(den_max[:, t.slot, :, :].rearrange("p j h -> p (j h)"),
                                            ps_inv[:, 0:J * HEADS], 1e-8, None, ALU.max).then_inc(max_done, 1)
                    wait(dve, max_done, t.n + 1)
                    wait(dve, wide_done, t.n - 1)
                    nc.vector.reciprocal(den_inv[:, t.slot, :, :].rearrange("p j h -> p (j h)"),
                                         den_max[:, t.slot, :, :].rearrange("p j h -> p (j h)")).then_inc(inv_done, 1)
                if t := tile_at(1):
                    wait(dve, top_done, t.n)
                    wait(dve, arg_done, t.n - 1)
                    prev = top[:, 1 - t.slot, SUPER:SUPER + 1]
                    first = isinstance(t.n, int) and t.n == 0
                    if first:
                        nc.vector.memset(top[:, 0, 0:1], 0.0).then_inc(carry_done, 1)
                    else:
                        nc.vector.tensor_copy(top[:, t.slot, 0:1], prev).then_inc(carry_done, 1)
                    wait(dve, carry_done, t.n + 1)
                    wait(dve, cut_loaded[t.slot4], 16 * (t.u4 + 1))
                    wait(dve, s_done, t.n + 1)
                    nc.vector.tensor_tensor_scan(top[:, t.slot, 1:SUPER + 1], cut[:, t.slot4, :], s[:, t.slot, :],
                                                 top[:, t.slot, 0:1], ALU.add, ALU.max).then_inc(top_done, 1)
                    wait(dve, top_done, t.n + 1)
                    wait(dve, ex_done, t.n - 1)
                    nc.vector.tensor_tensor(arg[:, t.slot, 0, :], s[:, t.slot, :], top[:, t.slot, 1:SUPER + 1],
                                            ALU.subtract).then_inc(arg0_done, 1)
                    nc.vector.tensor_tensor(drop[:, t.slot, :], top[:, t.slot, 0:SUPER], cut[:, t.slot4, :],
                                            ALU.add).then_inc(drop_done, 1)
                    wait(dve, drop_done, t.n + 1)
                    nc.vector.tensor_tensor(arg[:, t.slot, 1, :], drop[:, t.slot, :], top[:, t.slot, 1:SUPER + 1],
                                            ALU.subtract).then_inc(arg_done, 1)
                if t := tile_at(2):
                    wait(dve, inv_turned, t.n + 1)
                    wait(dve, out_made, t.n - 1)
                    nc.vector.tensor_tensor(att[:, t.slot, :], num[:, t.slot, :], ps_inv[:, :],
                                            ALU.mult).then_inc(att_done, 1)
                if t := tile_at(1):
                    wait(dve, ex_done, t.n + 1)
                    wait(dve, v_done, t.n + 1)
                    nc.vector.tensor_tensor(pv[:, t.slot, :], v[:, t.slot, :], ex[:, t.slot, 0, :],
                                            ALU.mult).then_inc(pv_done, 1)
                    first = isinstance(t.n, int) and t.n == 0
                    wait(dve, den_made, t.n - 1)
                    wait(dve, den_done, t.n)
                    nc.vector.tensor_tensor_scan(
                        den[:, t.slot, :], ex[:, t.slot, 1, :], ex[:, t.slot, 0, :],
                        0.0 if first else den[:, 1 - t.slot, SUPER - 1:SUPER],
                        ALU.mult, ALU.add).then_inc(den_done, 1)
                    wait(dve, pv_done, t.n + 1)
                    wait(dve, num_done, t.n)
                    wait(dve, att_done, t.n - 1)
                    nc.vector.tensor_tensor_scan(
                        num[:, t.slot, :], ex[:, t.slot, 1, :], pv[:, t.slot, :],
                        0.0 if first else num[:, 1 - t.slot, SUPER - 1:SUPER],
                        ALU.mult, ALU.add).then_inc(num_done, 1)
                if t := tile_at(2):
                    wait(dve, out_made, t.n + 1)
                    wait(dve, stored[t.slot], 16 * t.u)
                    nc.vector.tensor_tensor(
                        out[:, t.slot, :].rearrange("p (j d) -> p j d", j=J),
                        ps_out[:, :].rearrange("p (j d) -> p j d", j=J),
                        ob[:, :].unsqueeze(1).broadcast_to([P, J, D]), ALU.add).then_inc(out_done, 1)
            over_tiles(dve, ET, 2, step)

        @block.scalar
        def _(act):
            act.wait_ge(w_loaded, 16 * loads)
            act.wait_ge(eb_done, 2)

            def step(tile_at):
                if t := tile_at(0):
                    wait(act, rows_turned, t.n + 1)
                    wait(act, v_made, t.n - 1)
                    nc.scalar.activation(send_t[:, t.slot, :], ps_send[:, :], ACT.Copy).then_inc(send_done, 1)
                    nc.scalar.activation(recv_t[:, t.slot, :], ps_recv[:, :], ACT.Copy).then_inc(recv_done, 1)
                    wait(act, q_made, t.n + 1)
                    wait(act, qk_done, t.n - 1)
                    nc.scalar.activation(q[:, t.slot, :], ps_q[:, :], ACT.Identity, bias=qb[:, :]).then_inc(q_done, 1)
                if t := tile_at(2):
                    wait(act, inv_done, t.n + 1)
                    wait(act, inv_turned, t.n - 1)
                    nc.scalar.activation(
                        inv_wide[:, t.slot, :, :, :].rearrange("p j h d -> p (j h) d"),
                        den_inv[:, t.slot, :, :].rearrange("p j h -> p (j h)").unsqueeze(2).broadcast_to(
                            [P, J * HEADS, HEAD_DIM]), ACT.Copy).then_inc(wide_done, 1)
                if t := tile_at(1):
                    wait(act, arg0_done, t.n + 1)
                    wait(act, arg_done, t.n + 1)
                    wait(act, num_done, t.n - 1)
                    nc.scalar.activation(ex[:, t.slot, :, :].rearrange("p a n -> p (a n)"),
                                         arg[:, t.slot, :, :].rearrange("p a n -> p (a n)"), ACT.Exp
                                         ).then_inc(ex_done, 1)
                if t := tile_at(0):
                    wait(act, v_made, t.n + 1)
                    wait(act, pv_done, t.n - 1)
                    nc.scalar.activation(v[:, t.slot, :], ps_v[:, :], ACT.Identity, bias=vb[:, :]).then_inc(v_done, 1)
                    wait(act, s_made, t.n + 1)
                    wait(act, arg0_done, t.n - 1)
                    nc.scalar.activation(s[:, t.slot, :], ps_s[:, :], ACT.Identity, bias=eb[:, :]).then_inc(s_done, 1)
                if t := tile_at(3):
                    wait(act, out_done, t.n + 1)
                    act.dma_start(nm_tile(g["att_sums"], t), out[:, t.slot, :]).then_inc(stored[t.slot], 16)
            over_tiles(act, ET, 3, step)
            for b in range(2):
                act.wait_ge(stored[b], 16 * (ET // 2))


def ffn_pass(nc, name, g):
    with ExitStack() as ctx:
        f = Phase(nc, ctx, name)
        C = FFN // P
        f1, f1c = f.sb("f1", [P, FFN]), f.sb("f1c", [P, FFN])
        fb, fbc, rest1, rest2 = (f.sb(s, [P, FFN]) for s in ("fb", "fbc", "rest1", "rest2"))
        hi, mid, lo, bias_rows = (f.sb(s, [P, FFN], BF16) for s in ("hi", "mid", "lo", "bias_rows"))
        ones = f.sb("ones", [P, P], BF16)
        total, mean = f.sb("total", [P, 2]), f.sb("mean", [P, 2])
        f2 = f.sb("f2", [P, C, D])
        g1, b1, f2b = (f.sb(s, [P, 1]) for s in ("g1", "b1", "f2b"))
        gf, bf = f.sb("gf", [P, C]), f.sb("bf", [P, C])
        g2, b2 = f.sb("g2", [P, D]), f.sb("b2", [P, D])
        idx = f.sb("idx", [P, 4, J], I32)
        rows, x = f.sb("rows", [P, 4, J, D]), f.sb("x", [P, 4, J, D])
        xr, a, xh, u, xb, z, y = (f.sb(s, [P, 2, J, D]) for s in ("xr", "a", "xh", "u", "xb", "z", "y"))
        x1t, y2t = f.sb("x1t", [P, 2, SUPER]), f.sb("y2t", [P, 2, SUPER])
        squares = f.sb("squares", [P, J, FFN])
        sumsq, varf, invf = (f.sb(s, [P, 2, J]) for s in ("sumsq", "varf", "invf"))
        hs = f.sb("hs", [P, J, FFN])
        hg = f.sb("hg", [P, C, SUPER])
        ln1, ln2, ln3 = (LayerNormBuffers(f, s) for s in ("ln1", "ln2", "ln3"))
        ps_h = [f.ps(f"ps_h{j}") for j in range(J)]
        ps_g = [f.ps(f"ps_g{b}") for b in range(2)]
        ps_f, ps_t = f.ps("ps_f"), f.ps("ps_t")
        idx_loaded, x_loaded, gathered = (f.sems(s, 4) for s in ("idx_loaded", "x_loaded", "gathered"))
        xr_loaded, stored = f.sems("xr_loaded"), f.sems("stored")
        (w_loaded, ones_set, total_done, mean_done, centred, hi_done, rest1_done, mid_done, rest2_done,
         lo_done, rows_done) = (
            f.sem(s) for s in ("w_loaded", "ones_set", "total_done", "mean_done", "centred", "hi_done",
                               "rest1_done", "mid_done", "rest2_done", "lo_done", "rows_done"))
        (a_done, xh_done, xh_turned, x1t_done, h_made, sumsq_done, varf_done, invf_done, hs_done, g_turned, gelu_done,
         f2_made, y2t_done, y2_turned, u_done, xb_done, z_done, y_done) = (
            f.sem(s) for s in ("a_done", "xh_done", "xh_turned", "x1t_done", "h_made", "sumsq_done", "varf_done",
                               "invf_done", "hs_done", "g_turned", "gelu_done", "f2_made", "y2t_done", "y2_turned",
                               "u_done", "xb_done", "z_done", "y_done"))
        power = ln1.power
        loads = 11
        block = ctx.enter_context(nc.Block())

        @block.sync
        def _(sp):
            for dst_, src_ in ((f1[:, :], g["f1W"]), (fb[:, :], on_all(g["f1b"])),
                               (f2[:, :, :], g["f2W"].rearrange("(c p) d -> p c d", p=P)),
                               (g1[:, :], column(g["ln1_g"])), (b1[:, :], column(g["ln1_b"])), (f2b[:, :], column(g["f2b"])),
                               (gf[:, :], g["lnf_g"].rearrange("(c p) -> p c", p=P)),
                               (bf[:, :], g["lnf_b"].rearrange("(c p) -> p c", p=P)),
                               (g2[:, :], on_all(g["ln2_g"])), (b2[:, :], on_all(g["ln2_b"]))):
                sp.dma_start(dst_, src_, allow_slow_non_contiguous=True).then_inc(w_loaded, 16)

            def step(tile_at):
                if t := tile_at(0):
                    wait_alone(sp, gathered[t.slot4], 64 * t.u4)
                    sp.dma_start(idx[:, t.slot4, :], list_tile(g["ptr_dst"], t)).then_inc(idx_loaded[t.slot4], 16)
                    wait_alone(sp, a_done, t.n - 3)
                    sp.dma_start(flat(x[:, t.slot4, :, :]), nm_tile(g["x_in"], t)).then_inc(x_loaded[t.slot4], 16)
                if t := tile_at(3):
                    wait_alone(sp, xb_done, t.n - 1)
                    sp.dma_start(flat(xr[:, t.slot, :, :]), nm_tile(g["x_in"], t)).then_inc(xr_loaded[t.slot], 16)
            over_tiles(sp, NT, 3, step)

        @block.gpsimd
        def _(pool):
            nc.gpsimd.memset(power[:, :], -0.5).then_inc(ln1.power_set, 1)
            pool.wait_ge(ln1.power_set, 1)
            pool.wait_ge(w_loaded, 16 * (loads - 1))

            def gather(t, js):
                for j in js:
                    nc.gpsimd.indirect_dma_start(
                        out=rows[:, t.slot4, j, :], out_offset=None, in_=g["att_sums"][:, :],
                        in_offset=bass.IndirectOffsetOnAxis(ap=idx[:, t.slot4, j:j + 1], axis=0)).then_inc(gathered[t.slot4], 16)

            def inverse_root(out, var, ready, done, t):
                wait(pool, ready, t.n + 1)
                nc.gpsimd.tensor_tensor(out[:, t.slot, :], var[:, t.slot, :], power[:, :], ALU.pow).then_inc(done, 1)

            def step(tile_at):
                if t := tile_at(4):
                    inverse_root(invf, varf, varf_done, invf_done, t)
                if t := tile_at(2):
                    wait(pool, gathered[t.slot4], 64 * (t.u4 + 1))
                    wait(pool, x_loaded[t.slot4], 16 * (t.u4 + 1))
                    wait(pool, xh_done, t.n - 1)
                    wait(pool, ln1.stats_done, t.n - 1)
                    nc.gpsimd.tensor_tensor(flat(a[:, t.slot, :, :]), flat(rows[:, t.slot4, :, :]),
                                            flat(x[:, t.slot4, :, :]), ALU.add).then_inc(a_done, 1)
                if t := tile_at(5):
                    inverse_root(ln2.inv, ln2.var, ln2.var_done, ln2.inv_done, t)
                if t := tile_at(4):
                    wait(pool, xr_loaded[t.slot], 16 * (t.u + 1))
                    wait(pool, z_done, t.n - 1)
                    nc.gpsimd.tensor_tensor(xb[:, t.slot, :, :], xr[:, t.slot, :, :],
                                            b2[:, :].unsqueeze(1).broadcast_to([P, J, D]), ALU.add
                                            ).then_inc(xb_done, 1)
                if t := tile_at(0):
                    wait(pool, idx_loaded[t.slot4], 16 * (t.u4 + 1))
                    wait(pool, a_done, t.n - 3)
                    pool.nop(nofuse=True)
                    gather(t, (0, 1))
                if t := tile_at(2):
                    inverse_root(ln1.inv, ln1.var, ln1.var_done, ln1.inv_done, t)
                if t := tile_at(0):
                    gather(t, (2, 3))
                if t := tile_at(5):
                    inverse_root(ln3.inv, ln3.var, ln3.var_done, ln3.inv_done, t)
            over_tiles(pool, NT, 5, step)

        @block.tensor
        def _(pe):
            pe.wait_ge(w_loaded, 16 * (loads - 1))
            pe.wait_ge(rows_done, 3)
            pe.wait_ge(centred, 2)
            pe.wait_ge(ones_set, 2)

            def step(tile_at):
                if t := tile_at(3):
                    wait(pe, xh_done, t.n + 1)
                    wait(pe, u_done, t.n - 1)
                    wait(pe, x1t_done, t.n)
                    for j in range(J):
                        last = nc.tensor.transpose(ps_t[:, j * P:(j + 1) * P], xh[:, t.slot, j, :], g["ident"][:, :])
                    last.then_inc(xh_turned, 1)
                if t := tile_at(4):
                    wait(pe, hs_done, t.n + 1)
                    wait(pe, y2t_done, t.n)

                    def turn(c):
                        wait(pe, gelu_done, 4 * t.n + c - 1)
                        for j in range(J):
                            last = nc.tensor.transpose(ps_g[c % 2][:, j * P:(j + 1) * P],
                                                       hs[:, j, c * P:(c + 1) * P], g["ident"][:, :])
                        last.then_inc(g_turned, 1)

                    def down(c):
                        wait(pe, gelu_done, 4 * t.n + c + 1)
                        last = nc.tensor.matmul(ps_f[:, :], f2[:, c, :], hg[:, c, :], start=c == 0, stop=c == C - 1)
                        if c == C - 1:
                            last.then_inc(f2_made, 1)
                    turn(0)
                    turn(1)
                    for c in range(C):
                        down(c)
                        if c + 2 < C:
                            turn(c + 2)
                if t := tile_at(3):
                    wait(pe, x1t_done, t.n + 1)
                    wait(pe, hs_done, t.n)
                    for j in range(J):
                        nc.tensor.matmul(ps_h[j][:, :], x1t[:, t.slot, j * P:(j + 1) * P], f1c[:, :],
                                         start=True, stop=False)
                        nc.tensor.matmul(ps_h[j][:, :], ones[:, :], bias_rows[:, :], start=False,
                                         stop=True).then_inc(h_made, 1)
                if t := tile_at(4):
                    wait(pe, y2t_done, t.n + 1)
                    wait(pe, x1t_done, t.n + 2 if not isinstance(t.n, int) else min(t.n + 2, NT))
                    for j in range(J):
                        last = nc.tensor.transpose(ps_t[:, j * D:(j + 1) * D], y2t[:, t.slot, j * P:(j + 1) * P],
                                                   g["ident"][:, :])
                    last.then_inc(y2_turned, 1)
            over_tiles(pe, NT, 4, step)

        @block.vector
        def _(dve):
            dve.wait_ge(w_loaded, 16 * (loads - 1))
            nc.vector.memset(ones[:, :], 1.0).then_inc(ones_set, 1)
            nc.vector.memset(bias_rows[:, :], 0.0).then_inc(ones_set, 1)
            nc.vector.reduce_sum(total[:, 0:1], f1[:, :], axis=AX.X).then_inc(total_done, 1)
            nc.vector.reduce_sum(total[:, 1:2], fb[:, :], axis=AX.X).then_inc(total_done, 1)
            dve.wait_ge(total_done, 2)
            nc.vector.tensor_scalar(mean[:, :], total[:, :], 1.0 / FFN, None, ALU.mult).then_inc(mean_done, 1)
            dve.wait_ge(mean_done, 1)
            nc.vector.tensor_scalar(f1c[:, :], f1[:, :], mean[:, 0:1], None, ALU.subtract).then_inc(centred, 1)
            nc.vector.tensor_scalar(fbc[:, :], fb[:, :], mean[:, 1:2], None, ALU.subtract).then_inc(centred, 1)
            dve.wait_ge(centred, 2)
            nc.vector.tensor_copy(hi[:, :], fbc[:, :]).then_inc(hi_done, 1)
            dve.wait_ge(hi_done, 1)
            nc.vector.tensor_tensor(rest1[:, :], fbc[:, :], hi[:, :], ALU.subtract).then_inc(rest1_done, 1)
            dve.wait_ge(rest1_done, 1)
            nc.vector.tensor_copy(mid[:, :], rest1[:, :]).then_inc(mid_done, 1)
            dve.wait_ge(mid_done, 1)
            nc.vector.tensor_tensor(rest2[:, :], rest1[:, :], mid[:, :], ALU.subtract).then_inc(rest2_done, 1)
            dve.wait_ge(rest2_done, 1)
            nc.vector.tensor_copy(lo[:, :], rest2[:, :]).then_inc(lo_done, 1)
            dve.wait_ge(lo_done, 1)
            dve.wait_ge(ones_set, 2)
            for row, part in ((0, hi), (32, mid), (64, lo)):
                nc.vector.tensor_copy(bias_rows[row:row + 1, :], part[row:row + 1, :]).then_inc(rows_done, 1)

            def step(tile_at):
                if t := tile_at(3):
                    wait(dve, ln1.inv_done, t.n + 1)
                    wait(dve, xh_turned, t.n - 1)
                    for j in range(J):
                        last = nc.vector.tensor_scalar(xh[:, t.slot, j, :], a[:, t.slot, j, :],
                                                       ln1.mv[:, t.slot, j, 0:1], ln1.inv[:, t.slot, j:j + 1],
                                                       ALU.subtract, ALU.mult)
                    last.then_inc(xh_done, 1)
                if t := tile_at(4):
                    wait(dve, invf_done, t.n + 1)
                    wait(dve, g_turned, 4 * t.n)
                    for j in range(J):
                        last = nc.vector.tensor_scalar(hs[:, j, :], ps_h[j][:, :], invf[:, t.slot, j:j + 1], None,
                                                       ALU.mult)
                    last.then_inc(hs_done, 1)
                if t := tile_at(2):
                    wait(dve, a_done, t.n + 1)
                    ln1.statistics(nc, dve, t, [a[:, t.slot, j, :] for j in range(J)], xh_done)
                if t := tile_at(5):
                    wait(dve, ln2.inv_done, t.n + 1)
                    wait(dve, xb_done, t.n + 1)
                    wait(dve, u_done, t.n + 1)
                    wait(dve, y_done, t.n - 1)
                    for j in range(J):
                        last = nc.vector.scalar_tensor_tensor(z[:, t.slot, j, :], u[:, t.slot, j, :],
                                                              ln2.inv[:, t.slot, j:j + 1], xb[:, t.slot, j, :],
                                                              ALU.mult, ALU.add)
                    last.then_inc(z_done, 1)
                    wait(dve, z_done, t.n + 1)
                    ln3.statistics(nc, dve, t, [z[:, t.slot, j, :] for j in range(J)], y_done)
                if t := tile_at(6):
                    ln3.shifts(nc, dve, t)
                if t := tile_at(4):
                    wait(dve, f2_made, t.n + 1)
                    wait(dve, y2_turned, t.n - 1)
                    nc.vector.scalar_tensor_tensor(y2t[:, t.slot, :], ps_f[:, :], f2b[:, :], x1t[:, t.slot, :],
                                                   ALU.add, ALU.add).then_inc(y2t_done, 1)
                if t := tile_at(3):
                    wait(dve, sumsq_done, t.n + 1)
                    wait(dve, invf_done, t.n - 1)
                    nc.vector.tensor_scalar(varf[:, t.slot, :], sumsq[:, t.slot, :], 1.0 / FFN, EPS,
                                            ALU.mult, ALU.add).then_inc(varf_done, 1)
                if t := tile_at(4):
                    wait(dve, y2_turned, t.n + 1)
                    ln2.statistics(nc, dve, t, [ps_t[:, j * D:(j + 1) * D] for j in range(J)], z_done)
                    for j in range(J):
                        last = nc.vector.scalar_tensor_tensor(u[:, t.slot, j, :], ps_t[:, j * D:(j + 1) * D],
                                                              ln2.mv[:, t.slot, j, 0:1], g2[:, :],
                                                              ALU.subtract, ALU.mult)
                    last.then_inc(u_done, 1)
            over_tiles(dve, NT, 6, step)

        @block.scalar
        def _(act):
            act.wait_ge(w_loaded, 16 * (loads - 1))

            def step(tile_at):
                if t := tile_at(3):
                    wait(act, xh_turned, t.n + 1)
                    wait(act, y2t_done, t.n - 1)
                    nc.scalar.activation(x1t[:, t.slot, :], ps_t[:, :], ACT.Identity, bias=b1[:, :],
                                         scale=g1[:, :]).then_inc(x1t_done, 1)
                if t := tile_at(4):
                    for c in range(C):
                        wait(act, g_turned, 4 * t.n + c + 1)
                        wait(act, f2_made, t.n)
                        nc.scalar.activation(hg[:, c, :], ps_g[c % 2][:, :], ACT.Gelu, bias=bf[:, c:c + 1],
                                             scale=gf[:, c:c + 1]).then_inc(gelu_done, 1)
                if t := tile_at(3):
                    wait(act, varf_done, t.n - 1)
                    for j in range(J):
                        wait(act, h_made, 4 * t.n + j + 1)
                        last = nc.scalar.activation(squares[:, j, :], ps_h[j][:, :], ACT.Square,
                                                    accum_out=sumsq[:, t.slot, j:j + 1])
                    last.then_inc(sumsq_done, 1)
                if t := tile_at(6):
                    wait(act, stored[t.slot], 16 * t.u)
                    ln3.apply(nc, act, t, [z[:, t.slot, j, :] for j in range(J)],
                              [y[:, t.slot, j, :] for j in range(J)], y_done)
                if t := tile_at(7):
                    wait(act, y_done, t.n + 1)
                    act.dma_start(nm_tile(g["x_a"], t), flat(y[:, t.slot, :, :])).then_inc(stored[t.slot], 16)
            over_tiles(act, NT, 7, step)
            for b in range(2):
                act.wait_ge(stored[b], 16 * (NT // 2))


class Chain:

    def __init__(self, f, eng, name):
        self.eng, self.sem, self.count = eng, f.sem(name), 0

    def __call__(self, instruction):
        self.count += 1
        instruction.then_inc(self.sem, 1)
        self.eng.wait_ge(self.sem, self.count)


def segment_starts(nc, name, pairs, keep_out, cut_out):
    rows, width = ECOLS // 2, 2 * P
    with ExitStack() as ctx:
        f = Phase(nc, ctx, name)
        now, before = f.sb("now", [rows, width, 2], I32), f.sb("before", [rows, width, 2], I32)
        keep, cut = f.sb("keep", [rows, width], BF16), f.sb("cut", [rows, width], BF16)
        loaded, made, stored = f.sem("loaded"), f.sem("made"), f.sem("stored")
        block = ctx.enter_context(nc.Block())

        @block.sync
        def _(sp):
            for buf, lead in ((now, 1), (before, 0)):
                sp.dma_start(buf[:, :, :], pairs[lead:lead + EP, :].rearrange("(r w) two -> r w two", w=width)
                             ).then_inc(loaded, 16)
            sp.wait_ge(made, 1)
            sp.dma_start(keep_out.rearrange("(r w) -> r w", w=width), keep[:, :]).then_inc(stored, 16)
            if cut_out is not None:
                sp.wait_ge(made, 2)
                sp.dma_start(cut_out.rearrange("(r w) -> r w", w=width), cut[:, :]).then_inc(stored, 16)
            sp.wait_ge(stored, 16 if cut_out is None else 32)

        @block.vector
        def _(dve):
            dve.wait_ge(loaded, 32)
            nc.vector.tensor_tensor(keep[:, :], now[:, :, 0], before[:, :, 0], ALU.is_equal).then_inc(made, 1)
            if cut_out is not None:
                dve.wait_ge(made, 1)
                nc.vector.tensor_scalar(cut[:, :], keep[:, :], BIG, -BIG, ALU.mult, ALU.add).then_inc(made, 1)


def node_lists(nc, name, g, side, ptr_out, inv_out):
    ROWS = NP // SUPER
    with ExitStack() as ctx:
        f = Phase(nc, ctx, name)
        pairs = f.sb("pairs", [P, ECOLS, 2], I32)
        low_i, high_i = f.sb("low_i", [P, ECOLS], I32), f.sb("high_i", [P, ECOLS], I32)
        low, high = f.sb("low", [P, ECOLS]), f.sb("high", [P, ECOLS])
        digits_f, digits = f.sb("digits_f", [P, DIGIT]), f.sb("digits", [P, DIGIT], BF16)
        before = f.sb("before", [P, P])
        hot_high, hot_low = f.sb("hot_high", [P, 2, HI_DIGITS], BF16), f.sb("hot_low", [P, 2, DIGIT], BF16)
        (ones, count, cum, last_e, has, clipped, inverse, spare, moved, picked) = (
            f.sb(s, [ROWS, SUPER]) for s in ("ones", "count", "cum", "last_e", "has", "clipped", "inverse", "spare",
                                             "moved", "picked"))
        ptr_i = f.sb("ptr_i", [ROWS, SUPER], I32)
        offset = f.sb("offset", [ROWS, 1])
        ps_hist = [f.ps(f"ps_hist{b}") for b in range(2)]
        ps_off = f.ps("ps_off")
        loaded, hot_done, counted, cum_done, off_made, lists_made, stored = (
            f.sem(s) for s in ("loaded", "hot_done", "counted", "cum_done", "off_made", "lists_made", "stored"))
        block = ctx.enter_context(nc.Block())

        @block.sync
        def _(sp):
            for dst_, src_ in ((pairs[:, :, :], g["edges"][1:EP + 1, :].rearrange("(p c) two -> p c two", p=P)),
                               (digits_f[:, :], g["digits_c"]), (before[:, :], g["before_c"]), (spare[:, :], g["spare_c"])):
                sp.dma_start(dst_, src_).then_inc(loaded, 16)
            sp.wait_ge(lists_made, 2)
            sp.dma_start(ptr_out.rearrange("(r w) -> r w", w=SUPER), ptr_i[:, :]).then_inc(stored, 16)
            sp.dma_start(inv_out.rearrange("(r w) -> r w", w=SUPER), inverse[:, :]).then_inc(stored, 16)
            sp.wait_ge(stored, 32)

        @block.tensor
        def _(pe):
            def count_column(c, b, first):
                wait(pe, hot_done, 2 * (c + 1))
                for half in range(2):
                    last = nc.tensor.matmul(
                        ps_hist[half][0:ROWS, 0:DIGIT],
                        hot_high[:, b, :].rearrange("p (a h) -> p h a", h=2)[:, half, :],
                        hot_low[:, b, :], start=first, stop=True, skip_group_check=True)
                last.then_inc(counted, 1)
            for c in range(2):
                count_column(c, c, c == 0)
            with pe.Fori(1, ECOLS // 2) as k:
                for b in range(2):
                    count_column(2 * k + b, b, False)
            pe.wait_ge(cum_done, 1)
            nc.tensor.matmul(ps_off[0:ROWS, 0:1], before[0:ROWS, 0:ROWS], cum[:, SUPER - 1:SUPER],
                             start=True, stop=True).then_inc(off_made, 1)

        @block.vector
        def _(dve):
            link = Chain(f, dve, "link")
            dve.wait_ge(loaded, 16 * 4)
            link(nc.vector.memset(ones[:, :], 1.0))
            link(nc.vector.tensor_copy(digits[:, :], digits_f[:, :]))
            link(nc.vector.tensor_scalar(low_i[:, :], pairs[:, :, side], DIGIT - 1, None, ALU.bitwise_and))
            link(nc.vector.tensor_scalar(high_i[:, :], pairs[:, :, side], 8, None, ALU.logical_shift_right))
            link(nc.vector.tensor_copy(low[:, :], low_i[:, :]))
            link(nc.vector.tensor_copy(high[:, :], high_i[:, :]))

            def one_hot(c, b):
                wait(dve, counted, c - 1)
                nc.vector.tensor_scalar(hot_high[:, b, :], digits[:, 0:HI_DIGITS], high[:, bass.ds(c, 1)], None,
                                        ALU.is_equal).then_inc(hot_done, 1)
                nc.vector.tensor_scalar(hot_low[:, b, :], digits[:, :], low[:, bass.ds(c, 1)], None,
                                        ALU.is_equal).then_inc(hot_done, 1)
            for c in range(2):
                one_hot(c, c)
            with dve.Fori(1, ECOLS // 2) as k:
                for b in range(2):
                    one_hot(2 * k + b, b)
            dve.wait_ge(counted, ECOLS)
            for half in range(2):
                link(nc.vector.tensor_copy(count[:, half * DIGIT:(half + 1) * DIGIT], ps_hist[half][0:ROWS, 0:DIGIT]))
            nc.vector.tensor_tensor_scan(cum[:, :], ones[:, :], count[:, :], 0.0, ALU.mult,
                                         ALU.add).then_inc(cum_done, 1)
            link(nc.vector.tensor_scalar(has[:, :], count[:, :], 1.0, None, ALU.min))
            link(nc.vector.tensor_scalar(clipped[:, :], count[:, :], 1.0, None, ALU.max))
            nc.vector.reciprocal(inverse[:, :], clipped[:, :]).then_inc(lists_made, 1)
            dve.wait_ge(off_made, 1)
            link(nc.vector.tensor_copy(offset[:, :], ps_off[0:ROWS, 0:1]))
            link(nc.vector.tensor_scalar(last_e[:, :], cum[:, :], offset[:, :], -1.0, ALU.add, ALU.add))
            link(nc.vector.tensor_tensor(moved[:, :], last_e[:, :], spare[:, :], ALU.subtract))
            link(nc.vector.tensor_tensor(picked[:, :], moved[:, :], has[:, :], ALU.mult))
            nc.vector.tensor_tensor(ptr_i[:, :], picked[:, :], spare[:, :], ALU.add).then_inc(lists_made, 1)


def sort_digit(nc, name, g, pairs_in, swap, high_digit, pairs_out):
    GROUP = ECOLS // 2
    with ExitStack() as ctx:
        f = Phase(nc, ctx, name)
        raw, pairs = f.sb("raw", [P, ECOLS, 2], I32), f.sb("pairs", [P, ECOLS, 2], I32)
        digit_i, digit = f.sb("digit_i", [P, ECOLS], I32), f.sb("digit", [P, ECOLS])
        digits_f, digits = f.sb("digits_f", [P, DIGIT]), f.sb("digits", [P, DIGIT], BF16)
        before_f, before = f.sb("before_f", [P, P]), f.sb("before", [P, P], BF16)
        hot = f.sb("hot", [P, ECOLS, DIGIT], BF16)
        window = f.sb("window", [P, 2 * P], BF16)
        pick = f.sb("pick", [GROUP, GROUP, P], BF16)
        ones = f.sb("ones", [P, DIGIT], BF16)
        counts = f.sb("counts", [GROUP, 2, DIGIT], BF16)
        upto, smaller = f.sb("upto", [P, DIGIT]), f.sb("smaller", [P, DIGIT])
        start, start_i, start_lo_i = (f.sb("start", [GROUP, 2, DIGIT]), f.sb("start_i", [GROUP, 2, DIGIT], I32),
                                      f.sb("start_lo_i", [GROUP, 2, DIGIT], I32))
        start_hi, start_lo = f.sb("start_hi", [GROUP, 2, DIGIT], BF16), f.sb("start_lo", [GROUP, 2, DIGIT], BF16)
        own = f.sb("own", [P, 2, DIGIT])
        rank = f.sb("rank", [P, ECOLS])
        rank_i, rank_p, rank_c, dest = (f.sb(s, [P, ECOLS], I32) for s in ("rank_i", "rank_p", "rank_c", "dest"))
        dest_slot, pair_slot = f.sb("dest_slot", [P, 2, J], I32), f.sb("pair_slot", [P, 2, J, 2], I32)
        lead = f.sb("lead", [1, 2], I32)
        ps_count = [f.ps(f"ps_count{b}") for b in range(2)]
        ps_total, ps_start = f.ps("ps_total"), [f.ps(f"ps_start{b}") for b in range(2)]
        ps_rank = [f.ps(f"ps_rank{b}") for b in range(2)]
        (loaded, tables_set, pick_set, hot_done, counted, counts_done, total_made, starts_made, start_done, rank_made,
         rank_done, dest_done, slots_filled, lead_set, lead_stored) = (
            f.sem(s) for s in ("loaded", "tables_set", "pick_set", "hot_done", "counted", "counts_done", "total_made",
                               "starts_made", "start_done", "rank_made", "rank_done", "dest_done", "slots_filled",
                               "lead_set", "lead_stored"))
        scattered = f.sems("scattered")
        block = ctx.enter_context(nc.Block())

        @block.sync
        def _(sp):
            for dst_, src_ in ((raw[:, :, :], pairs_in), (digits_f[:, :], g["digits_c"]), (before_f[:, :], g["before_c"])):
                sp.dma_start(dst_, src_).then_inc(loaded, 16)
            if high_digit:
                sp.wait_ge(lead_set, 1)
                sp.dma_start(pairs_out[0:1, :], lead[:, :]).then_inc(lead_stored, 16)
                sp.wait_ge(lead_stored, 16)

        @block.gpsimd
        def _(pool):
            nc.gpsimd.tensor_copy(pick[:, :, :], g["ident"][0:GROUP, 0:GROUP].unsqueeze(2).broadcast_to(
                [GROUP, GROUP, P])).then_inc(pick_set, 1)
            pool.wait_ge(dest_done, 1)

            def scatter(c4, u, b):
                wait(pool, scattered[b], 64 * u)
                pool.nop(nofuse=True)
                nc.gpsimd.tensor_copy(dest_slot[:, b, :], dest[:, bass.ds(J * c4, J)]).then_inc(slots_filled, 1)
                nc.gpsimd.tensor_copy(pair_slot[:, b, :, :], pairs[:, bass.ds(J * c4, J), :]).then_inc(slots_filled, 1)
                wait(pool, slots_filled, 2 * (c4 + 1))
                pool.nop(nofuse=True)
                for j in range(J):
                    nc.gpsimd.indirect_dma_start(
                        out=pairs_out[:, :], out_offset=bass.IndirectOffsetOnAxis(ap=dest_slot[:, b, j:j + 1], axis=0),
                        in_=pair_slot[:, b, j, :], in_offset=None).then_inc(scattered[b], 16)
            for b in range(2):
                scatter(b, 0, b)
            with pool.Fori(1, ECOLS // (2 * J)) as k:
                for b in range(2):
                    scatter(2 * k + b, k, b)
            for b in range(2):
                pool.wait_ge(scattered[b], 64 * (ECOLS // (2 * J)))

        @block.tensor
        def _(pe):
            pe.wait_ge(tables_set, 3)

            def count_column(c, m, h, first):
                wait(pe, hot_done, c + 1)
                nc.tensor.matmul(ps_count[h][:, 0:DIGIT], window[:, bass.ds(P - 1 - m, P)],
                                 hot[:, bass.ds(c, 1), :].rearrange("p a d -> p (a d)"), start=first, stop=True,
                                 skip_group_check=True).then_inc(counted, 1)
            for h in range(2):
                count_column(h * GROUP, 0, h, True)
                with pe.Fori(1, GROUP) as m:
                    count_column(h * GROUP + m, m, h, False)
            pe.wait_ge(counts_done, 2)
            for h in range(2):
                last = nc.tensor.matmul(ps_total[:, 0:DIGIT], ones[0:GROUP, 0:P], counts[:, h, :],
                                        start=h == 0, stop=h == 1)
            last.then_inc(total_made, 1)
            nc.tensor.matmul(ps_start[0][0:GROUP, 0:DIGIT], before[0:GROUP, 0:GROUP], counts[:, 0, :],
                             start=True, stop=True).then_inc(starts_made, 1)
            nc.tensor.matmul(ps_start[1][0:GROUP, 0:DIGIT], ones[0:GROUP, 0:GROUP], counts[:, 0, :],
                             start=True, stop=False)
            nc.tensor.matmul(ps_start[1][0:GROUP, 0:DIGIT], before[0:GROUP, 0:GROUP], counts[:, 1, :],
                             start=False, stop=True).then_inc(starts_made, 1)
            pe.wait_ge(start_done, 1)
            pe.wait_ge(pick_set, 1)

            def rank_column(c, m, h, b):
                wait(pe, rank_done, c - 1)
                out = ps_rank[b][:, 0:DIGIT]
                nc.tensor.matmul(out, before[:, :], hot[:, bass.ds(c, 1), :].rearrange("p a d -> p (a d)"),
                                 start=True, stop=False)
                row = pick[:, bass.ds(m, 1), :].rearrange("k a p -> k (a p)")
                nc.tensor.matmul(out, row, start_hi[:, h, :], start=False, stop=False)
                nc.tensor.matmul(out, row, start_lo[:, h, :], start=False, stop=True).then_inc(rank_made, 1)
            for h in range(2):
                for b in range(2):
                    rank_column(h * GROUP + b, b, h, b)
                with pe.Fori(1, GROUP // 2) as k:
                    for b in range(2):
                        rank_column(h * GROUP + 2 * k + b, 2 * k + b, h, b)

        @block.vector
        def _(dve):
            link = Chain(f, dve, "link")
            nc.vector.memset(lead[:, :], -1).then_inc(lead_set, 1)
            link(nc.vector.memset(window[:, :], 0.0))
            nc.vector.memset(window[:, P - 1:P], 1.0).then_inc(tables_set, 1)
            nc.vector.memset(ones[:, :], 1.0).then_inc(tables_set, 1)
            dve.wait_ge(loaded, 16 * 3)
            nc.vector.tensor_copy(before[:, :], before_f[:, :]).then_inc(tables_set, 1)
            link(nc.vector.tensor_copy(digits[:, :], digits_f[:, :]))
            for col in range(2):
                link(nc.vector.tensor_copy(pairs[:, :, col], raw[:, :, 1 - col if swap else col]))
            if high_digit:
                link(nc.vector.tensor_scalar(digit_i[:, :], pairs[:, :, 0], 8, None, ALU.logical_shift_right))
            else:
                link(nc.vector.tensor_scalar(digit_i[:, :], pairs[:, :, 0], DIGIT - 1, None, ALU.bitwise_and))
            link(nc.vector.tensor_copy(digit[:, :], digit_i[:, :]))
            with dve.Fori(0, ECOLS) as c:
                nc.vector.tensor_scalar(hot[:, bass.ds(c, 1), :].rearrange("p a d -> p (a d)"), digits[:, :],
                                        digit[:, bass.ds(c, 1)], None, ALU.is_equal).then_inc(hot_done, 1)
            dve.wait_ge(counted, ECOLS)
            for h in range(2):
                nc.vector.tensor_copy(counts[:, h, :], ps_count[h][0:GROUP, 0:DIGIT]).then_inc(counts_done, 1)
            dve.wait_ge(total_made, 1)
            dve.wait_ge(tables_set, 2)
            link(nc.vector.tensor_tensor_scan(upto[:, :], ones[:, :], ps_total[:, 0:DIGIT], 0.0, ALU.mult, ALU.add))
            link(nc.vector.tensor_tensor(smaller[:, :], upto[:, :], ps_total[:, 0:DIGIT], ALU.subtract))
            dve.wait_ge(starts_made, 2)
            for h in range(2):
                link(nc.vector.tensor_tensor(start[:, h, :], smaller[0:GROUP, :], ps_start[h][0:GROUP, 0:DIGIT],
                                             ALU.add))
            link(nc.vector.tensor_copy(start_i[:, :, :], start[:, :, :]))
            link(nc.vector.tensor_scalar(start_lo_i[:, :, :], start_i[:, :, :], DIGIT - 1, None, ALU.bitwise_and))
            link(nc.vector.tensor_copy(start_lo[:, :, :], start_lo_i[:, :, :]))
            nc.vector.tensor_tensor(start_hi[:, :, :], start[:, :, :], start_lo[:, :, :],
                                    ALU.subtract).then_inc(start_done, 1)

            def rank_column(c, b):
                wait(dve, rank_made, c + 1)
                wait(dve, rank_done, c - 1)
                nc.vector.scalar_tensor_tensor(own[:, b, :], ps_rank[b][:, 0:DIGIT], 1.0,
                                               hot[:, bass.ds(c, 1), :].rearrange("p a d -> p (a d)"),
                                               ALU.mult, ALU.mult, accum_out=rank[:, bass.ds(c, 1)]
                                               ).then_inc(rank_done, 1)
            for b in range(2):
                rank_column(b, b)
            with dve.Fori(1, ECOLS // 2) as k:
                for b in range(2):
                    rank_column(2 * k + b, b)
            dve.wait_ge(rank_done, ECOLS)
            link(nc.vector.tensor_copy(rank_i[:, :], rank[:, :]))
            if high_digit:
                nc.vector.tensor_scalar(dest[:, :], rank_i[:, :], 1, None, ALU.add).then_inc(dest_done, 1)
            else:
                link(nc.vector.tensor_scalar(rank_p[:, :], rank_i[:, :], P - 1, None, ALU.bitwise_and))
                link(nc.vector.tensor_scalar(rank_c[:, :], rank_i[:, :], 7, None, ALU.logical_shift_right))
                nc.vector.scalar_tensor_tensor(dest[:, :], rank_p[:, :], float(ECOLS), rank_c[:, :], ALU.mult,
                                               ALU.add).then_inc(dest_done, 1)


def set_up(nc, name, g):
    with ExitStack() as ctx:
        f = Phase(nc, ctx, name)
        zeros, ob = f.sb("zeros", [P, J, D]), f.sb("ob", [P, D])
        loaded, zeros_set, stored = f.sem("loaded"), f.sem("zeros_set"), f.sem("stored")
        block = ctx.enter_context(nc.Block())

        @block.sync
        def _(sp):
            sp.dma_start(g["ident"][:, :], g["ident_c"]).then_inc(loaded, 16)
            sp.dma_start(ob[:, :], on_all(g["ob"])).then_inc(loaded, 16)
            sp.wait_ge(loaded, 32)
            for j in range(J):
                sp.dma_start(g["att_sums"][EP + j * P:EP + (j + 1) * P, :], ob[:, :]).then_inc(stored, 16)
            sp.wait_ge(zeros_set, 1)
            sp.dma_start(g["sums"][EP:EP + SUPER, :].rearrange("(p j) d -> p j d", j=J), zeros[:, :, :]
                         ).then_inc(stored, 16)
            sp.wait_ge(stored, 16 * (J + 1))

        @block.vector
        def _(dve):
            nc.vector.memset(zeros[:, :, :], 0.0).then_inc(zeros_set, 1)


FLOAT_INPUTS = {
    "L0_gnn_qW": "qW", "L0_gnn_qb": "qb", "L0_gnn_kW": "kW", "L0_gnn_kb": "kb", "L0_gnn_vW": "vW", "L0_gnn_vb": "vb",
    "L0_gnn_eW": "eW", "L0_gnn_eb": "eb", "L0_gnn_oW": "oW", "L0_gnn_ob": "ob", "L0_gnn_ln1_g": "ln1_g",
    "L0_gnn_ln1_b": "ln1_b", "L0_gnn_f1W": "f1W", "L0_gnn_f1b": "f1b", "L0_gnn_lnf_g": "lnf_g",
    "L0_gnn_lnf_b": "lnf_b", "L0_gnn_f2W": "f2W", "L0_gnn_f2b": "f2b", "L0_gnn_ln2_g": "ln2_g",
    "L0_gnn_ln2_b": "ln2_b", "L2_gnn_lin_b": "lin_b", "L2_gnn_b_ih": "b_ih", "L2_gnn_b_hh": "b_hh",
    "L3_gnn_weight": "w_cat",
}
TRANSPOSED_INPUTS = {
    "L1_gnn_W_l": "wl_t", "L1_gnn_W_r": "wr_t", "L2_gnn_lin_w": "lin_wt", "L2_gnn_w_ih": "wih_t",
    "L2_gnn_w_hh": "whh_t",
}


def build(nc, ins, out):
    g = dict(ins)

    def dram(name, shape, dt=F32):
        return nc.dram_tensor(name, shape, dt, kind="Internal").ap()

    g["att_sums"], g["sums"] = dram("att_sums", [EP + SUPER, D]), dram("sums", [EP + SUPER, D])
    g["x_a"], g["x_b"], g["x_c"] = (dram(n, [NP, D]) for n in ("x_a", "x_b", "x_c"))
    g["h_a"], g["h_b"] = (dram(n, [NP, D]) for n in ("h_a", "h_b"))
    g["ht_a"], g["ht_b"] = (dram(n, [NT, P, SUPER]) for n in ("ht_a", "ht_b"))
    g["ptr_dst"], g["ptr_src"] = dram("ptr_dst", [NP], I32), dram("ptr_src", [NP], I32)
    g["inv_dst"], g["inv_src"] = dram("inv_dst", [NP]), dram("inv_src", [NP])
    g["keep_dst"], g["cut_dst"], g["keep_src"] = (dram(n, [EP], BF16) for n in ("keep_dst", "cut_dst", "keep_src"))
    g["half_sorted"] = dram("half_sorted", [EP, 2], I32)
    g["by_src"] = dram("by_src", [EP + 1, 2], I32)
    g["by_dst"] = by_dst = g["edges"][1:EP + 1, :]
    by_src = g["by_src"][1:EP + 1, :]

    with ExitStack() as ctx:
        g["ident"] = ctx.enter_context(nc.sbuf_tensor("ident", [P, P], F32))
        set_up(nc, "setup", g)
        segment_starts(nc, "starts_dst", g["edges"], g["keep_dst"], g["cut_dst"])
        node_lists(nc, "lists_dst", g, 0, g["ptr_dst"], g["inv_dst"])
        node_lists(nc, "lists_src", g, 1, g["ptr_src"], g["inv_src"])
        sort_digit(nc, "sort_low", g, by_dst.rearrange("(p c) two -> p c two", p=P), True, False, g["half_sorted"])
        sort_digit(nc, "sort_high", g, g["half_sorted"].rearrange("(p c) two -> p c two", p=P), False, True, g["by_src"])
        segment_starts(nc, "starts_src", g["by_src"], g["keep_src"], None)
        attention_pass(nc, "attend", g)
        ffn_pass(nc, "ffn", g)
        sum_pass(nc, "sum1", g, g["x_a"], by_src, g["keep_src"], g["wr_t"])
        mean_pass(nc, "mean1", g, g["x_a"], g["ptr_src"], g["inv_src"], g["wl_t"], g["x_b"], True, g["h_a"], g["ht_a"])
        h = [(g["h_a"], g["ht_a"]), (g["h_b"], g["ht_b"]), (g["h_a"], g["ht_a"]), (None, None)]
        for i in range(3):
            sum_pass(nc, f"sum2{i}", g, h[i][0], by_dst, g["keep_dst"], None)
            gated_pass(nc, f"gate{i}", g, i, *h[i], *h[i + 1], g["x_b"], g["x_c"] if i == 2 else None)
        sum_pass(nc, "sum3", g, g["x_c"], by_dst, g["keep_dst"], g["w_cat"][D:2 * D, :])
        mean_pass(nc, "mean3", g, g["x_c"], g["ptr_dst"], g["inv_dst"], g["w_cat"][0:D, :], out, False)


def kernel(**inputs):
    import numpy as np
    import concourse.bacc as bacc
    from concourse import mybir as my
    from concourse.bass_utils import run_bass_kernel_spmd as run

    nc = bacc.Bacc("TRN2", target_bir_lowering=False, num_devices=1)
    arrays = {short: np.ascontiguousarray(inputs[key]) for key, short in FLOAT_INPUTS.items()}
    arrays.update({short: np.ascontiguousarray(np.asarray(inputs[key]).T) for key, short in TRANSPOSED_INPUTS.items()})
    arrays["msg_wt"] = np.ascontiguousarray(np.asarray(inputs["L2_gnn_weight"]).transpose(0, 2, 1))
    x = np.zeros((NP, D), np.float32)
    x[:N] = inputs["x"]
    edges = np.full((EP + 1, 2), PAD_NODE, np.int32)
    edges[0] = -1
    edges[1:E + 1, 0] = inputs["dst"]
    edges[1:E + 1, 1] = inputs["src"]
    edge_t = np.zeros((EDIM, EP), np.float32)
    edge_t[:, :E] = np.asarray(inputs["edge_attr_32"]).T
    arrays.update(x_in=x, edges=edges, edge_attr_t=edge_t)
    head = np.arange(D) // HEAD_DIM
    arrays["ident_c"] = np.eye(P, dtype=np.float32)
    arrays["before_c"] = np.triu(np.ones((P, P), np.float32), 1)
    arrays["digits_c"] = np.tile(np.arange(DIGIT, dtype=np.float32), (P, 1))
    arrays["spare_c"] = np.tile(np.arange(EP, EP + SUPER, dtype=np.float32), (NP // SUPER, 1))
    arrays["blocks_c"] = ((head[:, None] == head[None, :]) * HEAD_DIM ** -0.5).astype(np.float32).reshape(
        P, HEADS, HEAD_DIM)
    arrays["heads_c"] = (np.arange(D)[:, None] == HEAD_DIM * np.arange(HEADS)[None, :]).astype(np.float32)
    ins = {key: nc.dram_tensor(f"in_{key}", a.shape, my.dt.from_np(a.dtype), kind="ExternalInput").ap()
           for key, a in arrays.items()}
    out = nc.dram_tensor("out", (NP, D), F32, kind="ExternalOutput").ap()
    build(nc, ins, out)
    r = run(nc, [{f"in_{key}": a for key, a in arrays.items()}], core_ids=[0])
    return r.results[0]["out"][:N]
```

```python
import concourse.bass as bass
from concourse import mybir
from contextlib import ExitStack

F32 = mybir.dt.float32
BF16 = mybir.dt.bfloat16
I32 = mybir.dt.int32
ALU = mybir.AluOpType
ACT = mybir.ActivationFunctionType
AX = mybir.AxisListType

N, E, D, HEADS, EDIM, FFN = 50000, 25000, 128, 8, 32, 512
P, J = 128, 4
SUPER = P * J
NT = -(-N // (2 * SUPER)) * 2
ET = -(-E // (2 * SUPER)) * 2
NP, EP = NT * SUPER, ET * SUPER
ECOLS = EP // P
PAD_NODE = NP - 1
DIGIT = 256
HI_DIGITS = NP // DIGIT
EPS = 1e-5
BIG = 1e30
HEAD_DIM = D // HEADS


UNROLL = 4


class Tile:

    def __init__(self, u4, slot4):
        self.u4, self.slot4, self.n = u4, slot4, UNROLL * u4 + slot4
        self.slot, self.u = slot4 % 2, 2 * u4 + slot4 // 2


def over_tiles(eng, tiles, lag, step):
    def group(k):
        for b in range(UNROLL):
            def tile_at(behind):
                u4, slot4 = k + (b - behind) // UNROLL, (b - behind) % UNROLL
                if isinstance(k, int) and not 0 <= UNROLL * u4 + slot4 < tiles:
                    return None
                return Tile(u4, slot4)
            step(tile_at)
    first = (lag + 2 * UNROLL - 1) // UNROLL
    for k in range(first):
        group(k)
    with eng.Fori(first, tiles // UNROLL) as k:
        group(k)
    for k in range(tiles // UNROLL, -(-(tiles + lag) // UNROLL)):
        group(k)


def wait(eng, sem, count):
    if not isinstance(count, int) or count > 0:
        eng.wait_ge(sem, count)


def wait_alone(eng, sem, count):
    if not isinstance(count, int) or count > 0:
        eng.wait_ge(sem, count)
        eng.nop(nofuse=True)


def nm_tile(table, t):
    view = table.rearrange("(s p j) d -> s p (j d)", p=P, j=J)
    return view[bass.ds(t.n, 1), :, :].rearrange("s p n -> (s p) n")


def list_tile(values, t):
    view = values.rearrange("(s p j) -> s p j", p=P, j=J)
    return view[bass.ds(t.n, 1), :, :].rearrange("s p j -> (s p) j")


def row_tile(values, t, parts=P):
    view = values.rearrange("(s n) -> s n", n=SUPER)
    return view[bass.ds(t.n, 1), :].broadcast_to([parts, SUPER])


def fm_tile(table, t):
    return table[bass.ds(t.n, 1), :, :].rearrange("s p n -> (s p) n")


def on_all(row):
    n = row.shape[0]
    return row.rearrange("(a n) -> a n", a=1).broadcast_to([P, n])


def column(row):
    return row.rearrange("(n a) -> n a", a=1)


class Phase:

    def __init__(self, nc, ctx, name):
        self.nc, self.ctx, self.name = nc, ctx, name
        self.semaphores = []
        ctx.callback(self.clear)

    def clear(self):
        self.nc.clear_and_free_semaphores(self.semaphores)
        self.nc.all_engine_barrier()

    def sb(self, name, shape, dt=F32):
        return self.ctx.enter_context(self.nc.sbuf_tensor(f"{self.name}_{name}", shape, dt))

    def ps(self, name, shape=(P, SUPER), dt=F32):
        return self.ctx.enter_context(self.nc.psum_tensor(f"{self.name}_{name}", list(shape), dt))

    def sem(self, name):
        self.semaphores.append(self.nc.alloc_semaphore(f"{self.name}_{name}"))
        return self.semaphores[-1]

    def sems(self, name, buffers=2):
        return [self.sem(f"{name}{b}") for b in range(buffers)]


def flat(buf):
    return buf.rearrange("p j d -> p (j d)")


def edge_columns(buf):
    return buf.rearrange("f (p j) -> f j p", j=J)


def sum_pass(nc, name, g, gather_from, pairs, mask, weight):
    with ExitStack() as ctx:
        f = Phase(nc, ctx, name)
        idx = f.sb("idx", [P, 4, J, 2], I32)
        rows = f.sb("rows", [P, 4, J, D])
        keep = f.sb("keep", [P, 4, SUPER], BF16)
        run = f.sb("run", [P, 2, SUPER])
        sums = f.sb("sums", [P, 2, SUPER])
        w = f.sb("w", [P, D])
        ps_rows = [f.ps(f"ps_rows{b}") for b in range(2)]
        ps_sums = [f.ps(f"ps_sums{b}") for b in range(2)]
        w_loaded, idx_loaded, keep_loaded = f.sem("w_loaded"), f.sems("idx_loaded", 4), f.sems("keep_loaded", 4)
        gathered, stored = f.sems("gathered", 4), f.sems("stored")
        rows_turned, scanned, sums_made, sums_copied = (
            f.sem("rows_turned"), f.sem("scanned"), f.sem("sums_made"), f.sem("sums_copied"))
        block = ctx.enter_context(nc.Block())

        @block.sync
        def _(sp):
            if weight is not None:
                sp.dma_start(w[:, :], weight).then_inc(w_loaded, 16)

            def step(tile_at):
                if t := tile_at(0):
                    wait_alone(sp, gathered[t.slot4], 64 * t.u4)
                    sp.dma_start(idx[:, t.slot4, :, :].rearrange("p j c -> p (j c)"),
                                 nm_tile(pairs, t)).then_inc(idx_loaded[t.slot4], 16)
                    wait_alone(sp, scanned, t.n - 3)
                    sp.dma_start(keep[:, t.slot4, :], row_tile(mask, t)).then_inc(keep_loaded[t.slot4], 16)
            over_tiles(sp, ET, 0, step)

        @block.gpsimd
        def _(pool):
            def step(tile_at):
                if t := tile_at(0):
                    wait(pool, idx_loaded[t.slot4], 16 * (t.u4 + 1))
                    wait(pool, rows_turned, t.n - 3)
                    pool.nop(nofuse=True)
                    for j in range(J):
                        nc.gpsimd.indirect_dma_start(
                            out=rows[:, t.slot4, j, :], out_offset=None, in_=gather_from[:, :],
                            in_offset=bass.IndirectOffsetOnAxis(ap=idx[:, t.slot4, j, 1:2], axis=0)).then_inc(gathered[t.slot4], 16)
            over_tiles(pool, ET, 0, step)

        @block.tensor
        def _(pe):
            if weight is not None:
                pe.wait_ge(w_loaded, 16)

            def step(tile_at):
                if t := tile_at(0):
                    wait(pe, gathered[t.slot4], 64 * (t.u4 + 1))
                    wait(pe, scanned, t.n - 1)
                    for j in range(J):
                        last = nc.tensor.transpose(edge_columns(ps_rows[t.slot][:, :])[:, j, :],
                                                   rows[:, t.slot4, j, :], g["ident"][:, :])
                    last.then_inc(rows_turned, 1)
                if t := tile_at(1):
                    wait(pe, scanned, t.n + 1)
                    wait(pe, sums_copied, t.n - 1)
                    for j in range(J):
                        out = ps_sums[t.slot][:, j * D:(j + 1) * D]
                        part = edge_columns(run[:, t.slot, :])[:, j, :]
                        if weight is None:
                            last = nc.tensor.transpose(out, part, g["ident"][:, :])
                        else:
                            last = nc.tensor.matmul(out, part, w[:, :], start=True, stop=True)
                    last.then_inc(sums_made, 1)
            over_tiles(pe, ET, 1, step)

        @block.vector
        def _(dve):
            def step(tile_at):
                if t := tile_at(0):
                    wait(dve, keep_loaded[t.slot4], 16 * (t.u4 + 1))
                    wait(dve, rows_turned, t.n + 1)
                    wait(dve, sums_made, t.n - 1)
                    wait(dve, scanned, t.n)
                    first = isinstance(t.n, int) and t.n == 0
                    nc.vector.tensor_tensor_scan(
                        run[:, t.slot, :], keep[:, t.slot4, :], ps_rows[t.slot][:, :],
                        0.0 if first else run[:, 1 - t.slot, SUPER - 1:SUPER],
                        ALU.mult, ALU.add).then_inc(scanned, 1)
            over_tiles(dve, ET, 0, step)

        @block.scalar
        def _(act):
            def step(tile_at):
                if t := tile_at(1):
                    wait(act, sums_made, t.n + 1)
                    wait(act, stored[t.slot], 16 * t.u)
                    nc.scalar.activation(sums[:, t.slot, :], ps_sums[t.slot][:, :],
                                         ACT.Copy).then_inc(sums_copied, 1)
                if t := tile_at(2):
                    wait(act, sums_copied, t.n + 1)
                    act.dma_start(nm_tile(g["sums"], t), sums[:, t.slot, :]).then_inc(stored[t.slot], 16)
            over_tiles(act, ET, 2, step)
            for b in range(2):
                act.wait_ge(stored[b], 16 * (ET // 2))


def gather_step(nc, pool, t, idx, rows, table, idx_loaded, rows_free, gathered):
    wait(pool, idx_loaded[t.slot4], 16 * (t.u4 + 1))
    wait(pool, rows_free, t.n - 3)
    pool.nop(nofuse=True)
    for j in range(J):
        nc.gpsimd.indirect_dma_start(
            out=rows[:, t.slot4, j, :], out_offset=None, in_=table[:, :],
            in_offset=bass.IndirectOffsetOnAxis(ap=idx[:, t.slot4, j:j + 1], axis=0)).then_inc(gathered[t.slot4], 16)


def gated_pass(nc, name, g, i, h_in, ht_in, h_out, ht_out, x_res, x_out):
    final = x_out is not None
    with ExitStack() as ctx:
        f = Phase(nc, ctx, name)
        wt = f.sb("wt", [P, D])
        wih = f.sb("wih", [P, 3 * D])
        whh = f.sb("whh", [P, 3 * D])
        win = f.sb("win", [P, 3 * D])
        b_ih = f.sb("b_ih", [P, 3])
        b_hh = f.sb("b_hh", [P, 3])
        b_rz = f.sb("b_rz", [P, 2])
        idx = f.sb("idx", [P, 4, J], I32)
        rows = f.sb("rows", [P, 4, J, D])
        ht = f.sb("ht", [P, 4, SUPER])
        st = f.sb("st", [P, 2, SUPER])
        r, z, n1, n2, n3 = (f.sb(s, [P, 2, SUPER]) for s in ("r", "z", "n1", "n2", "n3"))
        d1, d2, hn = (f.sb(s, [P, 2, SUPER]) for s in ("d1", "d2", "hn"))
        out = f.sb("out", [P, 4, J, D])
        bank = [f.ps(f"bank{b}") for b in range(8)]
        ps_s, ps_out, ps_r, ps_z, ps_nh, ps_ni = bank[0], bank[1], bank[2:4], bank[4:6], bank[6], bank[7]
        w_loaded, w_made, w_copied, b_made = (f.sem(s) for s in ("w_loaded", "w_made", "w_copied", "b_made"))
        idx_loaded, gathered, ht_loaded = (
            f.sems(s, 4) for s in ("idx_loaded", "gathered", "ht_loaded"))
        stored, ht_stored = f.sems("stored"), f.sems("ht_stored")
        s_turned, s_copied, r_made, z_made, nh_made, ni_made, h_turned = (
            f.sem(s) for s in ("s_turned", "s_copied", "r_made", "z_made", "nh_made", "ni_made", "h_turned"))
        r_done, z_done, n_done, n1_done, n2_done, d1_done, d2_done, h_done, out_done = (
            f.sem(s) for s in ("r_done", "z_done", "n_done", "n1_done", "n2_done", "d1_done", "d2_done",
                               "h_done", "out_done"))
        if final:
            x = f.sb("x", [P, 4, J, D])
            y = f.sb("y", [P, 2, J, D])
            ln = LayerNormBuffers(f, "ln")
            x_loaded, y_done = f.sems("x_loaded", 4), f.sem("y_done")
        block = ctx.enter_context(nc.Block())

        @block.sync
        def _(sp):
            for dst_, src_ in ((wt[:, :], g["msg_wt"][i]), (wih[:, :], g["wih_t"]), (whh[:, :], g["whh_t"]),
                               (b_ih[:, :], g["b_ih"].rearrange("(c p) -> p c", p=P)),
                               (b_hh[:, :], g["b_hh"].rearrange("(c p) -> p c", p=P))):
                sp.dma_start(dst_, src_, allow_slow_non_contiguous=True).then_inc(w_loaded, 16)

            def step(tile_at):
                if t := tile_at(0):
                    wait_alone(sp, gathered[t.slot4], 64 * t.u4)
                    sp.dma_start(idx[:, t.slot4, :], list_tile(g["ptr_dst"], t)).then_inc(idx_loaded[t.slot4], 16)
                    wait_alone(sp, h_done, t.n - 3)
                    sp.dma_start(ht[:, t.slot4, :], fm_tile(ht_in, t)).then_inc(ht_loaded[t.slot4], 16)
                    if final:
                        wait_alone(sp, out_done, t.n - 3)
                        sp.dma_start(x[:, t.slot4, :, :].rearrange("p j d -> p (j d)"),
                                     nm_tile(x_res, t)).then_inc(x_loaded[t.slot4], 16)
            over_tiles(sp, NT, 0, step)

        @block.gpsimd
        def _(pool):
            if final:
                nc.gpsimd.memset(ln.power[:, :], -0.5).then_inc(ln.power_set, 1)

            def step(tile_at):
                if t := tile_at(0):
                    gather_step(nc, pool, t, idx, rows, g["sums"], idx_loaded, s_turned, gathered)
                if final and (t := tile_at(4)):
                    ln.rstd(nc, pool, t, y_done)
            over_tiles(pool, NT, 4, step)

        @block.tensor
        def _(pe):
            pe.wait_ge(w_loaded, 16 * 5)
            nc.tensor.matmul(ps_s[:, 0:3 * D], wt[:, :], wih[:, :], start=True, stop=True).then_inc(w_made, 1)
            pe.wait_ge(w_copied, 1)

            def gate(bank_, c, t, sem, hidden=True, inputs=True):
                if inputs:
                    last = nc.tensor.matmul(bank_[:, :], win[:, c * D:(c + 1) * D], st[:, t.slot, :],
                                            start=True, stop=not hidden)
                if hidden:
                    last = nc.tensor.matmul(bank_[:, :], whh[:, c * D:(c + 1) * D], ht[:, t.slot4, :],
                                            start=not inputs, stop=True)
                last.then_inc(sem, 1)

            def step(tile_at):
                if t := tile_at(0):
                    wait(pe, gathered[t.slot4], 64 * (t.u4 + 1))
                    wait(pe, s_copied, t.n)
                    for j in range(J):
                        last = nc.tensor.transpose(ps_s[:, j * P:(j + 1) * P], rows[:, t.slot4, j, :],
                                                   g["ident"][:, :])
                    last.then_inc(s_turned, 1)
                if t := tile_at(1):
                    wait(pe, s_copied, t.n + 1)
                    wait(pe, ht_loaded[t.slot4], 16 * (t.u4 + 1))
                    wait(pe, r_done, t.n - 1)
                    gate(ps_r[t.slot], 0, t, r_made)
                    wait(pe, n1_done, t.n)
                    gate(ps_nh, 2, t, nh_made, inputs=False)
                if t := tile_at(1):
                    wait(pe, z_done, t.n - 1)
                    gate(ps_z[t.slot], 1, t, z_made)
                if t := tile_at(2):
                    wait(pe, h_done, t.n + 1)
                    wait(pe, out_done, t.n)
                    for j in range(J):
                        last = nc.tensor.transpose(ps_out[:, j * D:(j + 1) * D],
                                                   hn[:, t.slot, j * P:(j + 1) * P], g["ident"][:, :])
                    last.then_inc(h_turned, 1)
                if t := tile_at(1):
                    wait(pe, n2_done, t.n)
                    gate(ps_ni, 2, t, ni_made, hidden=False)
            over_tiles(pe, NT, 2, step)

        @block.vector
        def _(dve):
            dve.wait_ge(w_loaded, 16 * 5)
            nc.vector.tensor_tensor(b_rz[:, :], b_ih[:, 0:2], b_hh[:, 0:2], ALU.add).then_inc(b_made, 1)
            dve.wait_ge(w_made, 1)
            nc.vector.tensor_copy(win[:, :], ps_s[:, 0:3 * D]).then_inc(w_copied, 1)

            def step(tile_at):
                if t := tile_at(2):
                    wait(dve, n_done, t.n + 1)
                    nc.vector.tensor_tensor(d1[:, t.slot, :], ht[:, t.slot4, :], n3[:, t.slot, :],
                                            ALU.subtract).then_inc(d1_done, 1)
                    wait(dve, z_done, t.n + 1)
                    wait(dve, d1_done, t.n + 1)
                    nc.vector.tensor_tensor(d2[:, t.slot, :], d1[:, t.slot, :], z[:, t.slot, :],
                                            ALU.mult).then_inc(d2_done, 1)
                    wait(dve, d2_done, t.n + 1)
                    wait(dve, h_turned, t.n - 1)
                    if not final:
                        wait(dve, ht_stored[t.slot], 16 * t.u)
                    nc.vector.tensor_tensor(hn[:, t.slot, :], d2[:, t.slot, :], n3[:, t.slot, :],
                                            ALU.add).then_inc(h_done, 1)
                if t := tile_at(1):
                    wait(dve, nh_made, t.n + 1)
                    wait(dve, r_done, t.n + 1)
                    nc.vector.scalar_tensor_tensor(n1[:, t.slot, :], ps_nh[:, :], b_hh[:, 2:3], r[:, t.slot, :],
                                                   ALU.add, ALU.mult).then_inc(n1_done, 1)
                if final and (t := tile_at(4)):
                    ln.shifts(nc, dve, t, y_done)
                if t := tile_at(2):
                    wait(dve, h_turned, t.n + 1)
                    if final:
                        wait(dve, x_loaded[t.slot4], 16 * (t.u4 + 1))
                        wait(dve, y_done, t.n - 3)
                        nc.vector.tensor_tensor(out[:, t.slot4, :, :].rearrange("p j d -> p (j d)"),
                                                ps_out[:, :], x[:, t.slot4, :, :].rearrange("p j d -> p (j d)"),
                                                ALU.add).then_inc(out_done, 1)
                    else:
                        wait(dve, stored[t.slot], 16 * (t.u - 1))
                        nc.vector.tensor_copy(out[:, t.slot4, :, :].rearrange("p j d -> p (j d)"),
                                              ps_out[:, :]).then_inc(out_done, 1)
                if t := tile_at(1):
                    wait(dve, n1_done, t.n + 1)
                    wait(dve, ni_made, t.n + 1)
                    wait(dve, n_done, t.n - 1)
                    nc.vector.tensor_tensor(n2[:, t.slot, :], n1[:, t.slot, :], ps_ni[:, :],
                                            ALU.add).then_inc(n2_done, 1)
                if final and (t := tile_at(2)):
                    wait(dve, out_done, t.n + 1)
                    ln.statistics(nc, dve, t, [out[:, t.slot4, j, :] for j in range(J)], ln.shift_done)
            over_tiles(dve, NT, 4 if final else 2, step)

        @block.scalar
        def _(act):
            act.wait_ge(b_made, 1)

            def step(tile_at):
                if t := tile_at(0):
                    wait(act, s_turned, t.n + 1)
                    wait(act, ni_made, t.n - 1)
                    nc.scalar.activation(st[:, t.slot, :], ps_s[:, :], ACT.Copy).then_inc(s_copied, 1)
                if t := tile_at(1):
                    wait(act, r_made, t.n + 1)
                    wait(act, n1_done, t.n - 1)
                    nc.scalar.activation(r[:, t.slot, :], ps_r[t.slot][:, :], ACT.Sigmoid,
                                         bias=b_rz[:, 0:1]).then_inc(r_done, 1)
                if final and (t := tile_at(5)):
                    wait(act, stored[t.slot], 16 * t.u)
                    ln.apply(nc, act, t, [out[:, t.slot4, j, :] for j in range(J)],
                             [y[:, t.slot, j, :] for j in range(J)], y_done)
                if not final and (t := tile_at(2)):
                    wait(act, h_done, t.n + 1)
                    act.dma_start(fm_tile(ht_out, t), hn[:, t.slot, :]).then_inc(ht_stored[t.slot], 16)
                if t := tile_at(1):
                    wait(act, z_made, t.n + 1)
                    wait(act, d2_done, t.n - 1)
                    nc.scalar.activation(z[:, t.slot, :], ps_z[t.slot][:, :], ACT.Sigmoid,
                                         bias=b_rz[:, 1:2]).then_inc(z_done, 1)
                if not final and (t := tile_at(2)):
                    wait(act, out_done, t.n + 1)
                    act.dma_start(nm_tile(h_out, t), out[:, t.slot4, :, :].rearrange("p j d -> p (j d)")
                                  ).then_inc(stored[t.slot], 16)
                if t := tile_at(1):
                    wait(act, n2_done, t.n + 1)
                    wait(act, h_done, t.n - 1)
                    nc.scalar.activation(n3[:, t.slot, :], n2[:, t.slot, :], ACT.Tanh,
                                         bias=b_ih[:, 2:3]).then_inc(n_done, 1)
                if final and (t := tile_at(5)):
                    wait(act, y_done, t.n + 1)
                    act.dma_start(nm_tile(x_out, t), y[:, t.slot, :, :].rearrange("p j d -> p (j d)")
                                  ).then_inc(stored[t.slot], 16)
            over_tiles(act, NT, 5 if final else 2, step)
            for b in range(2):
                act.wait_ge(stored[b], 16 * (NT // 2))
                if not final:
                    act.wait_ge(ht_stored[b], 16 * (NT // 2))


class LayerNormBuffers:

    def __init__(self, f, name):
        self.stats = f.sb(f"{name}_stats", [P, 2, J, 6])
        self.mv = f.sb(f"{name}_mv", [P, 2, J, 2])
        self.var = f.sb(f"{name}_var", [P, 2, J])
        self.inv = f.sb(f"{name}_inv", [P, 2, J])
        self.shift = f.sb(f"{name}_shift", [P, 2, J])
        self.power = f.sb(f"{name}_power", [P, J])
        self.power_set = f.sem(f"{name}_power_set")
        self.std = f.sb(f"{name}_std", [P, 2, J])
        self.stats_done, self.mv_done, self.var_done, self.std_done, self.inv_done, self.shift_done = (
            f.sem(f"{name}_{s}") for s in ("stats_done", "mv_done", "var_done", "std_done", "inv_done", "shift_done"))

    def statistics(self, nc, dve, t, parts, used):
        wait(dve, used, t.n - 1)
        for j, part in enumerate(parts):
            last = nc.vector.bn_stats(self.stats[:, t.slot, j, :], part)
        last.then_inc(self.stats_done, 1)
        wait_alone(dve, self.stats_done, t.n + 1)
        for j in range(J):
            last = nc.vector.bn_aggr(self.mv[:, t.slot, j, :], self.stats[:, t.slot, j, :])
        last.then_inc(self.mv_done, 1)
        wait(dve, self.mv_done, t.n + 1)
        wait(dve, self.inv_done, t.n - 1)
        nc.vector.tensor_scalar(self.var[:, t.slot, :], self.mv[:, t.slot, :, 1], EPS, None,
                                ALU.add).then_inc(self.var_done, 1)

    def root(self, nc, act, t):
        wait(act, self.var_done, t.n + 1)
        nc.scalar.activation(self.std[:, t.slot, :], self.var[:, t.slot, :], ACT.Sqrt).then_inc(self.std_done, 1)

    def invert(self, nc, dve, t):
        wait(dve, self.std_done, t.n + 1)
        nc.vector.reciprocal(self.inv[:, t.slot, :], self.std[:, t.slot, :]).then_inc(self.inv_done, 1)

    def rstd(self, nc, pool, t, applied):
        if isinstance(t.n, int) and t.n == 0:
            pool.wait_ge(self.power_set, 1)
        wait(pool, self.var_done, t.n + 1)
        wait(pool, applied, t.n - 1)
        nc.gpsimd.tensor_tensor(self.inv[:, t.slot, :], self.var[:, t.slot, :], self.power[:, :],
                                ALU.pow).then_inc(self.inv_done, 1)

    def shifts(self, nc, dve, t, applied):
        wait(dve, applied, t.n - 1)
        wait(dve, self.inv_done, t.n + 1)
        nc.vector.scalar_tensor_tensor(self.shift[:, t.slot, :], self.mv[:, t.slot, :, 0], -1.0,
                                       self.inv[:, t.slot, :], ALU.mult, ALU.mult).then_inc(self.shift_done, 1)

    def apply(self, nc, act, t, parts, outs, applied):
        wait(act, self.shift_done, t.n + 1)
        for j, (part, out) in enumerate(zip(parts, outs)):
            last = nc.scalar.activation(out, part, ACT.Identity, bias=self.shift[:, t.slot, j:j + 1],
                                        scale=self.inv[:, t.slot, j:j + 1])
        last.then_inc(applied, 1)


def mean_pass(nc, name, g, x_in, ptr, inv_count, w_x, x_out, normed, h_out=None, ht_out=None):
    with ExitStack() as ctx:
        f = Phase(nc, ctx, name)
        w = f.sb("w", [P, D])
        idx = f.sb("idx", [P, 4, J], I32)
        inv_n = f.sb("inv_n", [P, 4, J])
        rows = f.sb("rows", [P, 4, J, D])
        x = f.sb("x", [P, 4, J, D])
        xt = f.sb("xt", [P, 2, SUPER])
        v = f.sb("v", [P, 2, J, D])
        res = f.sb("res", [P, 2, J, D])
        y = f.sb("y", [P, 2, J, D])
        ln = LayerNormBuffers(f, "ln")
        ps_x, ps_v = f.ps("ps_x"), [f.ps(f"ps_v{b}") for b in range(2)]
        w_loaded = f.sem("w_loaded")
        idx_loaded, inv_loaded, x_loaded, gathered = (
            f.sems(s, 4) for s in ("idx_loaded", "inv_loaded", "x_loaded", "gathered"))
        stored = f.sems("stored")
        x_turned, xt_done, product_made, v_done, res_done, y_done = (
            f.sem(s) for s in ("x_turned", "xt_done", "product_made", "v_done", "res_done", "y_done"))
        if normed:
            squares = f.sb("squares", [P, 2, J, D])
            length2 = f.sb("length2", [P, 2, J])
            inv_len = f.sb("inv_len", [P, 2, J])
            length = f.sb("length", [P, 2, J])
            length2_done, length_done, inv_len_done = (
                f.sem(s) for s in ("length2_done", "length_done", "inv_len_done"))
        if h_out is not None:
            lin = f.sb("lin", [P, D])
            lin_b = f.sb("lin_b", [P, 1])
            yt = f.sb("yt", [P, 2, SUPER])
            ht = f.sb("ht", [P, 2, SUPER])
            h = f.sb("h", [P, 2, SUPER])
            ps_y, ps_ht, ps_h = f.ps("ps_y"), f.ps("ps_ht"), f.ps("ps_h")
            ht_stored, h_stored = f.sems("ht_stored"), f.sems("h_stored")
            y_turned, yt_done, ht_made, ht_done, h_turned, h_done = (
                f.sem(s) for s in ("y_turned", "yt_done", "ht_made", "ht_done", "h_turned", "h_done"))
        block = ctx.enter_context(nc.Block())

        last_lag = 7 if h_out is not None else 5

        @block.sync
        def _(sp):
            sp.dma_start(w[:, :], w_x).then_inc(w_loaded, 16)
            if h_out is not None:
                sp.dma_start(lin[:, :], g["lin_wt"]).then_inc(w_loaded, 16)
                sp.dma_start(lin_b[:, :], column(g["lin_b"])).then_inc(w_loaded, 16)

            def step(tile_at):
                if t := tile_at(0):
                    wait_alone(sp, gathered[t.slot4], 64 * t.u4)
                    sp.dma_start(idx[:, t.slot4, :], list_tile(ptr, t)).then_inc(idx_loaded[t.slot4], 16)
                    wait_alone(sp, v_done, t.n - 3)
                    sp.dma_start(inv_n[:, t.slot4, :], list_tile(inv_count, t)).then_inc(inv_loaded[t.slot4], 16)
                    wait_alone(sp, x_turned, t.n - 3)
                    wait_alone(sp, res_done, t.n - 3)
                    sp.dma_start(flat(x[:, t.slot4, :, :]), nm_tile(x_in, t)).then_inc(x_loaded[t.slot4], 16)
            over_tiles(sp, NT, 0, step)

        @block.gpsimd
        def _(pool):
            def step(tile_at):
                if t := tile_at(0):
                    gather_step(nc, pool, t, idx, rows, g["sums"], idx_loaded, v_done, gathered)
            over_tiles(pool, NT, 0, step)

        @block.tensor
        def _(pe):
            pe.wait_ge(w_loaded, 16 * (3 if h_out is not None else 1))

            def step(tile_at):
                if t := tile_at(1):
                    wait(pe, xt_done, t.n + 1)
                    wait(pe, v_done, t.n - 1)
                    for j in range(J):
                        last = nc.tensor.matmul(ps_v[t.slot][:, j * D:(j + 1) * D], xt[:, t.slot, j * P:(j + 1) * P],
                                                w[:, :], start=True, stop=True)
                    last.then_inc(product_made, 1)
                if h_out is not None and (t := tile_at(7)):
                    wait(pe, ht_done, t.n + 1)
                    wait(pe, h_done, t.n)
                    for j in range(J):
                        last = nc.tensor.transpose(ps_h[:, j * D:(j + 1) * D], ht[:, t.slot, j * P:(j + 1) * P],
                                                   g["ident"][:, :])
                    last.then_inc(h_turned, 1)
                if h_out is not None and (t := tile_at(6)):
                    wait(pe, yt_done, t.n + 1)
                    wait(pe, ht_done, t.n)
                    nc.tensor.matmul(ps_ht[:, :], lin[:, :], yt[:, t.slot, :], start=True,
                                     stop=True).then_inc(ht_made, 1)
                if t := tile_at(0):
                    wait(pe, x_loaded[t.slot4], 16 * (t.u4 + 1))
                    wait(pe, xt_done, t.n)
                    for j in range(J):
                        last = nc.tensor.transpose(ps_x[:, j * P:(j + 1) * P], x[:, t.slot4, j, :], g["ident"][:, :])
                    last.then_inc(x_turned, 1)
                if h_out is not None and (t := tile_at(5)):
                    wait(pe, y_done, t.n + 1)
                    wait(pe, yt_done, t.n)
                    for j in range(J):
                        last = nc.tensor.transpose(ps_y[:, j * P:(j + 1) * P], y[:, t.slot, j, :], g["ident"][:, :])
                    last.then_inc(y_turned, 1)
            over_tiles(pe, NT, last_lag, step)

        @block.vector
        def _(dve):
            def step(tile_at):
                if t := tile_at(3):
                    if normed:
                        wait(dve, length_done, t.n + 1)
                        nc.vector.reciprocal(inv_len[:, t.slot, :], length[:, t.slot, :]).then_inc(inv_len_done, 1)
                        wait_alone(dve, inv_len_done, t.n + 1)
                    wait(dve, y_done, t.n - 1)
                    wait(dve, v_done, t.n + 1)
                    if normed:
                        for j in range(J):
                            last = nc.vector.scalar_tensor_tensor(
                                res[:, t.slot, j, :], v[:, t.slot, j, :], inv_len[:, t.slot, j:j + 1],
                                x[:, t.slot4, j, :], ALU.mult, ALU.add)
                    else:
                        last = nc.vector.tensor_tensor(flat(res[:, t.slot, :, :]), flat(v[:, t.slot, :, :]),
                                                       flat(x[:, t.slot4, :, :]), ALU.add)
                    last.then_inc(res_done, 1)
                if t := tile_at(4):
                    ln.invert(nc, dve, t)
                    ln.shifts(nc, dve, t, y_done)
                if t := tile_at(3):
                    wait(dve, res_done, t.n + 1)
                    ln.statistics(nc, dve, t, [res[:, t.slot, j, :] for j in range(J)], y_done)
                if t := tile_at(1):
                    wait(dve, gathered[t.slot4], 64 * (t.u4 + 1))
                    wait(dve, inv_loaded[t.slot4], 16 * (t.u4 + 1))
                    wait(dve, product_made, t.n + 1)
                    wait(dve, res_done, t.n - 1)
                    if normed:
                        wait(dve, length2_done, t.n - 1)
                    for j in range(J):
                        last = nc.vector.scalar_tensor_tensor(
                            v[:, t.slot, j, :], rows[:, t.slot4, j, :], inv_n[:, t.slot4, j:j + 1],
                            ps_v[t.slot][:, j * D:(j + 1) * D], ALU.mult, ALU.add)
                    last.then_inc(v_done, 1)
                if h_out is not None and (t := tile_at(7)):
                    wait(dve, h_turned, t.n + 1)
                    wait(dve, h_stored[t.slot], 16 * t.u)
                    nc.vector.tensor_copy(h[:, t.slot, :], ps_h[:, :]).then_inc(h_done, 1)
            over_tiles(dve, NT, last_lag, step)

        @block.scalar
        def _(act):
            act.wait_ge(w_loaded, 16 * (3 if h_out is not None else 1))

            def step(tile_at):
                if h_out is not None and (t := tile_at(8)):
                    wait(act, h_done, t.n + 1)
                    act.dma_start(nm_tile(h_out, t), h[:, t.slot, :]).then_inc(h_stored[t.slot], 16)
                if h_out is not None and (t := tile_at(7)):
                    wait(act, ht_done, t.n + 1)
                    act.dma_start(fm_tile(ht_out, t), ht[:, t.slot, :]).then_inc(ht_stored[t.slot], 16)
                if normed and (t := tile_at(2)):
                    wait(act, v_done, t.n + 1)
                    wait(act, length_done, t.n - 1)
                    for j in range(J):
                        last = nc.scalar.activation(squares[:, t.slot, j, :], v[:, t.slot, j, :], ACT.Square,
                                                    accum_out=length2[:, t.slot, j:j + 1])
                    last.then_inc(length2_done, 1)
                    wait(act, length2_done, t.n + 1)
                    wait(act, inv_len_done, t.n - 1)
                    nc.scalar.activation(length[:, t.slot, :], length2[:, t.slot, :], ACT.Sqrt
                                         ).then_inc(length_done, 1)
                if h_out is not None and (t := tile_at(6)):
                    wait(act, ht_made, t.n + 1)
                    wait(act, ht_stored[t.slot], 16 * t.u)
                    wait(act, h_turned, t.n - 1)
                    nc.scalar.activation(ht[:, t.slot, :], ps_ht[:, :], ACT.Identity,
                                         bias=lin_b[:, :]).then_inc(ht_done, 1)
                if t := tile_at(0):
                    wait(act, x_turned, t.n + 1)
                    wait(act, product_made, t.n - 1)
                    nc.scalar.activation(xt[:, t.slot, :], ps_x[:, :], ACT.Copy).then_inc(xt_done, 1)
                if t := tile_at(4):
                    wait(act, stored[t.slot], 16 * t.u)
                    if h_out is not None:
                        wait(act, y_turned, t.n - 1)
                    ln.apply(nc, act, t, [res[:, t.slot, j, :] for j in range(J)],
                             [y[:, t.slot, j, :] for j in range(J)], y_done)
                if h_out is not None and (t := tile_at(5)):
                    wait(act, y_turned, t.n + 1)
                    wait(act, ht_made, t.n - 1)
                    nc.scalar.activation(yt[:, t.slot, :], ps_y[:, :], ACT.Copy).then_inc(yt_done, 1)
                if t := tile_at(5):
                    wait(act, y_done, t.n + 1)
                    act.dma_start(nm_tile(x_out, t), flat(y[:, t.slot, :, :])).then_inc(stored[t.slot], 16)
                if t := tile_at(3):
                    ln.root(nc, act, t)
            over_tiles(act, NT, 8 if h_out is not None else 5, step)
            for b in range(2):
                act.wait_ge(stored[b], 16 * (NT // 2))
                if h_out is not None:
                    act.wait_ge(ht_stored[b], 16 * (NT // 2))
                    act.wait_ge(h_stored[b], 16 * (NT // 2))


def attention_pass(nc, name, g):
    with ExitStack() as ctx:
        f = Phase(nc, ctx, name)
        qw, kw, vw, ow = (f.sb(s, [P, D]) for s in ("qw", "kw", "vw", "ow"))
        qb, kb, vb, eb = (f.sb(s, [P, 1]) for s in ("qb", "kb", "vb", "eb"))
        ew = f.sb("ew", [EDIM, HEADS])
        ew_rows = f.sb("ew_rows", [EDIM, HEADS, HEAD_DIM])
        eb_row = f.sb("eb_row", [1, HEADS])
        ones = f.sb("ones", [1, 1])
        eb_wide = f.sb("eb_wide", [1, HEADS, HEAD_DIM])
        ob = f.sb("ob", [P, D])
        blocks = f.sb("blocks", [P, HEADS, HEAD_DIM])
        heads = f.sb("heads", [P, HEADS])
        idx = f.sb("idx", [P, 4, J, 2], I32)
        send = f.sb("send", [P, 4, J, D])
        recv = f.sb("recv", [P, 4, J, D])
        edge_t = f.sb("edge_t", [EDIM, 4, SUPER])
        cut = f.sb("cut", [P, 4, SUPER], BF16)
        send_t, recv_t, q, qk, s = (f.sb(n, [P, 2, SUPER]) for n in ("send_t", "recv_t", "q", "qk", "s"))
        v = f.sb("v", [P, 4, SUPER])
        top = f.sb("top", [P, 2, SUPER + 1])
        drop = f.sb("drop", [P, 2, SUPER])
        arg = f.sb("arg", [P, 2, 2, SUPER])
        ex = f.sb("ex", [P, 2, 2, SUPER])
        pv, den, att = (f.sb(n, [P, 2, SUPER]) for n in ("pv", "den", "att"))
        num = f.sb("num", [P, 4, SUPER])
        den_max = f.sb("den_max", [P, 2, J, HEADS])
        den_inv = f.sb("den_inv", [P, 2, J, HEADS])
        inv_wide = f.sb("inv_wide", [P, 2, J, HEADS, HEAD_DIM])
        out = f.sb("out", [P, 2, SUPER])
        ps_send, ps_recv, ps_q, ps_k, ps_v, ps_s, ps_inv, ps_out = (
            f.ps(n) for n in ("ps_send", "ps_recv", "ps_q", "ps_k", "ps_v", "ps_s", "ps_inv", "ps_out"))
        w_loaded, consts_set, eb_made, eb_done, ew_done = (
            f.sem(n) for n in ("w_loaded", "consts_set", "eb_made", "eb_done", "ew_done"))
        idx_loaded, edge_loaded, cut_loaded, sent, received = (
            f.sems(n, 4) for n in ("idx_loaded", "edge_loaded", "cut_loaded", "sent", "received"))
        stored = f.sems("stored")
        (rows_turned, send_done, recv_done, q_made, k_made, v_made, q_done, v_done, qk_done, s_made, s_done,
         carry_done, top_done, arg0_done, drop_done, arg_done, ex_done, pv_done, den_done, num_done,
         den_made, max_done, inv_done, wide_done, inv_turned, att_done, out_made, out_done) = (
            f.sem(n) for n in ("rows_turned", "send_done", "recv_done", "q_made", "k_made", "v_made", "q_done",
                               "v_done", "qk_done", "s_made", "s_done", "carry_done", "top_done", "arg0_done",
                               "drop_done", "arg_done", "ex_done", "pv_done", "den_done", "num_done", "den_made",
                               "max_done", "inv_done", "wide_done", "inv_turned", "att_done", "out_made",
                               "out_done"))
        loads = 12
        block = ctx.enter_context(nc.Block())

        @block.sync
        def _(sp):
            for dst_, src_ in ((qw[:, :], g["qW"]), (kw[:, :], g["kW"]), (vw[:, :], g["vW"]), (ow[:, :], g["oW"]),
                               (qb[:, :], column(g["qb"])), (kb[:, :], column(g["kb"])), (vb[:, :], column(g["vb"])),
                               (ew[:, :], g["eW"]), (ob[:, :], on_all(g["ob"])),
                               (eb_row[:, :], g["eb"].rearrange("(a n) -> a n", a=1)),
                               (blocks[:, :, :], g["blocks_c"]), (heads[:, :], g["heads_c"])):
                sp.dma_start(dst_, src_, allow_slow_non_contiguous=True).then_inc(w_loaded, 16)

            def step(tile_at):
                if t := tile_at(0):
                    wait_alone(sp, sent[t.slot4], 64 * t.u4)
                    wait_alone(sp, received[t.slot4], 64 * t.u4)
                    sp.dma_start(idx[:, t.slot4, :, :].rearrange("p j c -> p (j c)"),
                                 nm_tile(g["by_dst"], t)).then_inc(idx_loaded[t.slot4], 16)
                if t := tile_at(1):
                    wait_alone(sp, s_made, t.n - 3)
                    sp.dma_start(edge_t[:, t.slot4, :], g["edge_attr_t"][:, bass.ds(t.n * SUPER, SUPER)]
                                 ).then_inc(edge_loaded[t.slot4], 16)
                if t := tile_at(2):
                    wait_alone(sp, drop_done, t.n - 3)
                    wait_alone(sp, top_done, t.n - 3)
                    sp.dma_start(cut[:, t.slot4, :], row_tile(g["cut_dst"], t)).then_inc(cut_loaded[t.slot4], 16)
            over_tiles(sp, ET, 2, step)

        @block.gpsimd
        def _(pool):
            def step(tile_at):
                if t := tile_at(0):
                    wait(pool, idx_loaded[t.slot4], 16 * (t.u4 + 1))
                    wait(pool, rows_turned, t.n - 3)
                    pool.nop(nofuse=True)
                    for j in range(J):
                        for col, rows, sem in ((1, send, sent), (0, recv, received)):
                            nc.gpsimd.indirect_dma_start(
                                out=rows[:, t.slot4, j, :], out_offset=None, in_=g["x_in"][:, :],
                                in_offset=bass.IndirectOffsetOnAxis(ap=idx[:, t.slot4, j, col:col + 1], axis=0)).then_inc(sem[t.slot4], 16)
            over_tiles(pool, ET, 0, step)

        @block.tensor
        def _(pe):
            pe.wait_ge(w_loaded, 16 * loads)
            pe.wait_ge(eb_done, 1)
            nc.tensor.matmul(ps_s[:, 0:1], eb_wide[:, :, :].rearrange("a h d -> a (h d)"), ones[:, :],
                             start=True, stop=True).then_inc(eb_made, 1)
            pe.wait_ge(eb_done, 2)
            pe.wait_ge(ew_done, 1)

            def step(tile_at):
                if t := tile_at(1):
                    wait(pe, send_done, t.n + 1)
                    wait(pe, q_done, t.n)
                    nc.tensor.matmul(ps_q[:, :], qw[:, :], send_t[:, t.slot, :], start=True,
                                     stop=True).then_inc(q_made, 1)
                    wait(pe, recv_done, t.n + 1)
                    wait(pe, qk_done, t.n)
                    nc.tensor.matmul(ps_k[:, :], kw[:, :], recv_t[:, t.slot, :], start=True,
                                     stop=True).then_inc(k_made, 1)
                    wait(pe, v_done, t.n)
                    nc.tensor.matmul(ps_v[:, :], vw[:, :], send_t[:, t.slot, :], start=True,
                                     stop=True).then_inc(v_made, 1)
                if t := tile_at(6):
                    wait(pe, wide_done, t.n + 1)
                    wait(pe, max_done, min(t.n + 2, ET) if isinstance(t.n, int) else t.n + 2)
                    for j in range(J):
                        last = nc.tensor.transpose(edge_columns(ps_inv[:, :])[:, j, :],
                                                   inv_wide[:, t.slot, j, :, :].rearrange("p h d -> p (h d)"),
                                                   g["ident"][:, :])
                    last.then_inc(inv_turned, 1)
                if t := tile_at(2):
                    wait(pe, qk_done, t.n + 1)
                    wait(pe, edge_loaded[t.slot4], 16 * (t.u4 + 1))
                    wait(pe, s_done, t.n)
                    nc.tensor.matmul(ps_s[:, :], blocks[:, :, :].rearrange("p h d -> p (h d)"), qk[:, t.slot, :],
                                     start=True, stop=False)
                    nc.tensor.matmul(ps_s[:, :], ew_rows[:, :, :].rearrange("p h d -> p (h d)"),
                                     edge_t[:, t.slot4, :], start=False, stop=True).then_inc(s_made, 1)
                if t := tile_at(0):
                    wait(pe, sent[t.slot4], 64 * (t.u4 + 1))
                    wait(pe, send_done, t.n)
                    for j in range(J):
                        nc.tensor.transpose(edge_columns(ps_send[:, :])[:, j, :], send[:, t.slot4, j, :], g["ident"][:, :])
                    wait(pe, received[t.slot4], 64 * (t.u4 + 1))
                    wait(pe, recv_done, t.n)
                    for j in range(J):
                        last = nc.tensor.transpose(edge_columns(ps_recv[:, :])[:, j, :], recv[:, t.slot4, j, :],
                                                   g["ident"][:, :])
                    last.then_inc(rows_turned, 1)
                if t := tile_at(6):
                    wait(pe, att_done, t.n + 1)
                    wait(pe, out_done, t.n)
                    for j in range(J):
                        last = nc.tensor.matmul(ps_out[:, j * D:(j + 1) * D], edge_columns(att[:, t.slot, :])[:, j, :],
                                                ow[:, :], start=True, stop=True)
                    last.then_inc(out_made, 1)
                if t := tile_at(4):
                    wait(pe, den_done, t.n + 1)
                    wait(pe, att_done, t.n - 1)
                    wait(pe, max_done, t.n)
                    for j in range(J):
                        last = nc.tensor.matmul(ps_inv[:, j * HEADS:(j + 1) * HEADS],
                                                edge_columns(den[:, t.slot, :])[:, j, :], heads[:, :],
                                                start=True, stop=True)
                    last.then_inc(den_made, 1)
            over_tiles(pe, ET, 6, step)

        @block.vector
        def _(dve):
            dve.wait_ge(w_loaded, 16 * loads)
            nc.vector.memset(ones[:, :], 1.0).then_inc(consts_set, 1)
            dve.wait_ge(consts_set, 1)
            nc.vector.tensor_copy(eb_wide[:, :, :], eb_row[:, :].unsqueeze(2).broadcast_to([1, HEADS, HEAD_DIM])
                                  ).then_inc(eb_done, 1)
            nc.vector.tensor_copy(ew_rows[:, :, :], ew[:, :].unsqueeze(2).broadcast_to([EDIM, HEADS, HEAD_DIM])
                                  ).then_inc(ew_done, 1)
            dve.wait_ge(eb_made, 1)
            nc.vector.tensor_copy(eb[:, :], ps_s[:, 0:1]).then_inc(eb_done, 1)

            def step(tile_at):
                if t := tile_at(5):
                    wait(dve, den_made, t.n + 1)
                    nc.vector.tensor_scalar(den_max[:, t.slot, :, :].rearrange("p j h -> p (j h)"),
                                            ps_inv[:, 0:J * HEADS], 1e-8, None, ALU.max).then_inc(max_done, 1)
                    wait(dve, max_done, t.n + 1)
                    wait(dve, wide_done, t.n - 1)
                    nc.vector.reciprocal(den_inv[:, t.slot, :, :].rearrange("p j h -> p (j h)"),
                                         den_max[:, t.slot, :, :].rearrange("p j h -> p (j h)")).then_inc(inv_done, 1)
                if t := tile_at(3):
                    wait(dve, top_done, t.n)
                    wait(dve, arg_done, t.n - 1)
                    prev = top[:, 1 - t.slot, SUPER:SUPER + 1]
                    first = isinstance(t.n, int) and t.n == 0
                    if first:
                        nc.vector.memset(top[:, 0, 0:1], 0.0).then_inc(carry_done, 1)
                    else:
                        nc.vector.tensor_copy(top[:, t.slot, 0:1], prev).then_inc(carry_done, 1)
                    wait(dve, carry_done, t.n + 1)
                    wait(dve, cut_loaded[t.slot4], 16 * (t.u4 + 1))
                    wait(dve, s_done, t.n + 1)
                    nc.vector.tensor_tensor_scan(top[:, t.slot, 1:SUPER + 1], cut[:, t.slot4, :], s[:, t.slot, :],
                                                 top[:, t.slot, 0:1], ALU.add, ALU.max).then_inc(top_done, 1)
                    wait(dve, top_done, t.n + 1)
                    wait(dve, ex_done, t.n - 1)
                    nc.vector.tensor_tensor(arg[:, t.slot, 0, :], s[:, t.slot, :], top[:, t.slot, 1:SUPER + 1],
                                            ALU.subtract).then_inc(arg0_done, 1)
                    nc.vector.tensor_tensor(drop[:, t.slot, :], top[:, t.slot, 0:SUPER], cut[:, t.slot4, :],
                                            ALU.add).then_inc(drop_done, 1)
                    wait(dve, drop_done, t.n + 1)
                    nc.vector.tensor_tensor(arg[:, t.slot, 1, :], drop[:, t.slot, :], top[:, t.slot, 1:SUPER + 1],
                                            ALU.subtract).then_inc(arg_done, 1)
                if t := tile_at(1):
                    wait(dve, k_made, t.n + 1)
                    wait(dve, q_done, t.n + 1)
                    wait(dve, s_made, t.n - 1)
                    nc.vector.scalar_tensor_tensor(qk[:, t.slot, :], ps_k[:, :], kb[:, :], q[:, t.slot, :],
                                                   ALU.add, ALU.mult).then_inc(qk_done, 1)
                if t := tile_at(6):
                    wait(dve, inv_turned, t.n + 1)
                    wait(dve, out_made, t.n - 1)
                    nc.vector.tensor_tensor(att[:, t.slot, :], num[:, t.slot4, :], ps_inv[:, :],
                                            ALU.mult).then_inc(att_done, 1)
                if t := tile_at(3):
                    wait(dve, ex_done, t.n + 1)
                    wait(dve, v_done, t.n + 1)
                    nc.vector.tensor_tensor(pv[:, t.slot, :], v[:, t.slot4, :], ex[:, t.slot, 0, :],
                                            ALU.mult).then_inc(pv_done, 1)
                    first = isinstance(t.n, int) and t.n == 0
                    wait(dve, den_made, t.n - 1)
                    wait(dve, den_done, t.n)
                    nc.vector.tensor_tensor_scan(
                        den[:, t.slot, :], ex[:, t.slot, 1, :], ex[:, t.slot, 0, :],
                        0.0 if first else den[:, 1 - t.slot, SUPER - 1:SUPER],
                        ALU.mult, ALU.add).then_inc(den_done, 1)
                    wait(dve, pv_done, t.n + 1)
                    wait(dve, num_done, t.n)
                    wait(dve, att_done, t.n - 3)
                    nc.vector.tensor_tensor_scan(
                        num[:, t.slot4, :], ex[:, t.slot, 1, :], pv[:, t.slot, :],
                        0.0 if first else num[:, (t.slot4 - 1) % 4, SUPER - 1:SUPER],
                        ALU.mult, ALU.add).then_inc(num_done, 1)
                if t := tile_at(6):
                    wait(dve, out_made, t.n + 1)
                    wait(dve, stored[t.slot], 16 * t.u)
                    nc.vector.tensor_tensor(
                        out[:, t.slot, :].rearrange("p (j d) -> p j d", j=J),
                        ps_out[:, :].rearrange("p (j d) -> p j d", j=J),
                        ob[:, :].unsqueeze(1).broadcast_to([P, J, D]), ALU.add).then_inc(out_done, 1)
            over_tiles(dve, ET, 6, step)

        @block.scalar
        def _(act):
            act.wait_ge(w_loaded, 16 * loads)
            act.wait_ge(eb_done, 2)

            def step(tile_at):
                if t := tile_at(1):
                    wait(act, q_made, t.n + 1)
                    wait(act, qk_done, t.n - 1)
                    nc.scalar.activation(q[:, t.slot, :], ps_q[:, :], ACT.Identity, bias=qb[:, :]).then_inc(q_done, 1)
                    wait(act, v_made, t.n + 1)
                    wait(act, pv_done, t.n - 3)
                    nc.scalar.activation(v[:, t.slot4, :], ps_v[:, :], ACT.Identity, bias=vb[:, :]).then_inc(v_done, 1)
                if t := tile_at(5):
                    wait(act, inv_done, t.n + 1)
                    wait(act, inv_turned, t.n - 1)
                    nc.scalar.activation(
                        inv_wide[:, t.slot, :, :, :].rearrange("p j h d -> p (j h) d"),
                        den_inv[:, t.slot, :, :].rearrange("p j h -> p (j h)").unsqueeze(2).broadcast_to(
                            [P, J * HEADS, HEAD_DIM]), ACT.Copy).then_inc(wide_done, 1)
                if t := tile_at(3):
                    wait(act, arg0_done, t.n + 1)
                    wait(act, arg_done, t.n + 1)
                    wait(act, num_done, t.n - 1)
                    nc.scalar.activation(ex[:, t.slot, :, :].rearrange("p a n -> p (a n)"),
                                         arg[:, t.slot, :, :].rearrange("p a n -> p (a n)"), ACT.Exp
                                         ).then_inc(ex_done, 1)
                if t := tile_at(2):
                    wait(act, s_made, t.n + 1)
                    wait(act, arg0_done, t.n - 1)
                    nc.scalar.activation(s[:, t.slot, :], ps_s[:, :], ACT.Identity, bias=eb[:, :]).then_inc(s_done, 1)
                if t := tile_at(0):
                    wait(act, rows_turned, t.n + 1)
                    wait(act, v_made, t.n - 1)
                    nc.scalar.activation(send_t[:, t.slot, :], ps_send[:, :], ACT.Copy).then_inc(send_done, 1)
                    nc.scalar.activation(recv_t[:, t.slot, :], ps_recv[:, :], ACT.Copy).then_inc(recv_done, 1)
                if t := tile_at(7):
                    wait(act, out_done, t.n + 1)
                    act.dma_start(nm_tile(g["att_sums"], t), out[:, t.slot, :]).then_inc(stored[t.slot], 16)
            over_tiles(act, ET, 7, step)
            for b in range(2):
                act.wait_ge(stored[b], 16 * (ET // 2))


ROOTS = {"hidden": 5, "ln1": 3, "ln2": 8, "ln3": 9}
FIRST_ROOT, LAST_ROOT = min(ROOTS.values()), max(ROOTS.values())


def ffn_pass(nc, name, g):
    with ExitStack() as ctx:
        f = Phase(nc, ctx, name)
        C = FFN // P
        f1, f1c = f.sb("f1", [P, FFN]), f.sb("f1c", [P, FFN])
        fb, fbc, rest1, rest2 = (f.sb(s, [P, FFN]) for s in ("fb", "fbc", "rest1", "rest2"))
        hi, mid, lo, bias_rows = (f.sb(s, [P, FFN], BF16) for s in ("hi", "mid", "lo", "bias_rows"))
        ones = f.sb("ones", [P, P], BF16)
        total, mean = f.sb("total", [P, 2]), f.sb("mean", [P, 2])
        f2 = f.sb("f2", [P, C, D])
        g1, b1, f2b = (f.sb(s, [P, 1]) for s in ("g1", "b1", "f2b"))
        gf, bf = f.sb("gf", [P, C]), f.sb("bf", [P, C])
        g2, b2 = f.sb("g2", [P, D]), f.sb("b2", [P, D])
        idx = f.sb("idx", [P, 4, J], I32)
        rows, x = f.sb("rows", [P, 4, J, D]), f.sb("x", [P, 4, J, D])
        xr, a, xh, u, xb, z, y = (f.sb(s, [P, 2, J, D]) for s in ("xr", "a", "xh", "u", "xb", "z", "y"))
        x1t, y2t = f.sb("x1t", [P, 4, SUPER]), f.sb("y2t", [P, 2, SUPER])
        squares = f.sb("squares", [P, J, FFN])
        sumsq, shift = f.sb("sumsq", [P, 2, J]), f.sb("shift", [P, 2, J])
        var, inv = (f.sb(s, [P, 2, len(ROOTS), J]) for s in ("var", "inv"))
        stats1, stats2, stats3 = (f.sb(s, [P, 2, J, 6]) for s in ("stats1", "stats2", "stats3"))
        mv1, mv2, mv3 = (f.sb(s, [P, 2, J, 2]) for s in ("mv1", "mv2", "mv3"))
        hs = f.sb("hs", [P, 2, J, FFN])
        hg = f.sb("hg", [P, C, SUPER])
        power = f.sb("power", [P, len(ROOTS) * J])
        ps_h = [f.ps(f"ps_h{j}") for j in range(J)]
        ps_g = [f.ps(f"ps_g{b}") for b in range(2)]
        ps_f, ps_t = f.ps("ps_f"), f.ps("ps_t")
        idx_loaded, x_loaded, gathered = (f.sems(s, 4) for s in ("idx_loaded", "x_loaded", "gathered"))
        xr_loaded, stored = f.sems("xr_loaded"), f.sems("stored")
        (w_loaded, ones_set, total_done, mean_done, centred, hi_done, rest1_done, mid_done, rest2_done,
         lo_done, rows_done) = (
            f.sem(s) for s in ("w_loaded", "ones_set", "total_done", "mean_done", "centred", "hi_done",
                               "rest1_done", "mid_done", "rest2_done", "lo_done", "rows_done"))
        (a_done, xh_done, xh_turned, x1t_done, h_made, sumsq_done, hs_done, g_turned, gelu_done, f2_made, y2t_done,
         y2_turned, u_done, xb_done, z_done, shift_done, y_done, roots_set, hidden_root_done,
         ln_roots_done) = (
            f.sem(s) for s in ("a_done", "xh_done", "xh_turned", "x1t_done", "h_made", "sumsq_done", "hs_done",
                               "g_turned", "gelu_done", "f2_made", "y2t_done", "y2_turned", "u_done", "xb_done",
                               "z_done", "shift_done", "y_done", "roots_set", "hidden_root_done", "ln_roots_done"))
        stats_done, mv_done, var_done = (
            {root: f.sem(f"{s}_{root}") for root in ROOTS} for s in ("stats_done", "mv_done", "var_done"))

        def root_slot(t, root):
            return (t.slot + ROOTS[root]) % 2

        def roots_of(t, root):
            return t.n + ROOTS[root] - FIRST_ROOT + 1

        loads = 11
        block = ctx.enter_context(nc.Block())

        @block.sync
        def _(sp):
            for dst_, src_ in ((f1[:, :], g["f1W"]), (fb[:, :], on_all(g["f1b"])),
                               (f2[:, :, :], g["f2W"].rearrange("(c p) d -> p c d", p=P)),
                               (g1[:, :], column(g["ln1_g"])), (b1[:, :], column(g["ln1_b"])), (f2b[:, :], column(g["f2b"])),
                               (gf[:, :], g["lnf_g"].rearrange("(c p) -> p c", p=P)),
                               (bf[:, :], g["lnf_b"].rearrange("(c p) -> p c", p=P)),
                               (g2[:, :], on_all(g["ln2_g"])), (b2[:, :], on_all(g["ln2_b"]))):
                sp.dma_start(dst_, src_, allow_slow_non_contiguous=True).then_inc(w_loaded, 16)

            def step(tile_at):
                if t := tile_at(0):
                    wait_alone(sp, gathered[t.slot4], 64 * t.u4)
                    sp.dma_start(idx[:, t.slot4, :], list_tile(g["ptr_dst"], t)).then_inc(idx_loaded[t.slot4], 16)
                    wait_alone(sp, a_done, t.n - 3)
                    sp.dma_start(flat(x[:, t.slot4, :, :]), nm_tile(g["x_in"], t)).then_inc(x_loaded[t.slot4], 16)
                if t := tile_at(6):
                    wait_alone(sp, xb_done, t.n - 1)
                    sp.dma_start(flat(xr[:, t.slot, :, :]), nm_tile(g["x_in"], t)).then_inc(xr_loaded[t.slot], 16)
            over_tiles(sp, NT, 6, step)

        @block.gpsimd
        def _(pool):
            nc.gpsimd.memset(power[:, :], -0.5).then_inc(roots_set, 1)
            nc.gpsimd.memset(var[:, :, :, :].rearrange("p b k j -> p (b k j)"), 1.0).then_inc(roots_set, 1)
            pool.wait_ge(roots_set, 2)
            pool.wait_ge(w_loaded, 16 * (loads - 1))
            used = {"ln1": xh_done, "ln2": z_done, "ln3": y_done}

            def step(tile_at):
                if t := tile_at(2):
                    wait(pool, gathered[t.slot4], 64 * (t.u4 + 1))
                    wait(pool, x_loaded[t.slot4], 16 * (t.u4 + 1))
                    wait(pool, xh_done, t.n - 1)
                    wait(pool, stats_done["ln1"], t.n - 1)
                    nc.gpsimd.tensor_tensor(flat(a[:, t.slot, :, :]), flat(rows[:, t.slot4, :, :]),
                                            flat(x[:, t.slot4, :, :]), ALU.add).then_inc(a_done, 1)
                if t := tile_at(ROOTS["hidden"]):
                    wait(pool, var_done["hidden"], t.n + 1)
                    wait(pool, hs_done, J * (t.n - 1))
                    b = root_slot(t, "hidden")
                    nc.gpsimd.tensor_tensor(inv[:, b, 0, :], var[:, b, 0, :], power[:, 0:J],
                                            ALU.pow).then_inc(hidden_root_done, 1)
                tiles = [(tile_at(ROOTS[root]), root) for root in used]
                tiles = [(t, root) for t, root in tiles if t]
                if tiles:
                    for t, root in tiles:
                        wait(pool, var_done[root], t.n + 1)
                    now = tiles[0][0].n + ROOTS[tiles[0][1]]
                    for root, sem in used.items():
                        count = now - ROOTS[root] - 1
                        wait(pool, sem, min(count, NT) if isinstance(count, int) else count)
                    b = root_slot(*tiles[0])
                    nc.gpsimd.tensor_tensor(inv[:, b, 1:, :].rearrange("p k j -> p (k j)"),
                                            var[:, b, 1:, :].rearrange("p k j -> p (k j)"), power[:, J:],
                                            ALU.pow).then_inc(ln_roots_done, 1)
                if t := tile_at(8):
                    wait(pool, xr_loaded[t.slot], 16 * (t.u + 1))
                    wait(pool, z_done, t.n - 1)
                    nc.gpsimd.tensor_tensor(xb[:, t.slot, :, :], xr[:, t.slot, :, :],
                                            b2[:, :].unsqueeze(1).broadcast_to([P, J, D]), ALU.add
                                            ).then_inc(xb_done, 1)
                if t := tile_at(0):
                    gather_step(nc, pool, t, idx, rows, g["att_sums"], idx_loaded, a_done, gathered)
            over_tiles(pool, NT, LAST_ROOT, step)

        @block.tensor
        def _(pe):
            pe.wait_ge(w_loaded, 16 * (loads - 1))
            pe.wait_ge(rows_done, 3)
            pe.wait_ge(centred, 2)
            pe.wait_ge(ones_set, 2)

            def clip(count):
                return min(count, NT) if isinstance(count, int) else count

            def step(tile_at):
                if t := tile_at(5):
                    wait(pe, x1t_done, t.n + 1)
                    for j in range(J):
                        wait(pe, hs_done, J * (t.n - 1) + j + 1)
                        nc.tensor.matmul(ps_h[j][:, :], x1t[:, t.slot4, j * P:(j + 1) * P], f1c[:, :],
                                         start=True, stop=False)
                        nc.tensor.matmul(ps_h[j][:, :], ones[:, :], bias_rows[:, :], start=False,
                                         stop=True).then_inc(h_made, 1)

                def turn_y2():
                    if t := tile_at(7):
                        wait(pe, y2t_done, t.n + 1)
                        wait(pe, x1t_done, clip(t.n + 3))
                        for j in range(J):
                            last = nc.tensor.transpose(ps_t[:, j * D:(j + 1) * D],
                                                       y2t[:, t.slot, j * P:(j + 1) * P], g["ident"][:, :])
                        last.then_inc(y2_turned, 1)

                def turn_xh():
                    if t := tile_at(4):
                        wait(pe, xh_done, t.n + 1)
                        wait(pe, x1t_done, t.n)
                        wait(pe, u_done, t.n - 2)
                        for j in range(J):
                            last = nc.tensor.transpose(ps_t[:, j * P:(j + 1) * P], xh[:, t.slot, j, :],
                                                       g["ident"][:, :])
                        last.then_inc(xh_turned, 1)
                if t := tile_at(6):
                    wait(pe, hs_done, J * (t.n + 1))

                    def turn(c):
                        wait(pe, gelu_done, C * t.n + c - 1)
                        for j in range(J):
                            last = nc.tensor.transpose(ps_g[c % 2][:, j * P:(j + 1) * P],
                                                       hs[:, t.slot, j, c * P:(c + 1) * P], g["ident"][:, :])
                        last.then_inc(g_turned, 1)

                    def down(c):
                        wait(pe, gelu_done, C * t.n + c + 1)
                        wait(pe, y2t_done, t.n)
                        last = nc.tensor.matmul(ps_f[:, :], f2[:, c, :], hg[:, c, :], start=c == 0, stop=c == C - 1)
                        if c == C - 1:
                            last.then_inc(f2_made, 1)
                    turn(0)
                    turn(1)
                    turn_y2()
                    for c in range(C):
                        down(c)
                        if c + 2 < C:
                            turn(c + 2)
                        if c + 3 == C:
                            turn_xh()
                else:
                    turn_y2()
                    turn_xh()
            over_tiles(pe, NT, 7, step)

        @block.vector
        def _(dve):
            dve.wait_ge(w_loaded, 16 * (loads - 1))
            nc.vector.memset(ones[:, :], 1.0).then_inc(ones_set, 1)
            nc.vector.memset(bias_rows[:, :], 0.0).then_inc(ones_set, 1)
            nc.vector.reduce_sum(total[:, 0:1], f1[:, :], axis=AX.X).then_inc(total_done, 1)
            nc.vector.reduce_sum(total[:, 1:2], fb[:, :], axis=AX.X).then_inc(total_done, 1)
            dve.wait_ge(total_done, 2)
            nc.vector.tensor_scalar(mean[:, :], total[:, :], 1.0 / FFN, None, ALU.mult).then_inc(mean_done, 1)
            dve.wait_ge(mean_done, 1)
            nc.vector.tensor_scalar(f1c[:, :], f1[:, :], mean[:, 0:1], None, ALU.subtract).then_inc(centred, 1)
            nc.vector.tensor_scalar(fbc[:, :], fb[:, :], mean[:, 1:2], None, ALU.subtract).then_inc(centred, 1)
            dve.wait_ge(centred, 2)
            nc.vector.tensor_copy(hi[:, :], fbc[:, :]).then_inc(hi_done, 1)
            dve.wait_ge(hi_done, 1)
            nc.vector.tensor_tensor(rest1[:, :], fbc[:, :], hi[:, :], ALU.subtract).then_inc(rest1_done, 1)
            dve.wait_ge(rest1_done, 1)
            nc.vector.tensor_copy(mid[:, :], rest1[:, :]).then_inc(mid_done, 1)
            dve.wait_ge(mid_done, 1)
            nc.vector.tensor_tensor(rest2[:, :], rest1[:, :], mid[:, :], ALU.subtract).then_inc(rest2_done, 1)
            dve.wait_ge(rest2_done, 1)
            nc.vector.tensor_copy(lo[:, :], rest2[:, :]).then_inc(lo_done, 1)
            dve.wait_ge(lo_done, 1)
            dve.wait_ge(ones_set, 2)
            for row, part in ((0, hi), (32, mid), (64, lo)):
                nc.vector.tensor_copy(bias_rows[row:row + 1, :], part[row:row + 1, :]).then_inc(rows_done, 1)

            def statistics(t, root, stats, mv, parts, free):
                wait(dve, free, t.n - 1)
                for j, part in enumerate(parts):
                    last = nc.vector.bn_stats(stats[:, t.slot, j, :], part)
                last.then_inc(stats_done[root], 1)
                wait_alone(dve, stats_done[root], t.n + 1)
                for j in range(J):
                    last = nc.vector.bn_aggr(mv[:, t.slot, j, :], stats[:, t.slot, j, :])
                last.then_inc(mv_done[root], 1)
                wait(dve, mv_done[root], t.n + 1)
                wait(dve, ln_roots_done, roots_of(t, root) - 2)
                nc.vector.tensor_scalar(var[:, root_slot(t, root), list(ROOTS).index(root), :],
                                        mv[:, t.slot, :, 1], EPS, None, ALU.add).then_inc(var_done[root], 1)

            def inverse(t, root):
                return inv[:, root_slot(t, root), list(ROOTS).index(root), :]

            dve.wait_ge(roots_set, 2)

            def step(tile_at):
                if t := tile_at(7):
                    wait(dve, f2_made, t.n + 1)
                    wait(dve, y2_turned, t.n - 1)
                    nc.vector.scalar_tensor_tensor(y2t[:, t.slot, :], ps_f[:, :], f2b[:, :], x1t[:, t.slot4, :],
                                                   ALU.add, ALU.add).then_inc(y2t_done, 1)
                if t := tile_at(9):
                    wait(dve, ln_roots_done, roots_of(t, "ln2"))
                    wait(dve, xb_done, t.n + 1)
                    wait(dve, u_done, t.n + 1)
                    wait(dve, y_done, t.n - 1)
                    for j in range(J):
                        last = nc.vector.scalar_tensor_tensor(z[:, t.slot, j, :], u[:, t.slot, j, :],
                                                              inverse(t, "ln2")[:, j:j + 1], xb[:, t.slot, j, :],
                                                              ALU.mult, ALU.add)
                    last.then_inc(z_done, 1)
                if t := tile_at(3):
                    wait(dve, a_done, t.n + 1)
                    statistics(t, "ln1", stats1, mv1, [a[:, t.slot, j, :] for j in range(J)], xh_done)
                if t := tile_at(9):
                    wait(dve, z_done, t.n + 1)
                    statistics(t, "ln3", stats3, mv3, [z[:, t.slot, j, :] for j in range(J)], shift_done)
                if t := tile_at(5):
                    wait(dve, sumsq_done, t.n + 1)
                    wait(dve, hidden_root_done, t.n - 1)
                    nc.vector.tensor_scalar(var[:, root_slot(t, "hidden"), list(ROOTS).index("hidden"), :],
                                            sumsq[:, t.slot, :], 1.0 / FFN, EPS,
                                            ALU.mult, ALU.add).then_inc(var_done["hidden"], 1)
                if t := tile_at(7):
                    wait(dve, y2_turned, t.n + 1)
                    statistics(t, "ln2", stats2, mv2, [ps_t[:, j * D:(j + 1) * D] for j in range(J)], u_done)
                    wait(dve, z_done, t.n - 1)
                    for j in range(J):
                        last = nc.vector.scalar_tensor_tensor(u[:, t.slot, j, :], ps_t[:, j * D:(j + 1) * D],
                                                              mv2[:, t.slot, j, 0:1], g2[:, :],
                                                              ALU.subtract, ALU.mult)
                    last.then_inc(u_done, 1)
                if t := tile_at(5):
                    wait(dve, hidden_root_done, t.n + 1)
                    wait(dve, g_turned, C * (t.n - 1))
                    for j in range(J):
                        nc.vector.tensor_scalar(hs[:, t.slot, j, :], ps_h[j][:, :],
                                                inverse(t, "hidden")[:, j:j + 1], None, ALU.mult
                                                ).then_inc(hs_done, 1)
                if t := tile_at(3):
                    wait(dve, ln_roots_done, roots_of(t, "ln1"))
                    wait(dve, xh_turned, t.n - 1)
                    for j in range(J):
                        last = nc.vector.tensor_scalar(xh[:, t.slot, j, :], a[:, t.slot, j, :],
                                                       mv1[:, t.slot, j, 0:1], inverse(t, "ln1")[:, j:j + 1],
                                                       ALU.subtract, ALU.mult)
                    last.then_inc(xh_done, 1)
                if t := tile_at(9):
                    wait(dve, ln_roots_done, roots_of(t, "ln3"))
                    wait(dve, y_done, t.n - 1)
                    nc.vector.scalar_tensor_tensor(shift[:, t.slot, :], mv3[:, t.slot, :, 0], -1.0,
                                                   inverse(t, "ln3"), ALU.mult, ALU.mult).then_inc(shift_done, 1)
            over_tiles(dve, NT, 9, step)

        @block.scalar
        def _(act):
            act.wait_ge(w_loaded, 16 * (loads - 1))

            def step(tile_at):
                def apply_last_norm(js):
                    if t := tile_at(10):
                        for j in js:
                            wait(act, shift_done, t.n + 1)
                            wait(act, stored[t.slot], 16 * t.u)
                            scaled = nc.scalar.activation(y[:, t.slot, j, :], z[:, t.slot, j, :], ACT.Identity,
                                                          bias=shift[:, t.slot, j:j + 1],
                                                          scale=inv[:, root_slot(t, "ln3"),
                                                                    list(ROOTS).index("ln3"), j:j + 1])
                        if j == J - 1:
                            scaled.then_inc(y_done, 1)

                def gelu(cs):
                    if t := tile_at(6):
                        for c in cs:
                            wait(act, g_turned, C * t.n + c + 1)
                            wait(act, f2_made, t.n)
                            nc.scalar.activation(hg[:, c, :], ps_g[c % 2][:, :], ACT.Gelu, bias=bf[:, c:c + 1],
                                                 scale=gf[:, c:c + 1]).then_inc(gelu_done, 1)
                if t := tile_at(5):
                    wait(act, var_done["hidden"], t.n - 1)
                    for j in range(J):
                        wait(act, h_made, J * t.n + j + 1)
                        last = nc.scalar.activation(squares[:, j, :], ps_h[j][:, :], ACT.Square,
                                                    accum_out=sumsq[:, t.slot, j:j + 1])
                    last.then_inc(sumsq_done, 1)
                gelu((0, 1))
                apply_last_norm((0, 1))
                gelu((2,))
                apply_last_norm((2, 3))
                gelu((3,))
                if t := tile_at(4):
                    wait(act, xh_turned, t.n + 1)
                    wait(act, y2t_done, t.n - 3)
                    nc.scalar.activation(x1t[:, t.slot4, :], ps_t[:, :], ACT.Identity, bias=b1[:, :],
                                         scale=g1[:, :]).then_inc(x1t_done, 1)
                if t := tile_at(10):
                    wait(act, y_done, t.n + 1)
                    act.dma_start(nm_tile(g["x_a"], t), flat(y[:, t.slot, :, :])).then_inc(stored[t.slot], 16)
            over_tiles(act, NT, 10, step)
            for b in range(2):
                act.wait_ge(stored[b], 16 * (NT // 2))


class Chain:

    def __init__(self, f, eng, name):
        self.eng, self.sem, self.count = eng, f.sem(name), 0

    def __call__(self, instruction):
        self.count += 1
        instruction.then_inc(self.sem, 1)
        self.eng.wait_ge(self.sem, self.count)


def segment_starts(nc, name, pairs, keep_out, cut_out):
    rows, width = ECOLS // 2, 2 * P
    with ExitStack() as ctx:
        f = Phase(nc, ctx, name)
        now, before = f.sb("now", [rows, width, 2], I32), f.sb("before", [rows, width, 2], I32)
        keep, cut = f.sb("keep", [rows, width], BF16), f.sb("cut", [rows, width], BF16)
        loaded, made, stored = f.sem("loaded"), f.sem("made"), f.sem("stored")
        block = ctx.enter_context(nc.Block())

        @block.sync
        def _(sp):
            for buf, lead in ((now, 1), (before, 0)):
                sp.dma_start(buf[:, :, :], pairs[lead:lead + EP, :].rearrange("(r w) two -> r w two", w=width)
                             ).then_inc(loaded, 16)
            sp.wait_ge(made, 1)
            sp.dma_start(keep_out.rearrange("(r w) -> r w", w=width), keep[:, :]).then_inc(stored, 16)
            if cut_out is not None:
                sp.wait_ge(made, 2)
                sp.dma_start(cut_out.rearrange("(r w) -> r w", w=width), cut[:, :]).then_inc(stored, 16)
            sp.wait_ge(stored, 16 if cut_out is None else 32)

        @block.vector
        def _(dve):
            dve.wait_ge(loaded, 32)
            nc.vector.tensor_tensor(keep[:, :], now[:, :, 0], before[:, :, 0], ALU.is_equal).then_inc(made, 1)
            if cut_out is not None:
                dve.wait_ge(made, 1)
                nc.vector.tensor_scalar(cut[:, :], keep[:, :], BIG, -BIG, ALU.mult, ALU.add).then_inc(made, 1)


class NodeLists:
    ROWS = NP // SUPER
    LOADS = 3

    def __init__(self, f, g, side, ptr_out, inv_out):
        self.nc, self.g, self.side, self.ptr_out, self.inv_out = f.nc, g, side, ptr_out, inv_out
        rows = self.ROWS
        self.edges = f.sb("edges", [P, ECOLS, 2], I32)
        self.low_i, self.high_i = f.sb("low_i", [P, ECOLS], I32), f.sb("high_i", [P, ECOLS], I32)
        self.low, self.high = f.sb("low", [P, ECOLS]), f.sb("high", [P, ECOLS])
        self.before = f.sb("rows_before", [P, P])
        self.hot_high = f.sb("hot_high", [P, 2, HI_DIGITS], BF16)
        self.hot_low = f.sb("hot_low", [P, 2, DIGIT], BF16)
        (self.ones, self.count, self.cum, self.last_e, self.has, self.clipped, self.inverse, self.spare, self.moved,
         self.picked) = (f.sb(f"node_{s}", [rows, SUPER]) for s in (
             "ones", "count", "cum", "last_e", "has", "clipped", "inverse", "spare", "moved", "picked"))
        self.ptr_i = f.sb("ptr_i", [rows, SUPER], I32)
        self.offset = f.sb("offset", [rows, 1])
        self.ps_hist = [f.ps(f"ps_hist{b}") for b in range(2)]
        self.ps_off = f.ps("ps_off")
        self.loaded, self.one_hot_done, self.counted, self.cum_done, self.off_made, self.lists_made, self.stored = (
            f.sem(f"nodes_{s}") for s in ("loaded", "one_hot_done", "counted", "cum_done", "off_made", "lists_made",
                                          "stored"))

    def load(self, sp):
        for dst_, src_ in ((self.edges[:, :, :], self.g["edges"][1:EP + 1, :].rearrange("(p c) two -> p c two", p=P)),
                           (self.before[:, :], self.g["before_c"]), (self.spare[:, :], self.g["spare_c"])):
            sp.dma_start(dst_, src_).then_inc(self.loaded, 16)

    def store(self, sp):
        sp.wait_ge(self.lists_made, 2)
        sp.dma_start(self.ptr_out.rearrange("(r w) -> r w", w=SUPER), self.ptr_i[:, :]).then_inc(self.stored, 16)
        sp.dma_start(self.inv_out.rearrange("(r w) -> r w", w=SUPER), self.inverse[:, :]).then_inc(self.stored, 16)
        sp.wait_ge(self.stored, 32)

    def count_column(self, pe, c, b, first=False):
        wait(pe, self.one_hot_done, 2 * (c + 1))
        for half in range(2):
            last = self.nc.tensor.matmul(
                self.ps_hist[half][0:self.ROWS, 0:DIGIT],
                self.hot_high[:, b, :].rearrange("p (a h) -> p h a", h=2)[:, half, :],
                self.hot_low[:, b, :], start=first, stop=True, skip_group_check=True)
        last.then_inc(self.counted, 1)

    def offsets(self, pe):
        pe.wait_ge(self.cum_done, 1)
        self.nc.tensor.matmul(self.ps_off[0:self.ROWS, 0:1], self.before[0:self.ROWS, 0:self.ROWS],
                              self.cum[:, SUPER - 1:SUPER], start=True, stop=True).then_inc(self.off_made, 1)

    def split(self, dve, link):
        vector = self.nc.vector
        dve.wait_ge(self.loaded, 16 * self.LOADS)
        link(vector.memset(self.ones[:, :], 1.0))
        link(vector.tensor_scalar(self.low_i[:, :], self.edges[:, :, self.side], DIGIT - 1, None, ALU.bitwise_and))
        link(vector.tensor_scalar(self.high_i[:, :], self.edges[:, :, self.side], 8, None, ALU.logical_shift_right))
        link(vector.tensor_copy(self.low[:, :], self.low_i[:, :]))
        link(vector.tensor_copy(self.high[:, :], self.high_i[:, :]))

    def one_hot(self, dve, digits, c, b):
        wait(dve, self.counted, c - 1)
        self.nc.vector.tensor_scalar(self.hot_high[:, b, :], digits[:, 0:HI_DIGITS], self.high[:, bass.ds(c, 1)],
                                     None, ALU.is_equal).then_inc(self.one_hot_done, 1)
        self.nc.vector.tensor_scalar(self.hot_low[:, b, :], digits[:, :], self.low[:, bass.ds(c, 1)], None,
                                     ALU.is_equal).then_inc(self.one_hot_done, 1)

    def make_lists(self, dve, link):
        vector = self.nc.vector
        dve.wait_ge(self.counted, ECOLS)
        for half in range(2):
            link(vector.tensor_copy(self.count[:, half * DIGIT:(half + 1) * DIGIT],
                                    self.ps_hist[half][0:self.ROWS, 0:DIGIT]))
        vector.tensor_tensor_scan(self.cum[:, :], self.ones[:, :], self.count[:, :], 0.0, ALU.mult,
                                  ALU.add).then_inc(self.cum_done, 1)
        link(vector.tensor_scalar(self.has[:, :], self.count[:, :], 1.0, None, ALU.min))
        link(vector.tensor_scalar(self.clipped[:, :], self.count[:, :], 1.0, None, ALU.max))
        vector.reciprocal(self.inverse[:, :], self.clipped[:, :]).then_inc(self.lists_made, 1)
        dve.wait_ge(self.off_made, 1)
        link(vector.tensor_copy(self.offset[:, :], self.ps_off[0:self.ROWS, 0:1]))
        link(vector.tensor_scalar(self.last_e[:, :], self.cum[:, :], self.offset[:, :], -1.0, ALU.add, ALU.add))
        link(vector.tensor_tensor(self.moved[:, :], self.last_e[:, :], self.spare[:, :], ALU.subtract))
        link(vector.tensor_tensor(self.picked[:, :], self.moved[:, :], self.has[:, :], ALU.mult))
        vector.tensor_tensor(self.ptr_i[:, :], self.picked[:, :], self.spare[:, :],
                             ALU.add).then_inc(self.lists_made, 1)


HOT_STEP = 8
SLOT_COLS, SLOTS = 5, 4
RANK_STEP = SLOT_COLS * SLOTS


def sort_digit(nc, name, g, pairs_in, swap, high_digit, pairs_out, side, ptr_out, inv_out):
    with ExitStack() as ctx:
        f = Phase(nc, ctx, name)
        raw, pairs = f.sb("raw", [P, ECOLS, 2], I32), f.sb("pairs", [P, ECOLS, 2], I32)
        digit_i, digit = f.sb("digit_i", [P, ECOLS], I32), f.sb("digit", [P, ECOLS])
        digits_f, digits = f.sb("digits_f", [P, DIGIT]), f.sb("digits", [P, DIGIT], BF16)
        before_f, before = f.sb("before_f", [P, P]), f.sb("before", [P, P], BF16)
        rest = f.sb("rest", [P, P], BF16)
        hot = f.sb("hot", [P, ECOLS, DIGIT], BF16)
        ones = f.sb("ones", [P, DIGIT], BF16)
        upto, smaller = f.sb("upto", [P, DIGIT]), f.sb("smaller", [P, DIGIT])
        smaller_i, smaller_lo_i = f.sb("smaller_i", [P, DIGIT], I32), f.sb("smaller_lo_i", [P, DIGIT], I32)
        smaller_hi, smaller_lo = f.sb("smaller_hi", [P, DIGIT], BF16), f.sb("smaller_lo", [P, DIGIT], BF16)
        own = f.sb("own", [P, 2, DIGIT])
        rank = f.sb("rank", [P, SLOTS, SLOT_COLS])
        rank_i, rank_p, rank_c = (f.sb(s, [P, SLOTS, SLOT_COLS], I32) for s in ("rank_i", "rank_p", "rank_c"))
        dest_slot = f.sb("dest_slot", [P, SLOTS, SLOT_COLS], I32)
        pair_slot = f.sb("pair_slot", [P, SLOTS, SLOT_COLS, 2], I32)
        lead = f.sb("lead", [1, 2], I32)
        ps_total, ps_rank = f.ps("ps_total"), [f.ps(f"ps_rank{b}") for b in range(2)]
        (loaded, tables_set, hot_done, total_made, smaller_done, rank_made, rank_done, rank_int, parts_done,
         slots_filled, lead_set, lead_stored) = (
            f.sem(s) for s in ("loaded", "tables_set", "hot_done", "total_made", "smaller_done", "rank_made",
                               "rank_done", "rank_int", "parts_done", "slots_filled", "lead_set", "lead_stored"))
        scattered = f.sems("scattered", SLOTS)
        nodes = NodeLists(f, g, side, ptr_out, inv_out)
        block = ctx.enter_context(nc.Block())

        def hot_column(c):
            return hot[:, bass.ds(c, 1), :].rearrange("p a d -> p (a d)")

        @block.sync
        def _(sp):
            for dst_, src_ in ((raw[:, :, :], pairs_in), (digits_f[:, :], g["digits_c"]), (before_f[:, :], g["before_c"])):
                sp.dma_start(dst_, src_).then_inc(loaded, 16)
            nodes.load(sp)
            if high_digit:
                sp.wait_ge(lead_set, 1)
                sp.dma_start(pairs_out[0:1, :], lead[:, :]).then_inc(lead_stored, 16)
                sp.wait_ge(lead_stored, 16)
            nodes.store(sp)

        @block.gpsimd
        def _(pool):
            def scatter(k, b):
                wait(pool, slots_filled, 2 * (SLOTS * k + b + 1))
                pool.nop(nofuse=True)
                for i in range(SLOT_COLS):
                    nc.gpsimd.indirect_dma_start(
                        out=pairs_out[:, :], out_offset=bass.IndirectOffsetOnAxis(ap=dest_slot[:, b, i:i + 1], axis=0),
                        in_=pair_slot[:, b, i, :], in_offset=None).then_inc(scattered[b], 16)
            with pool.Fori(0, ECOLS // RANK_STEP) as k:
                for b in range(SLOTS):
                    scatter(k, b)
            for b in range(SLOTS):
                pool.wait_ge(scattered[b], 16 * ECOLS // SLOTS)

        @block.tensor
        def _(pe):
            pe.wait_ge(tables_set, 3)

            def total_column(c, first=False):
                wait(pe, hot_done, c + 1)
                last = nc.tensor.matmul(ps_total[:, 0:DIGIT], ones[:, 0:P], hot_column(c), start=first, stop=True,
                                        skip_group_check=True)
                last.then_inc(total_made, 1)
            for c in range(HOT_STEP):
                total_column(c, c == 0)
            with pe.Fori(1, ECOLS // HOT_STEP) as k:
                for i in range(HOT_STEP):
                    total_column(HOT_STEP * k + i)
            pe.wait_ge(smaller_done, 2)

            def rank_column(c, b):
                wait(pe, rank_done, c - 1)
                out = ps_rank[b][:, 0:DIGIT]
                if isinstance(c, int) and c < 2:
                    nc.tensor.matmul(out, ones[0:1, 0:P], smaller_hi[0:1, :], start=True, stop=True,
                                     skip_group_check=True)
                    nc.tensor.matmul(out, ones[0:1, 0:P], smaller_lo[0:1, :], start=False, stop=True,
                                     skip_group_check=True)
                else:
                    nc.tensor.matmul(out, rest[:, :], hot_column(c - 2), start=False, stop=True,
                                     skip_group_check=True)
                if not isinstance(c, int) or c > 0:
                    nc.tensor.matmul(out, ones[:, 0:P], hot_column(c - 1), start=False, stop=True,
                                     skip_group_check=True)
                nc.tensor.matmul(out, before[:, :], hot_column(c), start=False, stop=True,
                                 skip_group_check=True).then_inc(rank_made, 1)
            for c in range(RANK_STEP):
                rank_column(c, c % 2)
                if c > 0:
                    nodes.count_column(pe, c - 1, (c - 1) % 2, first=c == 1)
            with pe.Fori(1, ECOLS // RANK_STEP) as k:
                for i in range(RANK_STEP):
                    rank_column(RANK_STEP * k + i, i % 2)
                    nodes.count_column(pe, RANK_STEP * k + i - 1, (i - 1) % 2)
            nodes.count_column(pe, ECOLS - 1, (ECOLS - 1) % 2)
            nodes.offsets(pe)

        @block.vector
        def _(dve):
            link = Chain(f, dve, "link")
            nc.vector.memset(lead[:, :], -1).then_inc(lead_set, 1)
            link(nc.vector.memset(ones[:, :], 1.0))
            dve.wait_ge(loaded, 16 * 3)
            nc.vector.tensor_copy(before[:, :], before_f[:, :]).then_inc(tables_set, 1)
            nc.vector.tensor_tensor(rest[:, :], ones[:, 0:P], before_f[:, :], ALU.subtract).then_inc(tables_set, 1)
            link(nc.vector.tensor_copy(digits[:, :], digits_f[:, :]))
            for col in range(2):
                link(nc.vector.tensor_copy(pairs[:, :, col], raw[:, :, 1 - col if swap else col]))
            if high_digit:
                link(nc.vector.tensor_scalar(digit_i[:, :], pairs[:, :, 0], 8, None, ALU.logical_shift_right))
            else:
                link(nc.vector.tensor_scalar(digit_i[:, :], pairs[:, :, 0], DIGIT - 1, None, ALU.bitwise_and))
            nc.vector.tensor_copy(digit[:, :], digit_i[:, :]).then_inc(tables_set, 1)
            dve.wait_ge(tables_set, 3)
            with dve.Fori(0, ECOLS // HOT_STEP) as k:
                for i in range(HOT_STEP):
                    c = HOT_STEP * k + i
                    nc.vector.tensor_scalar(hot_column(c), digits[:, :], digit[:, bass.ds(c, 1)], None,
                                            ALU.is_equal).then_inc(hot_done, 1)
            nodes.split(dve, link)
            dve.wait_ge(total_made, ECOLS)
            link(nc.vector.tensor_tensor_scan(upto[:, :], ones[:, :], ps_total[:, 0:DIGIT], 0.0, ALU.mult, ALU.add))
            link(nc.vector.tensor_tensor(smaller[:, :], upto[:, :], ps_total[:, 0:DIGIT], ALU.subtract))
            link(nc.vector.tensor_copy(smaller_i[:, :], smaller[:, :]))
            link(nc.vector.tensor_scalar(smaller_lo_i[:, :], smaller_i[:, :], DIGIT - 1, None, ALU.bitwise_and))
            nc.vector.tensor_copy(smaller_lo[:, :], smaller_lo_i[:, :]).then_inc(smaller_done, 1)
            dve.wait_ge(smaller_done, 1)
            nc.vector.tensor_tensor(smaller_hi[:, :], smaller[:, :], smaller_lo[:, :],
                                    ALU.subtract).then_inc(smaller_done, 1)

            def rank_column(c, s, i):
                wait(dve, rank_made, c + 1)
                wait(dve, rank_done, c - 1)
                nc.vector.scalar_tensor_tensor(own[:, (s * SLOT_COLS + i) % 2, :],
                                               ps_rank[(s * SLOT_COLS + i) % 2][:, 0:DIGIT], 1.0, hot_column(c),
                                               ALU.mult, ALU.mult, accum_out=rank[:, s, i:i + 1]
                                               ).then_inc(rank_done, 1)

            def rank_step(k):
                for s in range(SLOTS):
                    filled = SLOTS * k + s
                    first = RANK_STEP * k + s * SLOT_COLS
                    for i in range(SLOT_COLS):
                        rank_column(first + i, s, i)
                        if i < SLOT_COLS - 1:
                            nodes.one_hot(dve, digits, first + i, (s * SLOT_COLS + i) % 2)
                    wait(dve, rank_done, first + SLOT_COLS)
                    nc.vector.tensor_copy(rank_i[:, s, :], rank[:, s, :]).then_inc(rank_int, 1)
                    nodes.one_hot(dve, digits, first + SLOT_COLS - 1, ((s + 1) * SLOT_COLS - 1) % 2)
                    wait(dve, rank_int, filled + 1)
                    wait(dve, scattered[s], 16 * SLOT_COLS * k)
                    if high_digit:
                        nc.vector.tensor_scalar(dest_slot[:, s, :], rank_i[:, s, :], 1, None,
                                                ALU.add).then_inc(slots_filled, 1)
                    else:
                        nc.vector.tensor_scalar(rank_p[:, s, :], rank_i[:, s, :], P - 1, None,
                                                ALU.bitwise_and).then_inc(parts_done, 1)
                        nc.vector.tensor_scalar(rank_c[:, s, :], rank_i[:, s, :], 7, None,
                                                ALU.logical_shift_right).then_inc(parts_done, 1)
                    nc.vector.tensor_copy(pair_slot[:, s, :, :], pairs[:, bass.ds(first, SLOT_COLS), :]
                                          ).then_inc(slots_filled, 1)
                    if not high_digit:
                        wait(dve, parts_done, 2 * (filled + 1))
                        nc.vector.scalar_tensor_tensor(dest_slot[:, s, :], rank_p[:, s, :], float(ECOLS),
                                                       rank_c[:, s, :], ALU.mult, ALU.add).then_inc(slots_filled, 1)
            rank_step(0)
            with dve.Fori(1, ECOLS // RANK_STEP) as k:
                rank_step(k)
            nodes.make_lists(dve, link)


def set_up(nc, name, g):
    with ExitStack() as ctx:
        f = Phase(nc, ctx, name)
        zeros, ob = f.sb("zeros", [P, J, D]), f.sb("ob", [P, D])
        loaded, zeros_set, stored = f.sem("loaded"), f.sem("zeros_set"), f.sem("stored")
        block = ctx.enter_context(nc.Block())

        @block.sync
        def _(sp):
            sp.dma_start(g["ident"][:, :], g["ident_c"]).then_inc(loaded, 16)
            sp.dma_start(ob[:, :], on_all(g["ob"])).then_inc(loaded, 16)
            sp.wait_ge(loaded, 32)
            for j in range(J):
                sp.dma_start(g["att_sums"][EP + j * P:EP + (j + 1) * P, :], ob[:, :]).then_inc(stored, 16)
            sp.wait_ge(zeros_set, 1)
            sp.dma_start(g["sums"][EP:EP + SUPER, :].rearrange("(p j) d -> p j d", j=J), zeros[:, :, :]
                         ).then_inc(stored, 16)
            sp.wait_ge(stored, 16 * (J + 1))

        @block.vector
        def _(dve):
            nc.vector.memset(zeros[:, :, :], 0.0).then_inc(zeros_set, 1)


FLOAT_INPUTS = {
    "L0_gnn_qW": "qW", "L0_gnn_qb": "qb", "L0_gnn_kW": "kW", "L0_gnn_kb": "kb", "L0_gnn_vW": "vW", "L0_gnn_vb": "vb",
    "L0_gnn_eW": "eW", "L0_gnn_eb": "eb", "L0_gnn_oW": "oW", "L0_gnn_ob": "ob", "L0_gnn_ln1_g": "ln1_g",
    "L0_gnn_ln1_b": "ln1_b", "L0_gnn_f1W": "f1W", "L0_gnn_f1b": "f1b", "L0_gnn_lnf_g": "lnf_g",
    "L0_gnn_lnf_b": "lnf_b", "L0_gnn_f2W": "f2W", "L0_gnn_f2b": "f2b", "L0_gnn_ln2_g": "ln2_g",
    "L0_gnn_ln2_b": "ln2_b", "L2_gnn_lin_b": "lin_b", "L2_gnn_b_ih": "b_ih", "L2_gnn_b_hh": "b_hh",
    "L3_gnn_weight": "w_cat",
}
TRANSPOSED_INPUTS = {
    "L1_gnn_W_l": "wl_t", "L1_gnn_W_r": "wr_t", "L2_gnn_lin_w": "lin_wt", "L2_gnn_w_ih": "wih_t",
    "L2_gnn_w_hh": "whh_t",
}


def build(nc, ins, out):
    g = dict(ins)

    def dram(name, shape, dt=F32):
        return nc.dram_tensor(name, shape, dt, kind="Internal").ap()

    g["att_sums"], g["sums"] = dram("att_sums", [EP + SUPER, D]), dram("sums", [EP + SUPER, D])
    g["x_a"], g["x_b"], g["x_c"] = (dram(n, [NP, D]) for n in ("x_a", "x_b", "x_c"))
    g["h_a"], g["h_b"] = (dram(n, [NP, D]) for n in ("h_a", "h_b"))
    g["ht_a"], g["ht_b"] = (dram(n, [NT, P, SUPER]) for n in ("ht_a", "ht_b"))
    g["ptr_dst"], g["ptr_src"] = dram("ptr_dst", [NP], I32), dram("ptr_src", [NP], I32)
    g["inv_dst"], g["inv_src"] = dram("inv_dst", [NP]), dram("inv_src", [NP])
    g["keep_dst"], g["cut_dst"], g["keep_src"] = (dram(n, [EP], BF16) for n in ("keep_dst", "cut_dst", "keep_src"))
    g["half_sorted"] = dram("half_sorted", [EP, 2], I32)
    g["by_src"] = dram("by_src", [EP + 1, 2], I32)
    g["by_dst"] = by_dst = g["edges"][1:EP + 1, :]
    by_src = g["by_src"][1:EP + 1, :]

    with ExitStack() as ctx:
        g["ident"] = ctx.enter_context(nc.sbuf_tensor("ident", [P, P], F32))
        set_up(nc, "setup", g)
        segment_starts(nc, "starts_dst", g["edges"], g["keep_dst"], g["cut_dst"])
        sort_digit(nc, "sort_low", g, by_dst.rearrange("(p c) two -> p c two", p=P), True, False, g["half_sorted"],
                   0, g["ptr_dst"], g["inv_dst"])
        sort_digit(nc, "sort_high", g, g["half_sorted"].rearrange("(p c) two -> p c two", p=P), False, True, g["by_src"],
                   1, g["ptr_src"], g["inv_src"])
        segment_starts(nc, "starts_src", g["by_src"], g["keep_src"], None)
        attention_pass(nc, "attend", g)
        ffn_pass(nc, "ffn", g)
        sum_pass(nc, "sum1", g, g["x_a"], by_src, g["keep_src"], g["wr_t"])
        mean_pass(nc, "mean1", g, g["x_a"], g["ptr_src"], g["inv_src"], g["wl_t"], g["x_b"], True, g["h_a"], g["ht_a"])
        h = [(g["h_a"], g["ht_a"]), (g["h_b"], g["ht_b"]), (g["h_a"], g["ht_a"]), (None, None)]
        for i in range(3):
            sum_pass(nc, f"sum2{i}", g, h[i][0], by_dst, g["keep_dst"], None)
            gated_pass(nc, f"gate{i}", g, i, *h[i], *h[i + 1], g["x_b"], g["x_c"] if i == 2 else None)
        sum_pass(nc, "sum3", g, g["x_c"], by_dst, g["keep_dst"], g["w_cat"][D:2 * D, :])
        mean_pass(nc, "mean3", g, g["x_c"], g["ptr_dst"], g["inv_dst"], g["w_cat"][0:D, :], out, False)


def kernel(**inputs):
    import numpy as np
    import concourse.bacc as bacc
    from concourse import mybir as my
    from concourse.bass_utils import run_bass_kernel_spmd as run

    nc = bacc.Bacc("TRN2", target_bir_lowering=False, num_devices=1)
    arrays = {short: np.ascontiguousarray(inputs[key]) for key, short in FLOAT_INPUTS.items()}
    arrays.update({short: np.ascontiguousarray(np.asarray(inputs[key]).T) for key, short in TRANSPOSED_INPUTS.items()})
    arrays["msg_wt"] = np.ascontiguousarray(np.asarray(inputs["L2_gnn_weight"]).transpose(0, 2, 1))
    x = np.zeros((NP, D), np.float32)
    x[:N] = inputs["x"]
    edges = np.full((EP + 1, 2), PAD_NODE, np.int32)
    edges[0] = -1
    edges[1:E + 1, 0] = inputs["dst"]
    edges[1:E + 1, 1] = inputs["src"]
    edge_t = np.zeros((EDIM, EP), np.float32)
    edge_t[:, :E] = np.asarray(inputs["edge_attr_32"]).T
    arrays.update(x_in=x, edges=edges, edge_attr_t=edge_t)
    head = np.arange(D) // HEAD_DIM
    arrays["ident_c"] = np.eye(P, dtype=np.float32)
    arrays["before_c"] = np.triu(np.ones((P, P), np.float32), 1)
    arrays["digits_c"] = np.tile(np.arange(DIGIT, dtype=np.float32), (P, 1))
    arrays["spare_c"] = np.tile(np.arange(EP, EP + SUPER, dtype=np.float32), (NP // SUPER, 1))
    arrays["blocks_c"] = ((head[:, None] == head[None, :]) * HEAD_DIM ** -0.5).astype(np.float32).reshape(
        P, HEADS, HEAD_DIM)
    arrays["heads_c"] = (np.arange(D)[:, None] == HEAD_DIM * np.arange(HEADS)[None, :]).astype(np.float32)
    ins = {key: nc.dram_tensor(f"in_{key}", a.shape, my.dt.from_np(a.dtype), kind="ExternalInput").ap()
           for key, a in arrays.items()}
    out = nc.dram_tensor("out", (NP, D), F32, kind="ExternalOutput").ap()
    build(nc, ins, out)
    r = run(nc, [{f"in_{key}": a for key, a in arrays.items()}], core_ids=[0])
    return r.results[0]["out"][:N]
```
